# Optimizing a Trainium2 kernel written in Bass

```python
import numpy as np
import jax
import jax.numpy as jnp

def _softmax(x, axis=-1):
    return jax.nn.softmax(x, axis=axis)

def _gelu(x):
    return jax.nn.gelu(x, approximate=True)

def _silu(x):
    return jax.nn.silu(x)

def _sigmoid(x):
    return jax.nn.sigmoid(x)

def _layernorm(x, axis=-1, eps=1e-05):
    m = jnp.mean(x, axis=axis, keepdims=True)
    v = jnp.var(x, axis=axis, keepdims=True)
    return (x - m) / jnp.sqrt(v + eps)

def _scatter_add(tgt, idx, src, axis=0):
    return tgt.at[idx].add(src)

def _segment_sum(src, seg, n):
    return jax.ops.segment_sum(src, seg, n)
kernel_name = 'mk_recurrent_d2_jaxref_r4_6fcb2d'

def setup_inputs(seed: int=0):
    np.random.seed(seed)
    _w = jnp.asarray

    def _L0_attn_setup():
        import jax, jax.numpy as jnp
        import numpy as np
        B_, L, D_MODEL = (2, 1024, 512)
        H, P, N, G, K = (32, 64, 128, 1, 4)
        EPS = 1e-05
        INTER = H * P
        CONV_DIM = INTER + 2 * G * N
        PROJ = INTER + CONV_DIM + H

        def _silu(x):
            return x * jax.nn.sigmoid(x)

        def _mamba2_mixer(hidden_states, W_in, conv_w, conv_b, dt_bias, A_log, D_param, norm_w, W_out):
            b, l, _ = hidden_states.shape
            proj = jnp.einsum('bld,pd->blp', hidden_states, W_in)
            gate = proj[..., :INTER]
            hBC = proj[..., INTER:INTER + CONV_DIM]
            dt = proj[..., INTER + CONV_DIM:]
            xc = jnp.transpose(hBC, (0, 2, 1))
            conv = jax.lax.conv_general_dilated(xc, conv_w[:, None, :], window_strides=(1,), padding=[(K - 1, 0)], dimension_numbers=('NCH', 'OIH', 'NCH'), feature_group_count=CONV_DIM)
            hBC = _silu(jnp.transpose(conv + conv_b[None, :, None], (0, 2, 1)))
            xs = hBC[..., :INTER].reshape(b, l, H, P)
            Bm = hBC[..., INTER:INTER + G * N].reshape(b, l, G, N)
            Cm = hBC[..., INTER + G * N:].reshape(b, l, G, N)
            Bh = jnp.repeat(Bm, H // G, axis=2)
            Ch = jnp.repeat(Cm, H // G, axis=2)
            dt = jax.nn.softplus(dt + dt_bias)
            A = -jnp.exp(A_log)
            dA = jnp.exp(dt * A)

            def step(h, inp):
                dA_t, dt_t, x_t, B_t, C_t = inp
                u = (dt_t[:, :, None] * x_t)[..., None] * B_t[:, :, None, :]
                h = dA_t[:, :, None, None] * h + u
                y = jnp.einsum('bhpn,bhn->bhp', h, C_t)
                return (h, y)
            tm = lambda a: jnp.moveaxis(a, 1, 0)
            h0 = jnp.zeros((b, H, P, N), hidden_states.dtype)
            _, ys = jax.lax.scan(step, h0, (tm(dA), tm(dt), tm(xs), tm(Bh), tm(Ch)))
            y = jnp.moveaxis(ys, 0, 1) + D_param[None, None, :, None] * xs
            y = y.reshape(b, l, INTER)
            g = y * _silu(gate)
            g = g * jax.lax.rsqrt(jnp.mean(g * g, axis=-1, keepdims=True) + EPS) * norm_w
            return jnp.einsum('bli,di->bld', g, W_out)
        key = jax.random.key(seed)
        ks = jax.random.split(key, 5)
        hidden_states = jax.random.normal(ks[0], (B_, L, D_MODEL), jnp.float32)
        W_in = jax.random.normal(ks[1], (PROJ, D_MODEL), jnp.float32) * 0.02
        conv_w = jax.random.normal(ks[2], (CONV_DIM, K), jnp.float32) * 0.1
        conv_b = jnp.zeros((CONV_DIM,), jnp.float32)
        dt_bias = jnp.ones((H,), jnp.float32)
        A_log = jnp.log(jnp.arange(1, H + 1, dtype=jnp.float32))
        D_param = jnp.ones((H,), jnp.float32)
        norm_w = jnp.ones((INTER,), jnp.float32)
        W_out = jax.random.normal(ks[3], (D_MODEL, INTER), jnp.float32) * 0.02
        return dict(hidden_states=hidden_states, W_in=W_in, conv_w=conv_w, conv_b=conv_b, dt_bias=dt_bias, A_log=A_log, D_param=D_param, norm_w=norm_w, W_out=W_out)
    _L0_attn_in = _L0_attn_setup()

    def _L0_ffn_setup():
        import jax, jax.numpy as jnp
        import numpy as np
        DIM = 512
        N_EXPERTS = 8
        TOP_K = 2
        key = jax.random.key(seed)
        ks = jax.random.split(key, 5)
        x = jax.random.normal(ks[0], (4, 1024, DIM), dtype=jnp.float32)
        W_up = jax.random.normal(ks[1], (DIM, DIM), dtype=jnp.float32) * (1.0 / np.sqrt(DIM))
        W_down = jax.random.normal(ks[2], (DIM, DIM), dtype=jnp.float32) * (1.0 / np.sqrt(DIM))
        W_gate = jax.random.normal(ks[3], (N_EXPERTS, DIM), dtype=jnp.float32) * (1.0 / np.sqrt(DIM))
        W_expert = jax.random.normal(ks[4], (DIM, DIM), dtype=jnp.float32) * (1.0 / np.sqrt(DIM))
        return {'x': x, 'W_up': W_up, 'W_down': W_down, 'W_gate': W_gate, 'W_expert': W_expert}
    _L0_ffn_in = _L0_ffn_setup()

    def _L1_attn_setup():
        import jax, jax.numpy as jnp
        import numpy as np
        H = 8
        R = 2
        D = 128
        DEG = 2
        GATE_OFFSET = 6.906768

        def _power_attention(q, k, v, log_g):
            B, T, hq, d = q.shape
            scale = 1.0 / d ** 0.5
            k = jnp.repeat(k, R, axis=2)
            v = jnp.repeat(v, R, axis=2)
            logG = jnp.cumsum(log_g, axis=1)
            logG = jnp.repeat(logG, R, axis=2)
            logG = jnp.transpose(logG, (0, 2, 1))
            qk = jnp.einsum('bthd,bshd->bhts', q, k) * scale
            a = qk ** DEG
            gate = logG[:, :, :, None] - logG[:, :, None, :]
            causal = jnp.tril(jnp.ones((T, T), dtype=bool))
            a = jnp.where(causal, a * jnp.exp(gate), 0.0)
            norm = jnp.sum(a, axis=-1) + 1e-06
            y = jnp.einsum('bhts,bshd->bthd', a, v)
            y = y / jnp.transpose(norm, (0, 2, 1))[..., None]
            return y
        key = jax.random.key(seed)
        ks = jax.random.split(key, 7)
        B, T, C = (1, 512, 512)
        q_dim = H * R * D
        kv_dim = H * D
        s = 0.02
        return {'hidden_states': jax.random.normal(ks[0], (B, T, C), dtype=jnp.float32), 'Wq': jax.random.normal(ks[1], (C, q_dim), dtype=jnp.float32) * s, 'Wk': jax.random.normal(ks[2], (C, kv_dim), dtype=jnp.float32) * s, 'Wv': jax.random.normal(ks[3], (C, kv_dim), dtype=jnp.float32) * s, 'Wg': jax.random.normal(ks[4], (C, H), dtype=jnp.float32) * s, 'Wc': jax.random.normal(ks[5], (q_dim, C), dtype=jnp.float32) * s, 'bc': jnp.zeros((C,), dtype=jnp.float32)}
    _L1_attn_in = _L1_attn_setup()

    def _L1_ffn_setup():
        import jax, jax.numpy as jnp
        import numpy as np
        HIDDEN = 512
        INTER = 2048
        MOE_INTER = 256
        N_ROUTED = 8
        NUM_LOCAL = 8
        TOP_K = 2
        B, S = (4, 512)

        def _mlp(x, gw, uw, dw):
            g = x @ gw.T
            u = x @ uw.T
            return g * jax.nn.sigmoid(g) * u @ dw.T
        key = jax.random.key(seed)
        ks = jax.random.split(key, 8)
        std = 0.02
        return {'hidden_states': jax.random.normal(ks[0], (B, S, HIDDEN), jnp.float32), 'router_weight': jax.random.normal(ks[1], (N_ROUTED, HIDDEN), jnp.float32) * std, 'sh_gate': jax.random.normal(ks[2], (INTER, HIDDEN), jnp.float32) * std, 'sh_up': jax.random.normal(ks[3], (INTER, HIDDEN), jnp.float32) * std, 'sh_down': jax.random.normal(ks[4], (HIDDEN, INTER), jnp.float32) * std, 'r_gate': jax.random.normal(ks[5], (MOE_INTER, HIDDEN), jnp.float32) * std, 'r_up': jax.random.normal(ks[6], (MOE_INTER, HIDDEN), jnp.float32) * std, 'r_down': jax.random.normal(ks[7], (HIDDEN, MOE_INTER), jnp.float32) * std}
    _L1_ffn_in = _L1_ffn_setup()
    _d = {'L0_attn_hidden_states': _L0_attn_in['hidden_states'], 'L0_attn_W_in': _L0_attn_in['W_in'], 'L0_attn_conv_w': _L0_attn_in['conv_w'], 'L0_attn_conv_b': _L0_attn_in['conv_b'], 'L0_attn_dt_bias': _L0_attn_in['dt_bias'], 'L0_attn_A_log': _L0_attn_in['A_log'], 'L0_attn_D_param': _L0_attn_in['D_param'], 'L0_attn_norm_w': _L0_attn_in['norm_w'], 'L0_attn_W_out': _L0_attn_in['W_out'], 'L0_ffn_W_up': _L0_ffn_in['W_up'], 'L0_ffn_W_down': _L0_ffn_in['W_down'], 'L0_ffn_W_gate': _L0_ffn_in['W_gate'], 'L0_ffn_W_expert': _L0_ffn_in['W_expert'], 'L1_attn_Wq': _L1_attn_in['Wq'], 'L1_attn_Wk': _L1_attn_in['Wk'], 'L1_attn_Wv': _L1_attn_in['Wv'], 'L1_attn_Wg': _L1_attn_in['Wg'], 'L1_attn_Wc': _L1_attn_in['Wc'], 'L1_attn_bc': _L1_attn_in['bc'], 'L1_ffn_router_weight': _L1_ffn_in['router_weight'], 'L1_ffn_sh_gate': _L1_ffn_in['sh_gate'], 'L1_ffn_sh_up': _L1_ffn_in['sh_up'], 'L1_ffn_sh_down': _L1_ffn_in['sh_down'], 'L1_ffn_r_gate': _L1_ffn_in['r_gate'], 'L1_ffn_r_up': _L1_ffn_in['r_up'], 'L1_ffn_r_down': _L1_ffn_in['r_down']}
    _x0 = _d['L0_attn_hidden_states']
    _d['L0_attn_hidden_states'] = jax.random.normal(jax.random.fold_in(jax.random.key(seed), 1), (4, 512, 512), dtype=_x0.dtype)
    del _x0
    return _d

def reference(L0_attn_hidden_states, L0_attn_W_in, L0_attn_conv_w, L0_attn_conv_b, L0_attn_dt_bias, L0_attn_A_log, L0_attn_D_param, L0_attn_norm_w, L0_attn_W_out, L0_ffn_W_up, L0_ffn_W_down, L0_ffn_W_gate, L0_ffn_W_expert, L1_attn_Wq, L1_attn_Wk, L1_attn_Wv, L1_attn_Wg, L1_attn_Wc, L1_attn_bc, L1_ffn_router_weight, L1_ffn_sh_gate, L1_ffn_sh_up, L1_ffn_sh_down, L1_ffn_r_gate, L1_ffn_r_up, L1_ffn_r_down):

    def _L0_attn_ref(hidden_states, W_in, conv_w, conv_b, dt_bias, A_log, D_param, norm_w, W_out):
        import jax, jax.numpy as jnp
        import numpy as np
        B_, L, D_MODEL = (2, 1024, 512)
        H, P, N, G, K = (32, 64, 128, 1, 4)
        EPS = 1e-05
        INTER = H * P
        CONV_DIM = INTER + 2 * G * N
        PROJ = INTER + CONV_DIM + H

        def _silu(x):
            return x * jax.nn.sigmoid(x)

        def _mamba2_mixer(hidden_states, W_in, conv_w, conv_b, dt_bias, A_log, D_param, norm_w, W_out):
            b, l, _ = hidden_states.shape
            proj = jnp.einsum('bld,pd->blp', hidden_states, W_in)
            gate = proj[..., :INTER]
            hBC = proj[..., INTER:INTER + CONV_DIM]
            dt = proj[..., INTER + CONV_DIM:]
            xc = jnp.transpose(hBC, (0, 2, 1))
            conv = jax.lax.conv_general_dilated(xc, conv_w[:, None, :], window_strides=(1,), padding=[(K - 1, 0)], dimension_numbers=('NCH', 'OIH', 'NCH'), feature_group_count=CONV_DIM)
            hBC = _silu(jnp.transpose(conv + conv_b[None, :, None], (0, 2, 1)))
            xs = hBC[..., :INTER].reshape(b, l, H, P)
            Bm = hBC[..., INTER:INTER + G * N].reshape(b, l, G, N)
            Cm = hBC[..., INTER + G * N:].reshape(b, l, G, N)
            Bh = jnp.repeat(Bm, H // G, axis=2)
            Ch = jnp.repeat(Cm, H // G, axis=2)
            dt = jax.nn.softplus(dt + dt_bias)
            A = -jnp.exp(A_log)
            dA = jnp.exp(dt * A)

            def step(h, inp):
                dA_t, dt_t, x_t, B_t, C_t = inp
                u = (dt_t[:, :, None] * x_t)[..., None] * B_t[:, :, None, :]
                h = dA_t[:, :, None, None] * h + u
                y = jnp.einsum('bhpn,bhn->bhp', h, C_t)
                return (h, y)
            tm = lambda a: jnp.moveaxis(a, 1, 0)
            h0 = jnp.zeros((b, H, P, N), hidden_states.dtype)
            _, ys = jax.lax.scan(step, h0, (tm(dA), tm(dt), tm(xs), tm(Bh), tm(Ch)))
            y = jnp.moveaxis(ys, 0, 1) + D_param[None, None, :, None] * xs
            y = y.reshape(b, l, INTER)
            g = y * _silu(gate)
            g = g * jax.lax.rsqrt(jnp.mean(g * g, axis=-1, keepdims=True) + EPS) * norm_w
            return jnp.einsum('bli,di->bld', g, W_out)
        return _mamba2_mixer(hidden_states, W_in, conv_w, conv_b, dt_bias, A_log, D_param, norm_w, W_out)

    def _L0_ffn_ref(x, W_up, W_down, W_gate, W_expert):
        import jax, jax.numpy as jnp
        import numpy as np
        DIM = 512
        N_EXPERTS = 8
        TOP_K = 2
        logits = jnp.einsum('bsd,ed->bse', x, W_gate)
        routing_weights, selected_experts = jax.lax.top_k(logits, TOP_K)
        shared_out = jnp.einsum('bsd,od->bso', jax.nn.relu(jnp.einsum('bsd,od->bso', x, W_up)), W_down)
        rw = jax.nn.softmax(routing_weights, axis=-1)
        expert_out = jnp.einsum('bsd,do->bso', x, W_expert)
        moe_out = jnp.sum(rw, axis=-1, keepdims=True) * expert_out
        return shared_out + moe_out

    def _L1_attn_ref(hidden_states, Wq, Wk, Wv, Wg, Wc, bc):
        import jax, jax.numpy as jnp
        import numpy as np
        H = 8
        R = 2
        D = 128
        DEG = 2
        GATE_OFFSET = 6.906768

        def _power_attention(q, k, v, log_g):
            B, T, hq, d = q.shape
            scale = 1.0 / d ** 0.5
            k = jnp.repeat(k, R, axis=2)
            v = jnp.repeat(v, R, axis=2)
            logG = jnp.cumsum(log_g, axis=1)
            logG = jnp.repeat(logG, R, axis=2)
            logG = jnp.transpose(logG, (0, 2, 1))
            qk = jnp.einsum('bthd,bshd->bhts', q, k) * scale
            a = qk ** DEG
            gate = logG[:, :, :, None] - logG[:, :, None, :]
            causal = jnp.tril(jnp.ones((T, T), dtype=bool))
            a = jnp.where(causal, a * jnp.exp(gate), 0.0)
            norm = jnp.sum(a, axis=-1) + 1e-06
            y = jnp.einsum('bhts,bshd->bthd', a, v)
            y = y / jnp.transpose(norm, (0, 2, 1))[..., None]
            return y
        B, T, C = hidden_states.shape
        q = (hidden_states @ Wq).reshape(B, T, H * R, D)
        k = (hidden_states @ Wk).reshape(B, T, H, D)
        v = (hidden_states @ Wv).reshape(B, T, H, D)
        g = hidden_states @ Wg
        log_g = jax.nn.log_sigmoid(GATE_OFFSET + g.astype(jnp.float32))
        y = _power_attention(q, k, v, log_g)
        y = y.reshape(B, T, H * R * D)
        return y @ Wc + bc

    def _L1_ffn_ref(hidden_states, router_weight, sh_gate, sh_up, sh_down, r_gate, r_up, r_down):
        import jax, jax.numpy as jnp
        import numpy as np
        HIDDEN = 512
        INTER = 2048
        MOE_INTER = 256
        N_ROUTED = 8
        NUM_LOCAL = 8
        TOP_K = 2
        B, S = (4, 512)

        def _mlp(x, gw, uw, dw):
            g = x @ gw.T
            u = x @ uw.T
            return g * jax.nn.sigmoid(g) * u @ dw.T
        Bsz, Seq, H = hidden_states.shape
        x = hidden_states.reshape(-1, H)
        logits = x.astype(jnp.float32) @ router_weight.astype(jnp.float32).T
        topk_vals, topk_idx = jax.lax.top_k(logits, TOP_K)
        topk_w = jax.nn.softmax(topk_vals, axis=-1)
        slot_mask = (topk_idx < NUM_LOCAL).astype(topk_w.dtype)
        comb_w = jnp.sum(topk_w * slot_mask, axis=-1).astype(x.dtype)
        shared = _mlp(x, sh_gate, sh_up, sh_down)
        routed = _mlp(x, r_gate, r_up, r_down) * comb_w[:, None]
        return (shared + routed).reshape(Bsz, Seq, H)
    x = L0_attn_hidden_states
    xn = _layernorm(x, axis=-1)
    s = _L0_attn_ref(xn, L0_attn_W_in, L0_attn_conv_w, L0_attn_conv_b, L0_attn_dt_bias, L0_attn_A_log, L0_attn_D_param, L0_attn_norm_w, L0_attn_W_out)
    g = _silu(_L0_ffn_ref(xn, L0_ffn_W_up, L0_ffn_W_down, L0_ffn_W_gate, L0_ffn_W_expert))
    x = x + s * g
    xn = _layernorm(x, axis=-1)
    s = _L1_attn_ref(xn, L1_attn_Wq, L1_attn_Wk, L1_attn_Wv, L1_attn_Wg, L1_attn_Wc, L1_attn_bc)
    g = _silu(_L1_ffn_ref(xn, L1_ffn_router_weight, L1_ffn_sh_gate, L1_ffn_sh_up, L1_ffn_sh_down, L1_ffn_r_gate, L1_ffn_r_up, L1_ffn_r_down))
    x = x + s * g
    return x

_drawn_inputs = setup_inputs


def setup_inputs(seed=0):
    import zlib

    import numpy as np

    out = dict(_drawn_inputs(seed))
    spreads = {'L0_attn_conv_b': (0.0, 0.1),
     'L0_attn_dt_bias': (1.0, 0.6),
     'L0_attn_D_param': (1.0, 0.2),
     'L0_attn_norm_w': (1.0, 0.2),
     'L1_attn_bc': (0.0, 0.8)}
    factors = {'L0_attn_A_log': 8.0,
     'L0_ffn_W_gate': 8.0,
     'L1_attn_Wq': 8.0,
     'L1_attn_Wk': 8.0,
     'L1_attn_Wv': 8.0,
     'L1_attn_Wg': 8.0,
     'L1_attn_Wc': 8.0,
     'L1_ffn_sh_gate': 8.0,
     'L1_ffn_sh_up': 8.0,
     'L1_ffn_sh_down': 8.0,
     'L1_ffn_r_gate': 8.0,
     'L1_ffn_r_up': 8.0,
     'L1_ffn_r_down': 8.0}
    for name, (base, spread) in spreads.items():
        noise = np.random.default_rng([zlib.crc32(name.encode()), seed]).standard_normal(out[name].shape)
        drawn = base * np.exp(spread * noise) if base else spread * noise
        out[name] = jnp.asarray(drawn.astype(out[name].dtype))
    for name, factor in factors.items():
        out[name] = (out[name] * factor).astype(out[name].dtype)
    return out
```

```python
from contextlib import ExitStack

import concourse.bass as bass
from concourse import mybir

F32 = mybir.dt.float32
F32R = mybir.dt.float32r
ACT = mybir.ActivationFunctionType
ALU = mybir.AluOpType
AX = mybir.AxisListType

P = 128
B, SEQ, D = 4, 512, 512
TOK = B * SEQ
TILES = TOK // P
CH = SEQ // P
KD = D // P
LN_EPS = 1e-5

HEADS, HEAD_P, STATE, TAPS = 32, 64, 128, 4
INTER = HEADS * HEAD_P
PAIRS = INTER // P
KI = INTER // P
EXPERTS = 8
KV_HEADS, REP, HEAD_D = 8, 2, 128
Q_DIM, KV_DIM = KV_HEADS * REP * HEAD_D, KV_HEADS * HEAD_D
SHARED, ROUTED = 2048, 256
HIDDEN = SHARED + ROUTED
BLOCKS = HIDDEN // P


def three_passes(pe, out, left, right, ks, first=True, last=True):
    ks = list(ks)
    for k in ks:
        (l_hi, l_lo), (r_hi, r_lo) = left(k), right(k)
        pe.matmul(out, l_lo, r_hi, start=first and k == ks[0], stop=False)
        pe.matmul(out, l_hi, r_lo, start=False, stop=False)
        end = pe.matmul(out, l_hi, r_hi, start=False, stop=last and k == ks[-1])
    return end


class Scope:

    def __init__(self, nc, stage):
        self.nc, self.stage, self.stack, self.sems = nc, stage, ExitStack(), []

    def __enter__(self):
        self.stack.__enter__()
        return self

    def __exit__(self, *exc):
        self.stack.__exit__(*exc)
        if exc[0] is None:
            self.nc.clear_and_free_semaphores(self.sems)
            self.nc.all_engine_barrier()

    def sb(self, name, shape, dtype=F32):
        return self.stack.enter_context(self.nc.sbuf_tensor(f"{self.stage}_{name}", shape, dtype))

    def ps(self, name, shape):
        return self.stack.enter_context(self.nc.psum_tensor(f"{self.stage}_{name}", shape, F32))

    def sem(self, name):
        self.sems.append(self.nc.alloc_semaphore(f"{self.stage}_{name}"))
        return self.sems[-1]

    def block(self):
        return self.stack.enter_context(self.nc.Block())


def normalize(nc, stage, x_dram, m):
    G = 4
    x_g = x_dram.rearrange("(g j p) d -> g p j d", j=G, p=P)
    with Scope(nc, stage) as s:
        x = s.sb("x", [P, 2, G, D])
        xn = s.sb("xn", [P, G, D])
        stats = s.sb("stats", [P, G, 6])
        mv = s.sb("mean_var", [P, G, 2])
        var_eps = s.sb("var_eps", [P, G])
        std = s.sb("std", [P, G])
        rstd = s.sb("rstd", [P, G])
        turned = s.ps("turned", [P, G, KD, P])
        x_loaded = [s.sem(f"x_loaded{i}") for i in range(2)]
        stats_done = s.sem("stats_done")
        var_done = s.sem("var_done")
        std_done = s.sem("std_done")
        rstd_done = s.sem("rstd_done")
        xn_done = s.sem("xn_done")
        turned_done = s.sem("turned_done")
        hi_done = s.sem("hi_done")
        lo_done = s.sem("lo_done")
        block = s.block()

        @block.sync
        def _(sync):
            for g in range(TILES // G):
                if g >= 2:
                    sync.wait_ge(xn_done, G * (g - 1))
                sync.dma_start(x[:, g % 2], x_g[g]).then_inc(x_loaded[g % 2], 16)

        @block.vector
        def _(dve):
            for g in range(TILES // G):
                dve.wait_ge(x_loaded[g % 2], 16 * (g // 2 + 1))
                for j in range(G):
                    dve.bn_stats(stats[:, j], x[:, g % 2, j]).then_inc(stats_done, 1)
                for j in range(G):
                    dve.wait_ge(stats_done, G * g + j + 1)
                    dve.bn_aggr(mv[:, j], stats[:, j]).then_inc(var_done, 1)
                dve.wait_ge(var_done, (G + 1) * g + G)
                dve.tensor_scalar(var_eps[:, :], mv[:, :, 1], LN_EPS, None, ALU.add).then_inc(var_done, 1)
                dve.wait_ge(std_done, g + 1)
                dve.reciprocal(rstd[:, :], std[:, :]).then_inc(rstd_done, 1)
                dve.wait_ge(rstd_done, g + 1)
                for j in range(G):
                    if g >= 1:
                        dve.wait_ge(turned_done, G * (g - 1) + j + 1)
                    dve.tensor_scalar(xn[:, j], x[:, g % 2, j], mv[:, j, 0:1], rstd[:, j:j + 1],
                                      ALU.subtract, ALU.mult).then_inc(xn_done, 1)
                for j in range(G):
                    t = G * g + j
                    dve.wait_ge(hi_done, t + 1)
                    dve.tensor_tensor(m.xn_lo[:, :, t * P:(t + 1) * P], turned[:, j],
                                      m.xn_hi[:, :, t * P:(t + 1) * P].bitcast(F32),
                                      ALU.subtract).then_inc(lo_done, 1)

        @block.scalar
        def _(act):
            for g in range(TILES // G):
                act.wait_ge(var_done, (G + 1) * (g + 1))
                act.activation(std[:, :], var_eps[:, :], ACT.Sqrt).then_inc(std_done, 1)
                for j in range(G):
                    t = G * g + j
                    act.wait_ge(turned_done, t + 1)
                    act.activation(m.xn_hi[:, :, t * P:(t + 1) * P], turned[:, j],
                                   ACT.Copy).then_inc(hi_done, 1)

        @block.tensor
        def _(pe):
            for g in range(TILES // G):
                for j in range(G):
                    pe.wait_ge(xn_done, G * g + j + 1)
                    if g >= 1:
                        pe.wait_ge(lo_done, G * (g - 1) + j + 1)
                    for k in range(KD):
                        ins = pe.transpose(turned[:, j, k], xn[:, j, k * P:(k + 1) * P], m.ident[:, :])
                    ins.then_inc(turned_done, 1)


class Steps:

    def __init__(self, load, round_hi, keep_lo, done, n):
        self.load, self.round_hi, self.keep_lo, self.done, self.n = load, round_hi, keep_lo, done, n


def split_weights(s, name, pieces, widest, ring=3):
    raw = s.sb(f"{name}_raw", [P, ring, widest])
    loaded = [s.sem(f"{name}_loaded{i}") for i in range(ring)]
    hi_done, lo_done = s.sem(f"{name}_hi_done"), s.sem(f"{name}_lo_done")

    def width(n):
        return pieces[n][1].shape[-1]

    def load(sync, n):
        if n >= ring:
            sync.wait_ge(lo_done, n - ring + 1)
        sync.dma_start(raw[:, n % ring, 0:width(n)], pieces[n][0]).then_inc(loaded[n % ring], 16)

    def round_hi(act, n):
        _, hi, _, scale = pieces[n]
        act.wait_ge(loaded[n % ring], 16 * (n // ring + 1))
        act.activation(hi, raw[:, n % ring, 0:width(n)], ACT.Identity,
                       scale=1.0 if scale is None else scale).then_inc(hi_done, 1)

    def keep_lo(dve, n):
        _, hi, lo, scale = pieces[n]
        dve.wait_ge(hi_done, n + 1)
        dve.scalar_tensor_tensor(out=lo, in0=raw[:, n % ring, 0:width(n)],
                                 scalar=1.0 if scale is None else scale, in1=hi.bitcast(F32),
                                 op0=ALU.mult, op1=ALU.subtract).then_inc(lo_done, 1)

    return Steps(load, round_hi, keep_lo, lo_done, len(pieces))


def mixture(nc, m):
    E_COLS = D + EXPERTS
    EH = E_COLS // 2
    with Scope(nc, "mix") as s:
        up = [s.sb(f"up_{x}", [P, KD, D], F32R) for x in ("hi", "lo")]
        down = [s.sb(f"down_{x}", [P, KD, D], F32R) for x in ("hi", "lo")]
        expert = [s.sb(f"expert_{x}", [P, KD, E_COLS], F32R) for x in ("hi", "lo")]
        h_hi = s.sb("h_hi", [P, 2, KD, SEQ], F32R)
        h_lo = s.sb("h_lo", [P, 2, KD, SEQ], F32R)
        top8 = s.sb("top8", [P, 2, 8])
        below = s.sb("below", [P, 2, 2])
        e2 = s.sb("e2", [P, 2, 2])
        esum = s.sb("esum", [P, 2])
        einv = s.sb("einv", [P, 2])
        rw = s.sb("rw", [P, 2, 2])
        rsum = s.sb("rsum", [P, 2])
        scaled = s.sb("scaled", [P, 2, D])
        total = s.sb("total", [P, CH, D])
        gate = s.sb("gate", [P, CH, D])
        up_ps = s.ps("up_ps", [P, 2, SEQ])
        sh_ps = s.ps("sh_ps", [P, 2, D])
        ex_ps = s.ps("ex_ps", [P, 2, 2, 512])
        pieces = [(dram[k], w[0][:, k], w[1][:, k], None)
                  for dram, w in ((m.w_up, up), (m.w_down, down), (m.w_expert, expert))
                  for k in range(KD)]
        w = split_weights(s, "w", pieces, E_COLS)
        up_done = s.sem("up_done")
        h_hi_done = s.sem("h_hi_done")
        h_lo_done = s.sem("h_lo_done")
        ffn_done = s.sem("ffn_done")
        top_done = s.sem("top_done")
        below_done = s.sem("below_done")
        e2_done = s.sem("e2_done")
        rw_step = s.sem("rw_step")
        scaled_done = s.sem("scaled_done")
        total_done = s.sem("total_done")
        gate_done = s.sem("gate_done")
        gate_stored = s.sem("gate_stored")
        block = s.block()
        gate_b = m.gate_dram.rearrange("(b c p) d -> b p c d", b=B, p=P)

        @block.sync
        def _(sync):
            for n in range(w.n):
                w.load(sync, n)
            for b in range(B):
                sync.wait_ge(gate_done, b + 1)
                sync.dma_start(gate_b[b], gate[:, :, :]).then_inc(gate_stored, 16)
            sync.wait_ge(gate_stored, 16 * B)

        @block.tensor
        def _(pe):
            def up_product(b):
                for f in range(KD):
                    n = KD * b + f
                    if n >= 2:
                        pe.wait_ge(h_lo_done, n - 1)
                    for k in range(KD):
                        if n == 0:
                            pe.wait_ge(w.done, k + 1)
                        end = three_passes(
                            pe, up_ps[:, n % 2],
                            lambda k: [x[:, k, f * P:(f + 1) * P] for x in up],
                            lambda k: [x[:, k, b * SEQ:(b + 1) * SEQ] for x in (m.xn_hi, m.xn_lo)],
                            [k], first=k == 0, last=k == KD - 1)
                    end.then_inc(up_done, 1)

            def down_and_expert(b):
                for j in range(CH):
                    t = CH * b + j
                    pe.wait_ge(h_lo_done, KD * (b + 1))
                    if t == 0:
                        pe.wait_ge(w.done, w.n)
                    if t >= 2:
                        pe.wait_ge(total_done, t - 1)
                    three_passes(pe, sh_ps[:, t % 2],
                                 lambda f: [x[:, b % 2, f, j * P:(j + 1) * P] for x in (h_hi, h_lo)],
                                 lambda f: [x[:, f] for x in down], range(KD))
                    for half in range(2):
                        end = three_passes(
                            pe, ex_ps[:, t % 2, half, 0:EH],
                            lambda k: [x[:, k, t * P:(t + 1) * P] for x in (m.xn_hi, m.xn_lo)],
                            lambda k: [x[:, k, half * EH:(half + 1) * EH] for x in expert], range(KD))
                    end.then_inc(ffn_done, 1)

            up_product(0)
            for b in range(B):
                if b + 1 < B:
                    up_product(b + 1)
                down_and_expert(b)

        @block.scalar
        def _(act):
            def relu_hi(b):
                for f in range(KD):
                    n = KD * b + f
                    act.wait_ge(up_done, n + 1)
                    if b >= 2:
                        act.wait_ge(ffn_done, CH * (b - 1))
                    act.activation(h_hi[:, b % 2, f], up_ps[:, n % 2], ACT.Relu).then_inc(h_hi_done, 1)

            for n in range(w.n):
                w.round_hi(act, n)
            relu_hi(0)
            for b in range(B):
                if b + 1 < B:
                    relu_hi(b + 1)
                for j in range(CH):
                    t = CH * b + j
                    act.wait_ge(below_done, t + 1)
                    act.activation(e2[:, t % 2], below[:, t % 2], ACT.Exp).then_inc(e2_done, 1)
                    act.wait_ge(rw_step, 4 * (t + 1))
                    if t >= 2:
                        act.wait_ge(total_done, t - 1)
                    act.activation(scaled[:, t % 2, 0:EH], ex_ps[:, t % 2, 0, 0:EH], ACT.Copy,
                                   scale=rsum[:, t % 2:t % 2 + 1]).then_inc(scaled_done, 1)
                    act.activation(scaled[:, t % 2, EH:D], ex_ps[:, t % 2, 1, 0:D - EH], ACT.Copy,
                                   scale=rsum[:, t % 2:t % 2 + 1]).then_inc(scaled_done, 1)
                act.wait_ge(total_done, CH * (b + 1))
                if b >= 1:
                    act.wait_ge(gate_stored, 16 * b)
                act.activation(gate[:, :, :], total[:, :, :], ACT.Silu).then_inc(gate_done, 1)

        @block.vector
        def _(dve):
            def relu_lo(b):
                for f in range(KD):
                    n = KD * b + f
                    dve.wait_ge(h_hi_done, n + 1)
                    dve.scalar_tensor_tensor(out=h_lo[:, b % 2, f], in0=up_ps[:, n % 2], scalar=0.0,
                                             in1=h_hi[:, b % 2, f].bitcast(F32),
                                             op0=ALU.max, op1=ALU.subtract).then_inc(h_lo_done, 1)

            for n in range(w.n):
                w.keep_lo(dve, n)
            relu_lo(0)
            for b in range(B):
                if b + 1 < B:
                    relu_lo(b + 1)
                for j in range(CH):
                    t, i = CH * b + j, (CH * b + j) % 2
                    dve.wait_ge(ffn_done, t + 1)
                    dve.max(top8[:, i], ex_ps[:, i, 1, D - EH:EH]).then_inc(top_done, 1)
                    dve.wait_ge(top_done, t + 1)
                    dve.tensor_scalar(below[:, i], top8[:, i, 0:2], top8[:, i, 0:1], None,
                                      ALU.subtract).then_inc(below_done, 1)
                    dve.wait_ge(e2_done, t + 1)
                    dve.tensor_tensor(esum[:, i:i + 1], e2[:, i, 0:1], e2[:, i, 1:2],
                                      ALU.add).then_inc(rw_step, 1)
                    dve.wait_ge(rw_step, 4 * t + 1)
                    dve.reciprocal(einv[:, i:i + 1], esum[:, i:i + 1]).then_inc(rw_step, 1)
                    dve.wait_ge(rw_step, 4 * t + 2)
                    dve.tensor_scalar(rw[:, i], e2[:, i], einv[:, i:i + 1], None,
                                      ALU.mult).then_inc(rw_step, 1)
                    dve.wait_ge(rw_step, 4 * t + 3)
                    dve.tensor_tensor(rsum[:, i:i + 1], rw[:, i, 0:1], rw[:, i, 1:2],
                                      ALU.add).then_inc(rw_step, 1)
                    dve.wait_ge(scaled_done, 2 * (t + 1))
                    if b >= 1 and j == 0:
                        dve.wait_ge(gate_done, b)
                    dve.tensor_tensor(total[:, j], scaled[:, i], sh_ps[:, i],
                                      ALU.add).then_inc(total_done, 1)


def ssm_shared(nc, m):
    with Scope(nc, "shared") as s:
        COLS = 2 * STATE + HEADS
        DT0, C0 = STATE, STATE + HEADS
        starts = {"dt": DT0, "B": 0, "C": C0}
        w_bcd = [s.sb(f"w_{x}", [P, KD, COLS], F32R) for x in ("hi", "lo")]
        raw = s.sb("raw", [P, 2, B, TAPS - 1 + SEQ])
        b_fm = s.sb("b_fm", [P, TOK])
        dtx = s.sb("dtx", [HEADS, TOK])
        dt_abs = s.sb("dt_abs", [HEADS, TOK])
        dt_exp = s.sb("dt_exp", [HEADS, TOK])
        dt_one = s.sb("dt_one", [HEADS, TOK])
        dt_err = s.sb("dt_err", [HEADS, TOK])
        dt = s.sb("dt", [HEADS, TOK])
        keep = m.square_sum[0:HEADS]
        ell = s.sb("ell", [HEADS, TILES, P])
        a_exp = s.sb("a_exp", [HEADS, 1])
        end_exp = s.sb("end_exp", [HEADS, TILES])
        diag = s.sb("diag", [HEADS, HEADS, TILES])
        ones = s.sb("ones", [HEADS, P])
        la, to_end, end_w, dt_end, dt_log = dt_abs, dt_exp, dt_one, dt_err, dt_one
        proj_ps = s.ps("proj_ps", [P, 3, SEQ])
        turn_ps = s.ps("turn_ps", [P, 4, 512])
        w = split_weights(s, "w", [(m.w_bcd[k], w_bcd[0][:, k], w_bcd[1][:, k], None)
                                   for k in range(KD)], COLS)
        proj_done, proj_read = s.sem("proj_done"), s.sem("proj_read")
        abs_done, exp_done, one_done = s.sem("abs_done"), s.sem("exp_done"), s.sem("one_done")
        log_done, err_done, log1p_done = s.sem("log_done"), s.sem("err_done"), s.sem("log1p_done")
        dt_done, la_done, keep_done, ell_done = (s.sem("dt_done"), s.sem("la_done"),
                                                 s.sem("keep_done"), s.sem("ell_done"))
        a_done, to_end_done, end_w_done, dt_end_done = (s.sem("a_done"), s.sem("to_end_done"),
                                                        s.sem("end_w_done"), s.sem("dt_end_done"))
        end_exp_done, diag_done = s.sem("end_exp_done"), s.sem("diag_done")
        pad_done, conv_done, silu_done = s.sem("pad_done"), s.sem("conv_done"), s.sem("silu_done")
        turned, turned_read = s.sem("turned"), s.sem("turned_read")
        cb_done, ell_stored = s.sem("cb_done"), s.sem("ell_stored")
        block = s.block()

        N_TABLE, N_DIAG, N_TURN, N_CB = 3, 1, TILES // 4, TILES // 4
        TURN0 = N_TABLE + N_DIAG
        CB0 = TURN0 + N_TURN

        @block.sync
        def _(sync):
            for n in range(w.n):
                w.load(sync, n)
            sync.wait_ge(ell_done, 1)
            sync.dma_start(m.ell_dram.rearrange("a h t -> (a h) t"), ell[:, :, :].rearrange("h t p -> h (t p)")).then_inc(ell_stored, 16)
            sync.wait_ge(ell_stored, 16)

        @block.tensor
        def _(pe):
            for n, (kind, b) in enumerate([(k, b) for k in ("dt", "B", "C") for b in range(B)]):
                if n >= 3:
                    pe.wait_ge(proj_read, n - 2)
                c0 = starts[kind]
                for k in range(KD):
                    if n == 0:
                        pe.wait_ge(w.done, k + 1)
                    end = three_passes(pe, proj_ps[:, n % 3],
                                       lambda k: [x[:, k, c0:c0 + P] for x in w_bcd],
                                       lambda k: [x[:, k, b * SEQ:(b + 1) * SEQ]
                                                  for x in (m.xn_hi, m.xn_lo)],
                                       [k], first=k == 0, last=k == KD - 1)
                end.then_inc(proj_done, 1)
            for n, (table, ready, count) in enumerate(((dt, dt_done, 1), (dt_end, dt_end_done, 1),
                                                       (None, ell_done, 1))):
                pe.wait_ge(ready, count)
                for t in range(TILES):
                    src = ell[:, t] if table is None else table[:, t * P:(t + 1) * P]
                    end = pe.transpose(turn_ps[:, n, t * HEADS:(t + 1) * HEADS], src,
                                       m.ident[0:HEADS, 0:HEADS])
                end.then_inc(turned, 1)
            pe.wait_ge(diag_done, 1)
            pe.matmul(turn_ps[:, N_TABLE, :], ones[:, :], diag[:, :, :].rearrange("h g t -> h (g t)"),
                      start=True, stop=True).then_inc(turned, 1)
            for n in range(N_TURN):
                pe.wait_ge(silu_done, 1)
                pe.wait_ge(turned_read, n + 1)
                for j in range(4):
                    t = 4 * n + j
                    end = pe.transpose(turn_ps[:, n % 4, j * P:(j + 1) * P], b_fm[:, t * P:(t + 1) * P],
                                       m.ident[:, :])
                end.then_inc(turned, 1)
            for n in range(N_CB):
                pe.wait_ge(silu_done, 2)
                pe.wait_ge(turned_read, TURN0 + n + 1)
                for j in range(4):
                    t = 4 * n + j
                    end = pe.matmul(turn_ps[:, n % 4, j * P:(j + 1) * P], b_fm[:, t * P:(t + 1) * P],
                                    m.c_fm[:, t * P:(t + 1) * P], start=True, stop=True)
                end.then_inc(turned, 1)

        @block.scalar
        def _(act):
            for n in range(w.n):
                w.round_hi(act, n)
            act.activation(a_exp[:, :], m.head_vec[:, 1:2], ACT.Exp).then_inc(a_done, 1)
            for b in range(B):
                act.wait_ge(proj_done, b + 1)
                act.activation(dtx[:, b * SEQ:(b + 1) * SEQ], proj_ps[0:HEADS, b % 3], ACT.Identity,
                               bias=m.head_vec[:, 0:1]).then_inc(proj_read, 1)
            act.wait_ge(proj_read, B)
            act.activation(dt_abs[:, :], dtx[:, :], ACT.Abs).then_inc(abs_done, 1)
            act.wait_ge(abs_done, 1)
            act.activation(dt_exp[:, :], dt_abs[:, :], ACT.Exp, scale=-1.0).then_inc(exp_done, 1)
            for n in range(B, 3 * B):
                kind, b = (n - B) // B, n % B
                act.wait_ge(proj_done, n + 1)
                act.activation(raw[:, kind, b, TAPS - 1:], proj_ps[:, n % 3],
                               ACT.Copy).then_inc(proj_read, 1)
                if n == B:
                    act.wait_ge(err_done, 1)
                    act.activation(dt_log[:, :], dt_one[:, :], ACT.Ln).then_inc(log_done, 1)
            act.wait_ge(to_end_done, 1)
            act.activation(end_w[:, :], to_end[:, :], ACT.Exp).then_inc(end_w_done, 1)
            act.activation(end_exp[:, :], ell[:, :, P - 1], ACT.Exp).then_inc(end_exp_done, 1)
            for kind, dest in enumerate((b_fm, m.c_fm)):
                act.wait_ge(conv_done, TAPS * (kind + 1))
                act.activation(dest[:, :], dest[:, :], ACT.Silu).then_inc(silu_done, 1)
            for n, dest in enumerate((m.dt_tm, m.dt_end_tm, m.ell_tm)):
                act.wait_ge(turned, n + 1)
                act.activation(dest, turn_ps[:, n, :].rearrange("p (t h) -> p t h", h=HEADS),
                               ACT.Copy).then_inc(turned_read, 1)
            act.wait_ge(turned, N_TABLE + 1)
            act.activation(m.chunk_decay[:, :, :], turn_ps[:, N_TABLE, :].rearrange(
                "p (h t) -> p h t", t=TILES), ACT.Copy).then_inc(turned_read, 1)
            for n in range(N_TURN):
                act.wait_ge(turned, TURN0 + n + 1)
                act.activation(m.b_tm[:, 4 * n:4 * n + 4], turn_ps[:, n % 4, :].rearrange(
                    "p (t n) -> p t n", n=P), ACT.Copy).then_inc(turned_read, 1)

        @block.vector
        def _(dve):
            for n in range(w.n):
                w.keep_lo(dve, n)
            dve.memset(keep[:, :], 1.0).then_inc(keep_done, 1)
            dve.wait_ge(keep_done, 1)
            dve.memset(keep[:, :].rearrange("h (t p) -> h t p", p=P)[:, :, 0:1], 0.0).then_inc(keep_done, 1)
            dve.memset(ones[:, :], 1.0).then_inc(pad_done, 1)
            dve.memset(raw[:, :, :, 0:TAPS - 1], 0.0).then_inc(pad_done, 1)
            dve.wait_ge(exp_done, 1)
            dve.tensor_scalar(dt_one[:, :], dt_exp[:, :], 1.0, None, ALU.add).then_inc(one_done, 1)
            dve.wait_ge(one_done, 1)
            dve.scalar_tensor_tensor(out=dt_err[:, :], in0=dt_one[:, :], scalar=1.0, in1=dt_exp[:, :],
                                     op0=ALU.subtract, op1=ALU.subtract).then_inc(err_done, 1)
            dve.wait_ge(err_done, 1)
            dve.wait_ge(log_done, 1)
            dve.tensor_tensor(dt_log[:, :], dt_log[:, :], dt_err[:, :], ALU.subtract).then_inc(log1p_done, 1)
            dve.wait_ge(log1p_done, 1)
            dve.scalar_tensor_tensor(out=dt[:, :], in0=dtx[:, :], scalar=0.0, in1=dt_log[:, :],
                                     op0=ALU.max, op1=ALU.add).then_inc(dt_done, 1)
            dve.wait_ge(dt_done, 1)
            dve.wait_ge(a_done, 1)
            dve.tensor_scalar(la[:, :], dt[:, :], a_exp[:, 0:1], -1.0, ALU.mult, ALU.mult).then_inc(la_done, 1)
            dve.wait_ge(la_done, 1)
            dve.wait_ge(keep_done, 2)
            dve.tensor_tensor_scan(ell[:, :, :].rearrange("h t p -> h (t p)"), keep[:, :], la[:, :], 0.0,
                                   ALU.mult, ALU.add).then_inc(ell_done, 1)
            dve.wait_ge(ell_done, 1)
            dve.tensor_tensor(to_end[:, :].rearrange("h (t p) -> h t p", p=P),
                              ell[:, :, P - 1:P].broadcast_to([HEADS, TILES, P]), ell[:, :, :],
                              ALU.subtract).then_inc(to_end_done, 1)
            dve.wait_ge(end_w_done, 1)
            dve.tensor_tensor(dt_end[:, :], end_w[:, :], dt[:, :], ALU.mult).then_inc(dt_end_done, 1)
            dve.wait_ge(end_exp_done, 1)
            dve.tensor_tensor(diag[:, :, :],
                              m.ident[0:HEADS, 0:HEADS].rearrange("h (g o) -> h g o", o=1).broadcast_to(
                                  [HEADS, HEADS, TILES]),
                              end_exp[:, :].rearrange("h (o t) -> h o t", o=1).broadcast_to(
                                  [HEADS, HEADS, TILES]), ALU.mult).then_inc(diag_done, 1)
            dve.wait_ge(pad_done, 2)
            for kind in range(2):
                dve.wait_ge(proj_read, B * (kind + 2))
                vec = m.bc_vec[:, kind]
                conv = (b_fm, m.c_fm)[kind][:, :].rearrange("p (b t) -> p b t", b=B)
                dve.tensor_scalar(conv, raw[:, kind, :, 0:SEQ], vec[:, 0:1], vec[:, TAPS:TAPS + 1],
                                  ALU.mult, ALU.add).then_inc(conv_done, 1)
                for j in range(1, TAPS):
                    dve.wait_ge(conv_done, TAPS * kind + j)
                    dve.scalar_tensor_tensor(out=conv, in0=raw[:, kind, :, j:j + SEQ],
                                             scalar=vec[:, j:j + 1], in1=conv,
                                             op0=ALU.mult, op1=ALU.add).then_inc(conv_done, 1)
            for n in range(N_CB):
                dve.wait_ge(turned, CB0 + n + 1)
                dve.tensor_tensor(m.cb[:, 4 * n:4 * n + 4], turn_ps[:, n % 4, :].rearrange(
                    "p (t n) -> p t n", n=P),
                    m.causal[:, :].rearrange("p (o n) -> p o n", o=1).broadcast_to([P, 4, P]),
                    ALU.mult).then_inc(cb_done, 1)


def row_of(eng, dram, n):
    size = 1
    for d in dram.shape[1:]:
        size *= d
    start = n * size if isinstance(n, int) else eng.snap(n * size)
    names = " ".join(f"d{k}" for k in range(len(dram.shape)))
    return dram.rearrange(f"{names} -> ({names})")[bass.ds(start, size)]


def columns_of(eng, n, size):
    return bass.ds(n * size if isinstance(n, int) else eng.snap(n * size), size)


def wait_all(eng, *waits):
    values = [v if isinstance(v, int) else eng.snap(v) for _, v in waits]
    for (sem, _), v in zip(waits, values):
        eng.wait_ge(sem, v)


def opening(i, r, upto):
    return isinstance(i, int) and i == 0 and r < upto


def each_unit(eng, body, units, steps, lead, tail):
    turns = units // steps
    for r in range(lead):
        body(0, r)
    with eng.Fori(0, turns - 1) as i:
        for r in range(lead, lead + steps):
            body(i, r)
    for r in range(lead, steps + tail):
        body(turns - 1, r)


def ssm_heads(nc, m):
    STEPS, UNITS, LEAD, TAIL = 2 * B, PAIRS * B, 6, 4
    LAST = UNITS // STEPS - 1
    with Scope(nc, "heads") as s:
        w_raw = s.sb("w_raw", [P, KD, 2, P])
        w_hi = s.sb("w_hi", [P, 2, KD, 2, P], F32R)
        w_lo = s.sb("w_lo", [P, 2, KD, 2, P], F32R)
        vec = s.sb("vec", [P, 2, 8])
        times = s.sb("times", [P, 2, 3, TILES, 2])
        decay = s.sb("decay", [P, 2, 2, TILES])
        ell_row = s.sb("ell_row", [P, 2, 2, SEQ])
        ell_exp = s.sb("ell_exp", [P, 4, SEQ])
        silu_gate = s.sb("silu_gate", [P, 4, SEQ])
        raw = s.sb("raw", [P, 2, TAPS - 1 + SEQ])
        x = s.sb("x", [P, 4, SEQ])
        x_dt = s.sb("x_dt", [P, 2, CH, P])
        x_end = s.sb("x_end", [P, 2, CH - 1, P])
        mix = s.sb("mix", [P, 2, 2, SEQ])
        state = s.sb("state", [P, 2, CH - 1, P])
        carried = s.sb("carried", [P, 2, SEQ - P])
        y = s.sb("y", [P, 2, SEQ])
        g = s.sb("g", [P, 2, SEQ])
        gg = s.sb("gg", [P, SEQ])
        gate_ps = s.ps("gate_ps", [P, SEQ])
        x_ps = s.ps("x_ps", [P, SEQ])
        turn_ps = s.ps("turn_ps", [P, CH, P])
        state_ps = s.ps("state_ps", [P, CH, P])
        inner_ps = s.ps("inner_ps", [P, 2, SEQ])
        outer_ps = s.ps("outer_ps", [P, 2, SEQ])
        w_loaded = [s.sem(f"w_loaded{q}") for q in range(2)]
        w_hi_done, w_lo_done = s.sem("w_hi_done"), s.sem("w_lo_done")
        rows_loaded = [s.sem(f"rows_loaded{q}") for q in range(2)]
        times_done, pad_done, zero_done = s.sem("times_done"), s.sem("pad_done"), s.sem("zero_done")
        gate_mm, x_mm, turn_mm, state_mm, y_mm = (s.sem("gate_mm"), s.sem("x_mm"), s.sem("turn_mm"),
                                                  s.sem("state_mm"), s.sem("y_mm"))
        gate_done, raw_done, conv_step, x_done = (s.sem("gate_done"), s.sem("raw_done"),
                                                  s.sem("conv_step"), s.sem("x_done"))
        ell_exp_done, diff_exp_done = s.sem("ell_exp_done"), s.sem("diff_exp_done")
        x_dt_done, x_end_done, diff_done = s.sem("x_dt_done"), s.sem("x_end_done"), s.sem("diff_done")
        mix0_done, mix1_done = s.sem("mix0_done"), s.sem("mix1_done")
        state_step, y_step, carried_done = s.sem("state_step"), s.sem("y_step"), s.sem("carried_done")
        g_done, gg_done, sum_done = s.sem("g_done"), s.sem("gg_done"), s.sem("sum_done")
        g_stored = [s.sem(f"g_stored{q}") for q in range(2)]
        block = s.block()

        def missing(i, r):
            return (isinstance(i, int) and i == 0 and r < 0) or (isinstance(i, int) and i == LAST
                                                                 and r >= STEPS)

        def nth(i, r, ring=1):
            return i * (STEPS // ring) + r // ring + 1

        @block.sync
        def _(sync):
            def load_pair(i, r):
                q, pair = (r // B) % 2, i * 2 + r // B
                weights = row_of(sync, m.w_gate_x, pair)
                vectors = row_of(sync, m.pair_vec, pair)
                if not opening(i, r, 1):
                    sync.wait_ge(w_lo_done, i * 2 + r // B)
                sync.dma_start(w_raw[:, :, :, :].rearrange("p k c n -> p (k c n)"),
                               weights.rearrange("(p n) -> p n", p=P)).then_inc(w_loaded[q], 16)
                if not opening(i, r, 2 * B):
                    sync.wait_ge(y_step, nth(i, r - B - 1) * 4 - 3)
                sync.dma_start(vec[:, q], vectors.rearrange("(p n) -> p n", p=P)).then_inc(
                    w_loaded[q], 16)

            def body(i, r):
                if not missing(i, r):
                    b, pair = r % B, i * 2 + r // B
                    rows = row_of(sync, m.ell_dram, pair)
                    if not opening(i, r, 2):
                        sync.wait_ge(diff_done, nth(i, r - 2))
                    heads = rows.rearrange("(o h t) -> o h t", o=1, h=2)[:, :, b * SEQ:(b + 1) * SEQ]
                    sync.dma_start(ell_row[:, r % 2], heads.broadcast_to([P, 2, SEQ])).then_inc(
                        rows_loaded[r % 2], 16)
                    if not opening(i, r, 4):
                        sync.wait_ge(y_step, nth(i, r - 4) * 4 - 2)
                    for h in range(2):
                        sync.dma_start(ell_exp[h * HEAD_P:(h + 1) * HEAD_P, r % 4],
                                       heads[:, h].broadcast_to([HEAD_P, SEQ])).then_inc(
                            rows_loaded[r % 2], 16)
                if r % B == 2 and not missing(i, r + B - 2):
                    load_pair(i, r + B - 2)
                if not missing(i, r - 4):
                    q, pair, b = r % 2, i * 2 + (r - 4) // B, r % B
                    mixed = row_of(sync, m.mixed_dram, pair).rearrange("(p t) -> p t", p=P)
                    wait_all(sync, (g_done, nth(i, r - 4)))
                    sync.dma_start(mixed[:, b * SEQ:(b + 1) * SEQ], g[:, q]).then_inc(g_stored[q], 16)

            load_pair(0, 0)
            each_unit(sync, body, UNITS, STEPS, LEAD, TAIL)
            for q in range(2):
                sync.wait_ge(g_stored[q], 16 * UNITS // 2)

        @block.tensor
        def _(pe):
            def project(i, r, kind, out):
                q, b = (r // B) % 2, r % B
                if b == 0:
                    pe.wait_ge(w_lo_done, i * 2 + r // B + 1)
                return three_passes(pe, out, lambda k: [x[:, q, k, kind] for x in (w_hi, w_lo)],
                                    lambda k: [x[:, k, b * SEQ:(b + 1) * SEQ]
                                               for x in (m.xn_hi, m.xn_lo)], range(KD))

            def body(i, r):
                first = opening(i, r, 1)
                if not missing(i, r):
                    if not first:
                        pe.wait_ge(gate_done, nth(i, r - 1))
                    project(i, r, 0, gate_ps[:, :]).then_inc(gate_mm, 1)
                if not missing(i, r - 1):
                    pe.wait_ge(x_done, nth(i, r - 1))
                    if not opening(i, r, 2):
                        pe.wait_ge(x_end_done, nth(i, r - 2))
                    for c in range(CH):
                        end = pe.transpose(turn_ps[:, c], x[:, (r - 1) % 4, c * P:(c + 1) * P],
                                           m.ident[:, :])
                    end.then_inc(turn_mm, 1)
                if not missing(i, r):
                    if not first:
                        pe.wait_ge(raw_done, nth(i, r - 1))
                    project(i, r, 1, x_ps[:, :]).then_inc(x_mm, 1)
                if not missing(i, r - 1):
                    b, q = (r - 1) % B, (r - 1) % 2
                    pe.wait_ge(x_end_done, nth(i, r - 1))
                    if not opening(i, r, 2):
                        pe.wait_ge(state_step, nth(i, r - 2) * 5)
                    for c in range(CH - 1):
                        end = pe.matmul(state_ps[:, c], m.b_tm[:, CH * b + c], x_end[:, q, c],
                                        start=True, stop=True)
                    end.then_inc(state_mm, 1)
                if not missing(i, r - 2):
                    b, q = (r - 2) % B, (r - 2) % 2
                    pe.wait_ge(mix0_done, nth(i, r - 2))
                    pe.wait_ge(mix1_done, nth(i, r - 2))
                    pe.wait_ge(state_step, nth(i, r - 2) * 5)
                    if not opening(i, r, 4):
                        pe.wait_ge(y_step, nth(i, r - 4) * 4 - 2)
                    for c in range(CH):
                        for h in range(2):
                            pe.matmul(inner_ps[h * HEAD_P:(h + 1) * HEAD_P, q, c * P:(c + 1) * P],
                                      x_dt[:, q, c, h * HEAD_P:(h + 1) * HEAD_P],
                                      mix[:, q, h, c * P:(c + 1) * P], start=True, stop=True)
                    for c in range(1, CH):
                        end = pe.matmul(outer_ps[:, q, c * P:(c + 1) * P], state[:, q, c - 1],
                                        m.c_fm[:, (CH * b + c) * P:(CH * b + c + 1) * P],
                                        start=True, stop=True)
                    end.then_inc(y_mm, 1)

            each_unit(pe, body, UNITS, STEPS, LEAD, TAIL)

        @block.scalar
        def _(act):
            def round_weights(i, r):
                q = (r // B) % 2
                act.wait_ge(w_loaded[q], 32 * (i + r // STEPS + 1))
                if not opening(i, r, 2 * B):
                    act.wait_ge(x_mm, nth(i, r - B - 1))
                act.activation(w_hi[:, q], w_raw[:, :, :, :], ACT.Copy).then_inc(w_hi_done, 1)

            def body(i, r):
                if not missing(i, r):
                    act.wait_ge(gate_mm, nth(i, r))
                    if not opening(i, r, 4):
                        act.wait_ge(g_done, nth(i, r - 4))
                    act.activation(silu_gate[:, r % 4], gate_ps[:, :], ACT.Silu).then_inc(gate_done, 1)
                    act.wait_ge(x_mm, nth(i, r))
                    if not opening(i, r, 2):
                        act.wait_ge(conv_step, nth(i, r - 2) * 4)
                    else:
                        act.wait_ge(pad_done, 1)
                    act.activation(raw[:, r % 2, TAPS - 1:], x_ps[:, :], ACT.Copy).then_inc(raw_done, 1)
                if not missing(i, r - 1):
                    b, q = (r - 1) % B, (r - 1) % 2
                    act.wait_ge(rows_loaded[q], 48 * nth(i, r - 1, 2))
                    act.activation(ell_exp[:, (r - 1) % 4], ell_exp[:, (r - 1) % 4],
                                   ACT.Exp).then_inc(ell_exp_done, 1)
                    act.wait_ge(diff_done, nth(i, r - 1))
                    act.activation(mix[:, q], mix[:, q], ACT.Exp).then_inc(diff_exp_done, 1)
                if not missing(i, r):
                    act.wait_ge(conv_step, nth(i, r) * 4)
                    act.activation(x[:, r % 4], x[:, r % 4], ACT.Silu).then_inc(x_done, 1)
                if r % B == 2 and not missing(i, r + B - 2):
                    round_weights(i, r + B - 2)

            round_weights(0, 0)
            each_unit(act, body, UNITS, STEPS, LEAD, TAIL)

        @block.vector
        def _(dve):
            def take_times(i, r):
                q, pair = (r // B) % 2, i * 2 + r // B
                dve.tensor_copy(times[:, q].rearrange("p a t h -> p (a t) h"),
                                m.times_tm[:, :, bass.ds(pair * 2, 2)]).then_inc(times_done, 1)
                dve.tensor_copy(decay[:, q], m.chunk_decay[:, bass.ds(pair * 2, 2), :]).then_inc(
                    times_done, 1)

            def outputs(i, r):
                q, pq = r % 2, (r // B) % 2
                dve.wait_ge(y_mm, nth(i, r))
                if not opening(i, r, 2):
                    dve.wait_ge(g_done, nth(i, r - 2))
                dve.scalar_tensor_tensor(out=y[:, q], in0=x[:, r % 4], scalar=vec[:, pq, 5:6],
                                         in1=inner_ps[:, q], op0=ALU.mult, op1=ALU.add).then_inc(y_step, 1)
                dve.wait_ge(ell_exp_done, nth(i, r))
                dve.tensor_tensor(carried[:, q], outer_ps[:, q, P:SEQ], ell_exp[:, r % 4, P:SEQ],
                                  ALU.mult).then_inc(y_step, 1)
                dve.wait_ge(y_step, nth(i, r) * 4 - 2)
                dve.tensor_tensor(y[:, q, P:SEQ], y[:, q, P:SEQ], carried[:, q], ALU.add).then_inc(y_step, 2)

            def body(i, r):
                if not missing(i, r - 3):
                    outputs(i, r - 3)
                if r % B == 0 and not missing(i, r):
                    take_times(i, r)
                if not missing(i, r - 1):
                    b, q, pq = (r - 1) % B, (r - 1) % 2, ((r - 1) // B) % 2
                    dve.wait_ge(turn_mm, nth(i, r - 1))
                    dve.wait_ge(times_done, 2 * (i * 2 + (r - 1) // B + 1))
                    if not opening(i, r, 3):
                        dve.wait_ge(y_mm, nth(i, r - 3))
                    for n, (out, done) in enumerate(((x_dt, x_dt_done), (x_end, x_end_done))):
                        cs = CH - n
                        dve.tensor_tensor(
                            out[:, q].rearrange("p c (h e) -> p c h e", h=2),
                            turn_ps[:, 0:cs].rearrange("p c (h e) -> p c h e", h=2),
                            times[:, pq, n, CH * b:CH * b + cs].rearrange(
                                "p c (h o) -> p c h o", o=1).broadcast_to([P, cs, 2, HEAD_P]),
                            ALU.mult).then_inc(done, 1)
                    dve.wait_ge(diff_exp_done, nth(i, r - 1))
                    dve.tensor_tensor(mix[:, q, 0].rearrange("p (c t) -> p c t", c=CH),
                                      mix[:, q, 0].rearrange("p (c t) -> p c t", c=CH),
                                      m.cb[:, CH * b:CH * (b + 1)], ALU.mult).then_inc(mix0_done, 1)
                if not missing(i, r):
                    q, pq = r % 2, (r // B) % 2
                    dve.wait_ge(raw_done, nth(i, r))
                    if not opening(i, r, 4):
                        dve.wait_ge(turn_mm, nth(i, r - 4))
                    dve.tensor_scalar(x[:, r % 4], raw[:, q, 0:SEQ], vec[:, pq, 0:1],
                                      vec[:, pq, TAPS:TAPS + 1], ALU.mult, ALU.add).then_inc(conv_step, 1)
                    for j in range(1, TAPS):
                        dve.wait_ge(conv_step, nth(i, r) * 4 - 4 + j)
                        dve.scalar_tensor_tensor(out=x[:, r % 4], in0=raw[:, q, j:j + SEQ],
                                                 scalar=vec[:, pq, j:j + 1], in1=x[:, r % 4],
                                                 op0=ALU.mult, op1=ALU.add).then_inc(conv_step, 1)
                if not missing(i, r - 1):
                    b, q, pq = (r - 1) % B, (r - 1) % 2, ((r - 1) // B) % 2
                    dve.wait_ge(state_mm, nth(i, r - 1))
                    if not opening(i, r, 3):
                        dve.wait_ge(y_mm, nth(i, r - 3))
                    dve.tensor_copy(state[:, q, 0], state_ps[:, 0]).then_inc(state_step, 1)
                    for c in range(1, CH - 1):
                        dve.wait_ge(state_step, nth(i, r - 1) * 5 - 6 + 2 * c)
                        for h in range(2):
                            cols = slice(h * HEAD_P, (h + 1) * HEAD_P)
                            dve.scalar_tensor_tensor(
                                out=state[:, q, c, cols], in0=state[:, q, c - 1, cols],
                                scalar=decay[:, pq, h, CH * b + c:CH * b + c + 1],
                                in1=state_ps[:, c, cols], op0=ALU.mult, op1=ALU.add).then_inc(state_step, 1)
                if not missing(i, r):
                    b, q, pq = r % B, r % 2, (r // B) % 2
                    dve.wait_ge(rows_loaded[q], 48 * nth(i, r, 2))
                    dve.wait_ge(times_done, 2 * (i * 2 + r // B + 1))
                    if not opening(i, r, 2):
                        dve.wait_ge(y_mm, nth(i, r - 2))
                    for h in range(2):
                        for c in range(CH):
                            cols, t = slice(c * P, (c + 1) * P), CH * b + c
                            end = dve.tensor_scalar(mix[:, q, h, cols], ell_row[:, q, h, cols],
                                                    times[:, pq, 2, t, h:h + 1], 0.0,
                                                    ALU.subtract, ALU.min)
                    end.then_inc(diff_done, 1)

            dve.memset(raw[:, :, 0:TAPS - 1], 0.0).then_inc(pad_done, 1)
            each_unit(dve, body, UNITS, STEPS, LEAD, TAIL)

        @block.gpsimd
        def _(pool):
            def keep_lo(i, r):
                q = (r // B) % 2
                pool.wait_ge(w_hi_done, i * 2 + r // B + 1)
                pool.tensor_tensor(w_lo[:, q], w_raw[:, :, :, :], w_hi[:, q].bitcast(F32),
                                   ALU.subtract).then_inc(w_lo_done, 1)

            def body(i, r):
                if not missing(i, r - 4):
                    b, q = r % B, r % 2
                    pool.wait_ge(y_step, nth(i, r - 4) * 4)
                    if not opening(i, r, 6):
                        pool.wait_ge(g_stored[q], 16 * nth(i, r - 6, 2))
                    pool.tensor_tensor(g[:, q], y[:, q], silu_gate[:, r % 4], ALU.mult).then_inc(g_done, 1)
                    pool.wait_ge(g_done, nth(i, r - 4))
                    if not opening(i, r, 5):
                        pool.wait_ge(sum_done, nth(i, r - 5))
                    pool.tensor_tensor(gg[:, :], g[:, q], g[:, q], ALU.mult).then_inc(gg_done, 1)
                    pool.wait_ge(gg_done, nth(i, r - 4))
                    total = m.square_sum[:, b * SEQ:(b + 1) * SEQ]
                    pool.tensor_tensor(total, total, gg[:, :], ALU.add).then_inc(sum_done, 1)
                if not missing(i, r - 1):
                    b, q = (r - 1) % B, (r - 1) % 2
                    pool.wait_ge(diff_exp_done, nth(i, r - 1))
                    pool.tensor_tensor(mix[:, q, 1].rearrange("p (c t) -> p c t", c=CH),
                                       mix[:, q, 1].rearrange("p (c t) -> p c t", c=CH),
                                       m.cb[:, CH * b:CH * (b + 1)], ALU.mult).then_inc(mix1_done, 1)
                if r % B == 2 and not missing(i, r + B - 2):
                    keep_lo(i, r + B - 2)

            pool.memset(m.square_sum[:, :], 0.0).then_inc(zero_done, 1)
            pool.wait_ge(zero_done, 1)
            keep_lo(0, 0)
            each_unit(pool, body, UNITS, STEPS, LEAD, TAIL)


def ssm_output(nc, m):
    STEPS = 4
    LAST = TILES // STEPS - 1
    with Scope(nc, "ssm_out") as s:
        w_out = [s.sb(f"w_{x}", [P, KI, D], F32R) for x in ("hi", "lo")]
        w = split_weights(s, "w", [(m.w_out[k], w_out[0][:, k], w_out[1][:, k], m.norm_w[:, k:k + 1])
                                   for k in range(KI)], D)
        ones = s.sb("ones", [P, 2])
        mean_sq, rms, inv_rms = s.sb("mean_sq", [P, TILES]), s.sb("rms", [P, TILES]), s.sb("inv_rms", [P, TILES])
        mixed = s.sb("mixed", [P, 2, KI, P])
        hi, lo = s.sb("mixed_hi", [P, 2, KI, P], F32R), s.sb("mixed_lo", [P, 2, KI, P], F32R)
        x, gate, gated, x1 = (s.sb(n, [P, 2, D]) for n in ("x", "gate", "gated", "x1"))
        out_ps = s.ps("out_ps", [P, 2, D])
        sq_ps = s.ps("sq_ps", [P, TILES, 2])
        ones_done, sq_mm, mean_done, rms_done, inv_done = (
            s.sem(n) for n in ("ones_done", "sq_mm", "mean_done", "rms_done", "inv_done"))
        mixed_loaded = [s.sem(f"mixed_loaded{q}") for q in range(2)]
        rows_loaded = [s.sem(f"rows_loaded{q}") for q in range(2)]
        hi_done, lo_done, out_mm, gated_done, x1_done = (
            s.sem(n) for n in ("hi_done", "lo_done", "out_mm", "gated_done", "x1_done"))
        x1_stored = [s.sem(f"x1_stored{q}") for q in range(2)]
        block = s.block()
        x_t, gate_t, x1_t = (d.rearrange("(n p) d -> n p d", p=P) for d in (m.x, m.gate_dram, m.x1_dram))
        mixed_p = m.mixed_dram.rearrange("k p t -> p k t")

        def missing(i, r):
            return opening(i, r, 0) or (isinstance(i, int) and i == LAST and r >= STEPS)

        def nth(i, r, ring=1):
            return i * (STEPS // ring) + r // ring + 1

        @block.sync
        def _(sync):
            def load(i, r):
                q, t = r % 2, i * STEPS + r
                tokens = columns_of(sync, t, P)
                x_rows, gate_rows = (row_of(sync, d, t).rearrange("(p d) -> p d", p=P)
                                     for d in (x_t, gate_t))
                if not opening(i, r, 2):
                    sync.wait_ge(lo_done, nth(i, r - 2))
                sync.dma_start(mixed[:, q], mixed_p[:, :, tokens]).then_inc(mixed_loaded[q], 16)
                if not opening(i, r, 2):
                    sync.wait_ge(x1_done, nth(i, r - 2))
                sync.dma_start(x[:, q], x_rows).then_inc(rows_loaded[q], 16)
                sync.dma_start(gate[:, q], gate_rows).then_inc(rows_loaded[q], 16)

            def body(i, r):
                if not missing(i, r - 1):
                    rows = row_of(sync, x1_t, i * STEPS + r - 1).rearrange("(p d) -> p d", p=P)
                    wait_all(sync, (x1_done, nth(i, r - 1)))
                    sync.dma_start(rows, x1[:, (r - 1) % 2]).then_inc(x1_stored[(r - 1) % 2], 16)
                if not missing(i, r + 1):
                    load(i, r + 1)

            load(0, 0)
            for n in range(w.n):
                w.load(sync, n)
            each_unit(sync, body, TILES, STEPS, 3, 1)
            for q in range(2):
                sync.wait_ge(x1_stored[q], 16 * TILES // 2)

        @block.tensor
        def _(pe):
            pe.wait_ge(ones_done, 1)
            for t in range(TILES):
                end = pe.matmul(sq_ps[:, t], m.square_sum[:, t * P:(t + 1) * P], ones[:, :],
                                start=True, stop=True)
            end.then_inc(sq_mm, 1)

            def body(i, r):
                if missing(i, r):
                    return
                q = r % 2
                pe.wait_ge(lo_done, nth(i, r))
                if not opening(i, r, 2):
                    pe.wait_ge(gated_done, nth(i, r - 2))
                for k in range(KI):
                    if opening(i, r, 1):
                        pe.wait_ge(w.done, k + 1)
                    end = three_passes(pe, out_ps[:, q], lambda k: (hi[:, q, k], lo[:, q, k]),
                                       lambda k: [x[:, k] for x in w_out], [k],
                                       first=k == 0, last=k == KI - 1)
                end.then_inc(out_mm, 1)

            each_unit(pe, body, TILES, STEPS, 3, 1)

        @block.scalar
        def _(act):
            def body(i, r):
                if missing(i, r):
                    return
                q = r % 2
                act.wait_ge(mixed_loaded[q], 16 * nth(i, r, 2))
                if not opening(i, r, 2):
                    act.wait_ge(out_mm, nth(i, r - 2))
                act.activation(hi[:, q], mixed[:, q], ACT.Copy).then_inc(hi_done, 1)

            act.wait_ge(mean_done, 1)
            act.activation(rms[:, :], mean_sq[:, :], ACT.Sqrt).then_inc(rms_done, 1)
            body(0, 0)
            for n in range(w.n):
                w.round_hi(act, n)
            each_unit(act, lambda i, r: None if opening(i, r, 1) else body(i, r), TILES, STEPS, 3, 1)

        @block.vector
        def _(dve):
            def split(i, r):
                q = r % 2
                dve.wait_ge(hi_done, nth(i, r))
                dve.tensor_tensor(lo[:, q], mixed[:, q], hi[:, q].bitcast(F32),
                                  ALU.subtract).then_inc(lo_done, 1)

            def finish(i, r):
                q, t = r % 2, i * STEPS + r
                wait_all(dve, (out_mm, nth(i, r)), (rows_loaded[q], 32 * nth(i, r, 2)),
                         *[(x1_stored[q], 16 * nth(i, r - 2, 2))][:not opening(i, r, 2)])
                dve.scalar_tensor_tensor(out=gated[:, q], in0=out_ps[:, q],
                                         scalar=inv_rms[:, bass.ds(t, 1)], in1=gate[:, q],
                                         op0=ALU.mult, op1=ALU.mult).then_inc(gated_done, 1)
                dve.wait_ge(gated_done, nth(i, r))
                dve.tensor_tensor(x1[:, q], gated[:, q], x[:, q], ALU.add).then_inc(x1_done, 1)

            def body(i, r):
                if not missing(i, r) and not opening(i, r, 1):
                    split(i, r)
                if not missing(i, r - 1):
                    finish(i, r - 1)

            dve.memset(ones[:, :], 1.0).then_inc(ones_done, 1)
            dve.wait_ge(sq_mm, 1)
            dve.tensor_scalar(mean_sq[:, :], sq_ps[:, :, 0], 1.0 / INTER, LN_EPS, ALU.mult,
                              ALU.add).then_inc(mean_done, 1)
            dve.wait_ge(rms_done, 1)
            dve.reciprocal(inv_rms[:, :], rms[:, :]).then_inc(inv_done, 1)
            dve.wait_ge(inv_done, 1)
            split(0, 0)
            for n in range(w.n):
                w.keep_lo(dve, n)
            each_unit(dve, body, TILES, STEPS, 3, 1)


def values_and_decays(nc, m):
    V0 = KV_HEADS
    COLS = KV_HEADS + KV_DIM + EXPERTS
    PARTS = 4
    W = (KV_DIM + EXPERTS) // PARTS
    GATE_OFFSET = 6.906768
    with Scope(nc, "values") as s:
        w_all = [s.sb(f"w_{x}", [P, KD, COLS], F32R) for x in ("hi", "lo")]
        w = split_weights(s, "w", [(m.w_gvr[k], w_all[0][:, k], w_all[1][:, k], None)
                                   for k in range(KD)], COLS)
        v = s.sb("v", [P, 2, PARTS, W])
        z, z_abs, z_exp, z_one, z_err, log_g, keep, total = (
            s.sb(n, [KV_HEADS, TOK]) for n in ("z", "z_abs", "z_exp", "z_one", "z_err", "log_g",
                                               "keep", "total"))
        top8 = s.sb("top8", [P, TILES, 8])
        below, e2, rw = (s.sb(n, [P, TILES, 2]) for n in ("below", "e2", "rw"))
        esum, einv = s.sb("esum", [P, TILES, 1]), s.sb("einv", [P, TILES, 1])
        g_ps = s.ps("g_ps", [P, SEQ])
        v_ps = s.ps("v_ps", [P, 6, 512])
        turn_ps = s.ps("turn_ps", [P, TILES, KV_HEADS])
        g_mm, z_done, abs_done, exp_done, one_done, log_done, err_done, log1p_done = (
            s.sem(n) for n in ("g_mm", "z_done", "abs_done", "exp_done", "one_done", "log_done",
                               "err_done", "log1p_done"))
        log_g_done, keep_done, total_done, turned, turned_read, total_stored = (
            s.sem(n) for n in ("log_g_done", "keep_done", "total_done", "turned", "turned_read",
                               "total_stored"))
        v_mm, v_read, top_done, below_done, e2_done, rw_step = (
            s.sem(n) for n in ("v_mm", "v_read", "top_done", "below_done", "e2_done", "rw_step"))
        v_stored = [s.sem(f"v_stored{q}") for q in range(2)]
        block = s.block()
        values_t = m.values_dram.rearrange("(n p) d -> n p d", p=P)

        @block.sync
        def _(sync):
            for n in range(w.n):
                w.load(sync, n)
            for t in range(TILES):
                sync.wait_ge(v_read, PARTS * (t + 1))
                sync.dma_start(values_t[t], v[:, t % 2].rearrange("p a w -> p (a w)")[:, 0:KV_DIM]
                               ).then_inc(v_stored[t % 2], 16)
                if t == 1:
                    sync.wait_ge(total_done, 1)
                    sync.dma_start(m.log_gate_dram, total[:, :]).then_inc(total_stored, 16)
            sync.wait_ge(total_stored, 16)
            for q in range(2):
                sync.wait_ge(v_stored[q], 16 * TILES // 2)

        @block.tensor
        def _(pe):
            for b in range(B):
                if b >= 1:
                    pe.wait_ge(z_done, b)
                for k in range(KD):
                    if b == 0:
                        pe.wait_ge(w.done, k + 1)
                    end = three_passes(pe, g_ps[:, :], lambda k: [x[:, k, 0:P] for x in w_all],
                                       lambda k: [x[:, k, b * SEQ:(b + 1) * SEQ]
                                                  for x in (m.xn_hi, m.xn_lo)],
                                       [k], first=k == 0, last=k == KD - 1)
                end.then_inc(g_mm, 1)
            for t in range(TILES):
                if t == TILES // 2:
                    pe.wait_ge(total_done, 1)
                    for n in range(TILES):
                        end = pe.transpose(turn_ps[:, n], total[:, n * P:(n + 1) * P],
                                           m.ident[0:KV_HEADS, 0:KV_HEADS])
                    end.then_inc(turned, 1)
                for a in range(PARTS):
                    n = PARTS * t + a
                    if n >= 6:
                        pe.wait_ge(v_read, n - 5)
                    three_passes(pe, v_ps[:, n % 6, 0:W],
                                 lambda k: [x[:, k, t * P:(t + 1) * P] for x in (m.xn_hi, m.xn_lo)],
                                 lambda k: [x[:, k, V0 + a * W:V0 + (a + 1) * W] for x in w_all],
                                 range(KD)).then_inc(v_mm, 1)

        @block.scalar
        def _(act):
            for n in range(w.n):
                w.round_hi(act, n)
            act.wait_ge(z_done, B)
            act.activation(z_abs[:, :], z[:, :], ACT.Abs).then_inc(abs_done, 1)
            act.wait_ge(abs_done, 1)
            act.activation(z_exp[:, :], z_abs[:, :], ACT.Exp, scale=-1.0).then_inc(exp_done, 1)
            act.wait_ge(one_done, 1)
            act.activation(log_g[:, :], z_one[:, :], ACT.Ln).then_inc(log_done, 1)
            for t in range(TILES):
                if t >= 2:
                    act.wait_ge(v_stored[t % 2], 16 * (t // 2))
                    act.wait_ge(top_done, t - 1)
                for a in range(PARTS):
                    n = PARTS * t + a
                    act.wait_ge(v_mm, n + 1)
                    act.activation(v[:, t % 2, a], v_ps[:, n % 6, 0:W], ACT.Copy).then_inc(v_read, 1)
            act.wait_ge(turned, 1)
            act.activation(m.log_gate_tm[:, :, :].rearrange("p h t -> p t h"), turn_ps[:, :, :],
                           ACT.Copy).then_inc(turned_read, 1)
            act.wait_ge(below_done, 1)
            act.activation(e2[:, :, :], below[:, :, :], ACT.Exp).then_inc(e2_done, 1)
            act.wait_ge(turned_read, 1)

        @block.vector
        def _(dve):
            for n in range(w.n):
                w.keep_lo(dve, n)
            dve.memset(keep[:, :], 1.0).then_inc(keep_done, 1)
            dve.wait_ge(keep_done, 1)
            dve.memset(keep[:, :].rearrange("h (b t) -> h b t", b=B)[:, :, 0:1], 0.0).then_inc(keep_done, 1)
            for b in range(B):
                dve.wait_ge(g_mm, b + 1)
                dve.tensor_scalar(z[:, b * SEQ:(b + 1) * SEQ], g_ps[0:KV_HEADS], GATE_OFFSET, None,
                                  ALU.add).then_inc(z_done, 1)
            dve.wait_ge(exp_done, 1)
            dve.tensor_scalar(z_one[:, :], z_exp[:, :], 1.0, None, ALU.add).then_inc(one_done, 1)
            dve.wait_ge(one_done, 1)
            dve.scalar_tensor_tensor(out=z_err[:, :], in0=z_one[:, :], scalar=1.0, in1=z_exp[:, :],
                                     op0=ALU.subtract, op1=ALU.subtract).then_inc(err_done, 1)
            wait_all(dve, (err_done, 1), (log_done, 1))
            dve.tensor_tensor(log_g[:, :], log_g[:, :], z_err[:, :], ALU.subtract).then_inc(log1p_done, 1)
            dve.wait_ge(log1p_done, 1)
            dve.scalar_tensor_tensor(out=log_g[:, :], in0=z[:, :], scalar=0.0, in1=log_g[:, :],
                                     op0=ALU.min, op1=ALU.subtract).then_inc(log_g_done, 1)
            wait_all(dve, (log_g_done, 1), (keep_done, 2))
            dve.tensor_tensor_scan(total[:, :], keep[:, :], log_g[:, :], 0.0, ALU.mult,
                                   ALU.add).then_inc(total_done, 1)
            for t in range(TILES):
                dve.wait_ge(v_read, PARTS * (t + 1))
                dve.max(top8[:, t], v[:, t % 2, PARTS - 1, W - EXPERTS:W]).then_inc(top_done, 1)
            dve.wait_ge(top_done, TILES)
            dve.tensor_tensor(below[:, :, :], top8[:, :, 0:2],
                              top8[:, :, 0:1].broadcast_to([P, TILES, 2]), ALU.subtract).then_inc(below_done, 1)
            dve.wait_ge(e2_done, 1)
            dve.tensor_tensor(esum[:, :, :], e2[:, :, 0:1], e2[:, :, 1:2], ALU.add).then_inc(rw_step, 1)
            dve.wait_ge(rw_step, 1)
            dve.reciprocal(einv[:, :, :], esum[:, :, :]).then_inc(rw_step, 1)
            dve.wait_ge(rw_step, 2)
            dve.tensor_tensor(rw[:, :, :], e2[:, :, :], einv[:, :, :].broadcast_to([P, TILES, 2]),
                              ALU.mult).then_inc(rw_step, 1)
            dve.wait_ge(rw_step, 3)
            dve.tensor_tensor(m.comb_w[:, :].rearrange("p (t o) -> p t o", o=1), rw[:, :, 0:1],
                              rw[:, :, 1:2], ALU.add).then_inc(rw_step, 1)
            dve.wait_ge(rw_step, 4)


def power_attention(nc, m):
    STEPS, UNITS, LEAD, TAIL = 2 * B, KV_HEADS * B, 6, 2
    LAST = UNITS // STEPS - 1
    WIDTH = [SEQ - j * P for j in range(CH)]
    AT = [0, 512, 1024, 896]
    COLS = sum(WIDTH)
    VC = HEAD_D + 2
    SCALE = HEAD_D ** -0.5
    with Scope(nc, "attn") as s:
        w_raw = s.sb("w_raw", [P, KD, 3, P])
        w_hi = s.sb("w_hi", [P, 2, KD, 3, P], F32R)
        w_lo = s.sb("w_lo", [P, 2, KD, 3, P], F32R)
        gate_row = s.sb("gate_row", [P, 2, SEQ])
        gate_cols = s.sb("gate_cols", [P, 2, TILES])
        v = s.sb("v", [P, 2, CH, VC])
        qk = s.sb("qk", [P, 2, 3, SEQ])
        decay = s.sb("decay", [P, 2, COLS])
        a = s.sb("a", [P, 2, COLS])
        norm, inv = s.sb("norm", [P, 2, CH]), s.sb("inv", [P, 2, CH])
        y = s.sb("y", [P, 2, CH, REP, HEAD_D])
        proj_ps = s.ps("proj_ps", [P, 3, SEQ])
        score_ps = s.ps("score_ps", [P, 3 * 512])
        out_ps = s.ps("out_ps", [P, 2, 512])
        w_loaded, w_hi_done, w_lo_done = s.sem("w_loaded"), s.sem("w_hi_done"), s.sem("w_lo_done")
        rows_loaded = [s.sem(f"rows_loaded{q}") for q in range(2)]
        v_loaded = [s.sem(f"v_loaded{q}") for q in range(2)]
        ones_done, cols_done, proj_mm, qk_done = (
            s.sem(n) for n in ("ones_done", "cols_done", "proj_mm", "qk_done"))
        score_mm, square_done, diff_done, decay_done, a_done = (
            s.sem(n) for n in ("score_mm", "square_done", "diff_done", "decay_done", "a_done"))
        out_mm, norm_done, inv_done, y_done = (
            s.sem(n) for n in ("out_mm", "norm_done", "inv_done", "y_done"))
        y_stored = [s.sem(f"y_stored{q}") for q in range(2)]
        block = s.block()

        def missing(i, r):
            return opening(i, r, 0) or (isinstance(i, int) and i == LAST and r >= STEPS)

        def nth(i, r, ring=1):
            return i * (STEPS // ring) + r // ring + 1

        def head_of(i, r):
            return i * 2 + r // B

        @block.sync
        def _(sync):
            def load_weights(i, r):
                weights = row_of(sync, m.w_qqk, head_of(i, r)).rearrange("(p n) -> p n", p=P)
                wait_all(sync, *[(w_lo_done, head_of(i, r))][:not opening(i, r, 1)])
                sync.dma_start(w_raw[:, :, :, :].rearrange("p k c n -> p (k c n)"),
                               weights).then_inc(w_loaded, 16)

            def body(i, r):
                b, q = r % B, r % 2
                if not missing(i, r):
                    row = row_of(sync, m.log_gate_dram, head_of(i, r))
                    values = m.values_dram.rearrange("(b c p) e -> b p c e", b=B, p=P)[
                        b][:, :, columns_of(sync, head_of(i, r), HEAD_D)]
                    if not opening(i, r, 2):
                        sync.wait_ge(diff_done, nth(i, r - 2))
                    sync.dma_start(gate_row[:, q], row.rearrange("(o t) -> o t", o=1)[
                        :, b * SEQ:(b + 1) * SEQ].broadcast_to([P, SEQ])).then_inc(rows_loaded[q], 16)
                    if not opening(i, r, 2):
                        sync.wait_ge(out_mm, 2 * nth(i, r - 2))
                    sync.dma_start(v[:, q, :, 0:HEAD_D], values).then_inc(v_loaded[q], 16)
                if r % B == 1 and not missing(i, r + B - 1):
                    load_weights(i, r + B - 1)
                if not missing(i, r - 2):
                    out = m.attended_dram.rearrange("(b c p) e -> b p c e", b=B, p=P)[
                        (r - 2) % B][:, :, columns_of(sync, head_of(i, r - 2), REP * HEAD_D)]
                    wait_all(sync, (y_done, 2 * nth(i, r - 2)))
                    sync.dma_start(out, y[:, q].rearrange("p c r e -> p c (r e)")).then_inc(
                        y_stored[q], 16)

            load_weights(0, 0)
            each_unit(sync, body, UNITS, STEPS, 4, TAIL)
            for q in range(2):
                sync.wait_ge(y_stored[q], 16 * UNITS // 2)

        @block.tensor
        def _(pe):
            def project(i, r, kind):
                if missing(i, r):
                    return
                q, b = (r // B) % 2, r % B
                if b == 0 and kind == 0:
                    wait_all(pe, (w_lo_done, head_of(i, r) + 1))
                if not opening(i, r, 1):
                    wait_all(pe, (qk_done, 3 * nth(i, r) - 5 + kind))
                three_passes(pe, proj_ps[:, kind], lambda k: [x[:, q, k, kind] for x in (w_hi, w_lo)],
                             lambda k: [x[:, k, b * SEQ:(b + 1) * SEQ] for x in (m.xn_hi, m.xn_lo)],
                             range(KD)).then_inc(proj_mm, 1)

            def scores(i, r, h):
                if missing(i, r):
                    return
                q = r % 2
                wait_all(pe, (qk_done, 3 * nth(i, r)),
                         *[(square_done, 2 * nth(i, r) - 2 + h)][:h or not opening(i, r, 1)])
                for j in range(CH):
                    end = pe.matmul(score_ps[:, AT[j]:AT[j] + WIDTH[j]], qk[:, q, 2, j * P:(j + 1) * P],
                                    qk[:, q, h, j * P:SEQ], start=True, stop=True)
                end.then_inc(score_mm, 1)

            def outputs(i, r, h):
                if missing(i, r):
                    return
                q = r % 2
                wait_all(pe, (a_done, 2 * nth(i, r) - 1 + h), (v_loaded[q], 16 * nth(i, r, 2)),
                         *[(y_done, 2 * nth(i, r) - 2 + h)][:h or not opening(i, r, 1)])
                for c in range(CH):
                    for j in range(c + 1):
                        at = AT[j] + (c - j) * P
                        end = pe.matmul(out_ps[:, c // 2, (c % 2) * VC:(c % 2 + 1) * VC],
                                        a[:, h, at:at + P], v[:, q, j], start=j == 0, stop=j == c)
                end.then_inc(out_mm, 1)

            def body(i, r):
                project(i, r, 0)
                scores(i, r - 1, 0)
                project(i, r, 1)
                outputs(i, r - 1, 0)
                scores(i, r - 1, 1)
                project(i, r, 2)
                outputs(i, r - 1, 1)

            pe.wait_ge(ones_done, 1)
            each_unit(pe, body, UNITS, STEPS, LEAD, TAIL)

        @block.scalar
        def _(act):
            def round_weights(i, r):
                q = (r // B) % 2
                wait_all(act, (w_loaded, 16 * (head_of(i, r) + 1)),
                         *[(proj_mm, 3 * nth(i, r - B - 1))][:not opening(i, r, 2 * B)])
                act.activation(w_hi[:, q], w_raw[:, :, :, :], ACT.Copy).then_inc(w_hi_done, 1)

            def take(i, r, kind):
                if missing(i, r):
                    return
                wait_all(act, (proj_mm, 3 * nth(i, r) - 2 + kind),
                         *[(score_mm, 2 * nth(i, r - 2))][:not opening(i, r, 2)])
                act.activation(qk[:, r % 2, kind], proj_ps[:, kind], ACT.Copy).then_inc(qk_done, 1)

            def square(i, r, h):
                if missing(i, r):
                    return
                wait_all(act, (score_mm, 2 * nth(i, r) - 1 + h),
                         *[(out_mm, 2 * nth(i, r - 1) - 1 + h)][:not opening(i, r, 1)])
                act.activation(a[:, h], score_ps[:, 0:COLS], ACT.Square,
                               scale=SCALE).then_inc(square_done, 1)

            def body(i, r):
                take(i, r, 0)
                square(i, r - 1, 0)
                take(i, r, 1)
                square(i, r - 1, 1)
                take(i, r, 2)
                if not missing(i, r):
                    wait_all(act, (diff_done, nth(i, r)))
                    act.activation(decay[:, r % 2], decay[:, r % 2], ACT.Exp).then_inc(decay_done, 1)
                if r % B == 2 and not missing(i, r + B - 2):
                    round_weights(i, r + B - 2)

            round_weights(0, 0)
            each_unit(act, body, UNITS, STEPS, LEAD, TAIL)

        @block.vector
        def _(dve):
            def keep_lo(i, r):
                q = (r // B) % 2
                wait_all(dve, (w_hi_done, head_of(i, r) + 1))
                dve.tensor_tensor(w_lo[:, q], w_raw[:, :, :, :], w_hi[:, q].bitcast(F32),
                                  ALU.subtract).then_inc(w_lo_done, 1)

            def take_columns(i, r):
                dve.tensor_copy(gate_cols[:, (r // B) % 2].rearrange("p (o t) -> p o t", o=1),
                                m.log_gate_tm[:, bass.ds(head_of(i, r), 1), :]).then_inc(cols_done, 1)

            def weigh(i, r, h):
                if missing(i, r):
                    return
                wait_all(dve, (square_done, 2 * nth(i, r) - 1 + h), (decay_done, nth(i, r)))
                dve.tensor_tensor(a[:, h], a[:, h], decay[:, r % 2], ALU.mult).then_inc(a_done, 1)

            def divide(i, r, h):
                if missing(i, r):
                    return
                q = r % 2
                n = 2 * nth(i, r) - 1 + h
                wait_all(dve, (out_mm, n), *[(y_stored[q], 16 * nth(i, r - 2, 2))][:not opening(i, r, 2)])
                heads = out_ps[:, :, 0:2 * VC].rearrange("p a (c e) -> p a c e", c=2)
                dve.tensor_scalar(norm[:, h].rearrange("p (a c) -> p a c", a=2), heads[:, :, :, HEAD_D],
                                  1e-6, None, ALU.add).then_inc(norm_done, 1)
                wait_all(dve, (norm_done, n))
                dve.reciprocal(inv[:, h], norm[:, h]).then_inc(inv_done, 1)
                wait_all(dve, (inv_done, n))
                dve.tensor_tensor(
                    y[:, q, :, h].rearrange("p (a c) e -> p a c e", a=2), heads[:, :, :, 0:HEAD_D],
                    inv[:, h].rearrange("p (a c o) -> p a c o", a=2, o=1).broadcast_to(
                        [P, 2, 2, HEAD_D]), ALU.mult).then_inc(y_done, 1)

            def body(i, r):
                if not missing(i, r):
                    b, q = r % B, r % 2
                    if b == 0:
                        take_columns(i, r)
                    wait_all(dve, (rows_loaded[q], 16 * nth(i, r, 2)), (cols_done, head_of(i, r) + 1))
                    for j in range(CH):
                        col = gate_cols[:, (r // B) % 2, CH * b + j:CH * b + j + 1]
                        end = dve.scalar_tensor_tensor(
                            out=decay[:, q, AT[j]:AT[j] + P], in0=gate_row[:, q, j * P:(j + 1) * P],
                            scalar=col, in1=m.never[:, :], op0=ALU.subtract, op1=ALU.min)
                        if j < CH - 1:
                            end = dve.tensor_scalar(
                                decay[:, q, AT[j] + P:AT[j] + WIDTH[j]], gate_row[:, q, (j + 1) * P:SEQ],
                                col, 0.0, ALU.subtract, ALU.min)
                    end.then_inc(diff_done, 1)
                weigh(i, r - 1, 0)
                divide(i, r - 1, 0)
                weigh(i, r - 1, 1)
                divide(i, r - 1, 1)
                if r % B == 2 and not missing(i, r + B - 2):
                    keep_lo(i, r + B - 2)

            dve.memset(v[:, :, :, HEAD_D:VC], 1.0).then_inc(ones_done, 1)
            keep_lo(0, 0)
            each_unit(dve, body, UNITS, STEPS, LEAD, TAIL)


def mlp_up(nc, m):
    STEPS, UNITS, LEAD, TAIL = 2 * B, BLOCKS * B, 6, 2
    LAST = UNITS // STEPS - 1
    with Scope(nc, "mlp_up") as s:
        w_raw = s.sb("w_raw", [P, KD, 2, P])
        w_hi = s.sb("w_hi", [P, 2, KD, 2, P], F32R)
        w_lo = s.sb("w_lo", [P, 2, KD, 2, P], F32R)
        silu_gate, hidden = s.sb("silu_gate", [P, 2, SEQ]), s.sb("hidden", [P, 2, SEQ])
        gate_ps, up_ps = s.ps("gate_ps", [P, 2, SEQ]), s.ps("up_ps", [P, 2, SEQ])
        w_loaded, w_hi_done, w_lo_done, gate_mm, up_mm, gate_done, hidden_done = (
            s.sem(n) for n in ("w_loaded", "w_hi_done", "w_lo_done", "gate_mm", "up_mm", "gate_done",
                               "hidden_done"))
        stored = [s.sem(f"stored{q}") for q in range(2)]
        block = s.block()

        def missing(i, r):
            return opening(i, r, 0) or (isinstance(i, int) and i == LAST and r >= STEPS)

        def nth(i, r, ring=1):
            return i * (STEPS // ring) + r // ring + 1

        def block_of(i, r):
            return i * 2 + r // B

        @block.sync
        def _(sync):
            def load_weights(i, r):
                weights = row_of(sync, m.w_gate_up, block_of(i, r)).rearrange("(p n) -> p n", p=P)
                wait_all(sync, *[(w_lo_done, block_of(i, r))][:not opening(i, r, 1)])
                sync.dma_start(w_raw[:, :, :, :].rearrange("p k c n -> p (k c n)"),
                               weights).then_inc(w_loaded, 16)

            def body(i, r):
                if r % B == 1 and not missing(i, r + B - 1):
                    load_weights(i, r + B - 1)
                if not missing(i, r - 1):
                    q, b = (r - 1) % 2, (r - 1) % B
                    out = row_of(sync, m.hidden_dram, block_of(i, r - 1)).rearrange("(p t) -> p t", p=P)
                    wait_all(sync, (hidden_done, nth(i, r - 1)))
                    sync.dma_start(out[:, b * SEQ:(b + 1) * SEQ], hidden[:, q]).then_inc(stored[q], 16)

            load_weights(0, 0)
            each_unit(sync, body, UNITS, STEPS, 4, TAIL)
            for q in range(2):
                sync.wait_ge(stored[q], 16 * UNITS // 2)

        @block.tensor
        def _(pe):
            def body(i, r):
                if missing(i, r):
                    return
                q, w_q, b = r % 2, (r // B) % 2, r % B
                if b == 0:
                    wait_all(pe, (w_lo_done, block_of(i, r) + 1))
                for kind, (ps, mm) in enumerate(((gate_ps, gate_mm), (up_ps, up_mm))):
                    if kind == 0 and not opening(i, r, 2):
                        wait_all(pe, (hidden_done, nth(i, r - 2)))
                    three_passes(pe, ps[:, q], lambda k: [x[:, w_q, k, kind] for x in (w_hi, w_lo)],
                                 lambda k: [x[:, k, b * SEQ:(b + 1) * SEQ] for x in (m.xn_hi, m.xn_lo)],
                                 range(KD)).then_inc(mm, 1)

            each_unit(pe, body, UNITS, STEPS, LEAD, TAIL)

        @block.scalar
        def _(act):
            def round_weights(i, r):
                q = (r // B) % 2
                wait_all(act, (w_loaded, 16 * (block_of(i, r) + 1)),
                         *[(up_mm, nth(i, r - B - 1))][:not opening(i, r, 2 * B)])
                act.activation(w_hi[:, q], w_raw[:, :, :, :], ACT.Copy).then_inc(w_hi_done, 1)

            def body(i, r):
                if not missing(i, r):
                    wait_all(act, (gate_mm, nth(i, r)),
                             *[(hidden_done, nth(i, r - 2))][:not opening(i, r, 2)])
                    act.activation(silu_gate[:, r % 2], gate_ps[:, r % 2], ACT.Silu).then_inc(gate_done, 1)
                if r % B == 2 and not missing(i, r + B - 2):
                    round_weights(i, r + B - 2)

            round_weights(0, 0)
            each_unit(act, body, UNITS, STEPS, LEAD, TAIL)

        @block.vector
        def _(dve):
            def keep_lo(i, r):
                q = (r // B) % 2
                wait_all(dve, (w_hi_done, block_of(i, r) + 1))
                dve.tensor_tensor(w_lo[:, q], w_raw[:, :, :, :], w_hi[:, q].bitcast(F32),
                                  ALU.subtract).then_inc(w_lo_done, 1)

            def body(i, r):
                q = r % 2
                if not missing(i, r):
                    wait_all(dve, (gate_done, nth(i, r)), (up_mm, nth(i, r)),
                             *[(stored[q], 16 * nth(i, r - 2, 2))][:not opening(i, r, 2)])
                    dve.tensor_tensor(hidden[:, q], silu_gate[:, q], up_ps[:, q],
                                      ALU.mult).then_inc(hidden_done, 1)
                if r % B == 2 and not missing(i, r + B - 2):
                    keep_lo(i, r + B - 2)

            keep_lo(0, 0)
            each_unit(dve, body, UNITS, STEPS, LEAD, TAIL)


def attention_output(nc, m):
    STEPS, LEAD, TAIL = 4, 3, 1
    LAST = TILES // STEPS - 1
    QUARTER = KI // 4
    with Scope(nc, "attn_out") as s:
        w_c = [s.sb(f"w_{x}", [P, KI, D], F32R) for x in ("hi", "lo")]
        w = split_weights(s, "w", [(m.w_c[k], w_c[0][:, k], w_c[1][:, k], None) for k in range(KI)], D)
        bias = s.sb("bias", [P, D])
        y = s.sb("y", [P, 2, KI, P])
        hi, lo = s.sb("y_hi", [P, 2, KI, P], F32R), s.sb("y_lo", [P, 2, KI, P], F32R)
        out = s.sb("out", [P, 2, D])
        turn_ps = s.ps("turn_ps", [P, 4, QUARTER, P])
        out_ps = s.ps("out_ps", [P, 2, D])
        bias_loaded = s.sem("bias_loaded")
        y_loaded = [s.sem(f"y_loaded{q}") for q in range(2)]
        turned, hi_done, lo_done, out_mm, out_done = (
            s.sem(n) for n in ("turned", "hi_done", "lo_done", "out_mm", "out_done"))
        stored = [s.sem(f"stored{q}") for q in range(2)]
        block = s.block()
        y_t = m.attended_dram.rearrange("(n p) d -> n p d", p=P)
        s_t = m.s_dram.rearrange("(n p) d -> n p d", p=P)

        def missing(i, r):
            return opening(i, r, 0) or (isinstance(i, int) and i == LAST and r >= STEPS)

        def nth(i, r, ring=1):
            return i * (STEPS // ring) + r // ring + 1

        @block.sync
        def _(sync):
            def load(i, r):
                q = r % 2
                rows = row_of(sync, y_t, i * STEPS + r).rearrange("(p d) -> p d", p=P)
                wait_all(sync, *[(turned, 4 * nth(i, r - 2))][:not opening(i, r, 2)])
                sync.dma_start(y[:, q].rearrange("p k e -> p (k e)"), rows).then_inc(y_loaded[q], 16)

            def body(i, r):
                if not missing(i, r + 1):
                    load(i, r + 1)
                if not missing(i, r - 1):
                    q = (r - 1) % 2
                    rows = row_of(sync, s_t, i * STEPS + r - 1).rearrange("(p d) -> p d", p=P)
                    wait_all(sync, (out_done, nth(i, r - 1)))
                    sync.dma_start(rows, out[:, q]).then_inc(stored[q], 16)

            load(0, 0)
            sync.dma_start(bias[:, :], m.b_c.broadcast_to([P, D])).then_inc(bias_loaded, 16)
            for n in range(w.n):
                w.load(sync, n)
            each_unit(sync, body, TILES, STEPS, LEAD, TAIL)
            for q in range(2):
                sync.wait_ge(stored[q], 16 * TILES // 2)

        @block.tensor
        def _(pe):
            def turn(i, r):
                if missing(i, r):
                    return
                q = r % 2
                for a in range(4):
                    wait_all(pe, *[(y_loaded[q], 16 * nth(i, r, 2))][:a == 0],
                             *[(lo_done, 4 * nth(i, r) - 7 + a)][:not opening(i, r, 1)])
                    for k in range(QUARTER):
                        end = pe.transpose(turn_ps[:, a, k], y[:, q, a * QUARTER + k], m.ident[:, :])
                    end.then_inc(turned, 1)

            def body(i, r):
                turn(i, r + 1)
                if missing(i, r):
                    return
                q = r % 2
                wait_all(pe, *[(out_done, nth(i, r - 2))][:not opening(i, r, 2)])
                for k in range(KI):
                    if k % QUARTER == 0:
                        wait_all(pe, (lo_done, 4 * nth(i, r) - 3 + k // QUARTER))
                    if opening(i, r, 1):
                        pe.wait_ge(w.done, k + 1)
                    end = three_passes(pe, out_ps[:, q], lambda k: (hi[:, q, k], lo[:, q, k]),
                                       lambda k: [x[:, k] for x in w_c], [k],
                                       first=k == 0, last=k == KI - 1)
                end.then_inc(out_mm, 1)

            turn(0, 0)
            each_unit(pe, body, TILES, STEPS, LEAD, TAIL)

        @block.scalar
        def _(act):
            def body(i, r):
                if missing(i, r):
                    return
                q = r % 2
                for a in range(4):
                    wait_all(act, (turned, 4 * nth(i, r) - 3 + a),
                             *[(out_mm, nth(i, r - 2))][:not opening(i, r, 2)])
                    act.activation(hi[:, q, a * QUARTER:(a + 1) * QUARTER], turn_ps[:, a],
                                   ACT.Copy).then_inc(hi_done, 1)

            body(0, 0)
            for n in range(w.n):
                w.round_hi(act, n)
            each_unit(act, lambda i, r: None if opening(i, r, 1) else body(i, r), TILES, STEPS, LEAD, TAIL)

        @block.vector
        def _(dve):
            def split(i, r):
                q = r % 2
                for a in range(4):
                    cols = slice(a * QUARTER, (a + 1) * QUARTER)
                    wait_all(dve, (hi_done, 4 * nth(i, r) - 3 + a))
                    dve.tensor_tensor(lo[:, q, cols], turn_ps[:, a], hi[:, q, cols].bitcast(F32),
                                      ALU.subtract).then_inc(lo_done, 1)

            def body(i, r):
                if not missing(i, r) and not opening(i, r, 1):
                    split(i, r)
                if not missing(i, r - 1):
                    q = (r - 1) % 2
                    wait_all(dve, (out_mm, nth(i, r - 1)), (bias_loaded, 16),
                             *[(stored[q], 16 * nth(i, r - 3, 2))][:not opening(i, r, 3)])
                    dve.tensor_tensor(out[:, q], out_ps[:, q], bias[:, :], ALU.add).then_inc(out_done, 1)

            split(0, 0)
            for n in range(w.n):
                w.keep_lo(dve, n)
            each_unit(dve, body, TILES, STEPS, LEAD, TAIL)


def mlp_down(nc, m):
    STEPS, LEAD, TAIL = 4, 3, 1
    LAST = TILES // STEPS - 1
    KS = SHARED // P
    with Scope(nc, "mlp_down") as s:
        w_down = [s.sb(f"w_{x}", [P, BLOCKS, D], F32R) for x in ("hi", "lo")]
        w = split_weights(s, "w", [(m.w_mlp_down[k], w_down[0][:, k], w_down[1][:, k], None)
                                   for k in range(BLOCKS)], D)
        h = s.sb("h", [P, 2, BLOCKS, P])
        hi, lo = s.sb("h_hi", [P, 2, BLOCKS, P], F32R), s.sb("h_lo", [P, 2, BLOCKS, P], F32R)
        x1, mixer, routed, total, gate, out = (
            s.sb(n, [P, 2, D]) for n in ("x1", "mixer", "routed", "total", "gate", "out"))
        shared_ps, routed_ps = s.ps("shared_ps", [P, 2, D]), s.ps("routed_ps", [P, 2, D])
        h_loaded = [s.sem(f"h_loaded{q}") for q in range(2)]
        rows_loaded = [s.sem(f"rows_loaded{q}") for q in range(2)]
        hi_done, lo_done, shared_mm, routed_done, total_done, gate_done, gated_done, out_done = (
            s.sem(n) for n in ("hi_done", "lo_done", "shared_mm", "routed_done", "total_done",
                               "gate_done", "gated_done", "out_done"))
        stored = [s.sem(f"stored{q}") for q in range(2)]
        block = s.block()
        x1_t, s_t, out_t = (d.rearrange("(n p) d -> n p d", p=P) for d in (m.x1_dram, m.s_dram, m.out))
        hidden_p = m.hidden_dram.rearrange("k p t -> p k t")

        def missing(i, r):
            return opening(i, r, 0) or (isinstance(i, int) and i == LAST and r >= STEPS)

        def nth(i, r, ring=1):
            return i * (STEPS // ring) + r // ring + 1

        @block.sync
        def _(sync):
            def load(i, r):
                q, t = r % 2, i * STEPS + r
                tokens = columns_of(sync, t, P)
                rows = [row_of(sync, d, t).rearrange("(p d) -> p d", p=P) for d in (x1_t, s_t)]
                if not opening(i, r, 2):
                    sync.wait_ge(lo_done, nth(i, r - 2))
                sync.dma_start(h[:, q], hidden_p[:, :, tokens]).then_inc(h_loaded[q], 16)
                if not opening(i, r, 2):
                    sync.wait_ge(out_done, nth(i, r - 2))
                for tile, source in zip((x1, mixer), rows):
                    sync.dma_start(tile[:, q], source).then_inc(rows_loaded[q], 16)

            def body(i, r):
                if not missing(i, r - 1):
                    q = (r - 1) % 2
                    rows = row_of(sync, out_t, i * STEPS + r - 1).rearrange("(p d) -> p d", p=P)
                    wait_all(sync, (out_done, nth(i, r - 1)))
                    sync.dma_start(rows, out[:, q]).then_inc(stored[q], 16)
                if not missing(i, r + 1):
                    load(i, r + 1)

            load(0, 0)
            for n in range(w.n):
                w.load(sync, n)
            each_unit(sync, body, TILES, STEPS, LEAD, TAIL)
            for q in range(2):
                sync.wait_ge(stored[q], 16 * TILES // 2)

        @block.tensor
        def _(pe):
            def body(i, r):
                if missing(i, r):
                    return
                q = r % 2
                wait_all(pe, (lo_done, nth(i, r)), *[(total_done, nth(i, r - 2))][:not opening(i, r, 2)])
                for ps, ks in ((shared_ps, range(KS)), (routed_ps, range(KS, BLOCKS))):
                    for k in ks:
                        if opening(i, r, 1):
                            pe.wait_ge(w.done, k + 1)
                        end = three_passes(pe, ps[:, q], lambda k: (hi[:, q, k], lo[:, q, k]),
                                           lambda k: [x[:, k] for x in w_down], [k],
                                           first=k == ks[0], last=k == ks[-1])
                end.then_inc(shared_mm, 1)

            each_unit(pe, body, TILES, STEPS, LEAD, TAIL)

        @block.scalar
        def _(act):
            def split(i, r):
                if missing(i, r):
                    return
                q = r % 2
                wait_all(act, (h_loaded[q], 16 * nth(i, r, 2)),
                         *[(shared_mm, nth(i, r - 2))][:not opening(i, r, 2)])
                act.activation(hi[:, q], h[:, q], ACT.Copy).then_inc(hi_done, 1)

            def body(i, r):
                if not opening(i, r, 1):
                    split(i, r)
                if not missing(i, r - 1):
                    q, t = (r - 1) % 2, i * STEPS + r - 1
                    wait_all(act, (shared_mm, nth(i, r - 1)))
                    act.activation(routed[:, q], routed_ps[:, q], ACT.Copy,
                                   scale=m.comb_w[:, bass.ds(t, 1)]).then_inc(routed_done, 1)
                    wait_all(act, (total_done, nth(i, r - 1)))
                    act.activation(gate[:, q], total[:, q], ACT.Silu).then_inc(gate_done, 1)

            split(0, 0)
            for n in range(w.n):
                w.round_hi(act, n)
            each_unit(act, body, TILES, STEPS, LEAD, TAIL)

        @block.vector
        def _(dve):
            def split(i, r):
                q = r % 2
                wait_all(dve, (hi_done, nth(i, r)))
                dve.tensor_tensor(lo[:, q], h[:, q], hi[:, q].bitcast(F32), ALU.subtract).then_inc(lo_done, 1)

            def finish(i, r):
                q = r % 2
                wait_all(dve, (routed_done, nth(i, r)),
                         *[(gate_done, nth(i, r - 2))][:not opening(i, r, 2)])
                dve.tensor_tensor(total[:, q], routed[:, q], shared_ps[:, q], ALU.add).then_inc(total_done, 1)
                wait_all(dve, (gate_done, nth(i, r)), (rows_loaded[q], 32 * nth(i, r, 2)),
                         *[(stored[q], 16 * nth(i, r - 2, 2))][:not opening(i, r, 2)])
                dve.tensor_tensor(gate[:, q], gate[:, q], mixer[:, q], ALU.mult).then_inc(gated_done, 1)
                wait_all(dve, (gated_done, nth(i, r)))
                dve.tensor_tensor(out[:, q], gate[:, q], x1[:, q], ALU.add).then_inc(out_done, 1)

            def body(i, r):
                if not missing(i, r) and not opening(i, r, 1):
                    split(i, r)
                if not missing(i, r - 1):
                    finish(i, r - 1)

            split(0, 0)
            for n in range(w.n):
                w.keep_lo(dve, n)
            each_unit(dve, body, TILES, STEPS, LEAD, TAIL)


_INS = ['L0_attn_hidden_states', 'L0_attn_W_in', 'L0_attn_conv_w', 'L0_attn_conv_b', 'L0_attn_dt_bias',
        'L0_attn_A_log', 'L0_attn_D_param', 'L0_attn_norm_w', 'L0_attn_W_out', 'L0_ffn_W_up',
        'L0_ffn_W_down', 'L0_ffn_W_gate', 'L0_ffn_W_expert', 'L1_attn_Wq', 'L1_attn_Wk', 'L1_attn_Wv',
        'L1_attn_Wg', 'L1_attn_Wc', 'L1_attn_bc', 'L1_ffn_router_weight', 'L1_ffn_sh_gate',
        'L1_ffn_sh_up', 'L1_ffn_sh_down', 'L1_ffn_r_gate', 'L1_ffn_r_up', 'L1_ffn_r_down']


def lay_out(i):
    import numpy as np
    a = {n: np.asarray(v) for n, v in i.items()}
    f = np.float32

    def rows(w):
        return w.reshape(-1, P, w.shape[1])

    def blocks(*parts):
        w = np.stack([p.reshape(-1, P, KD, P) for p in parts])
        return w.transpose(1, 4, 3, 0, 2)

    w_in = a['L0_attn_W_in']
    gate, xs, bc = w_in[:INTER], w_in[INTER:2 * INTER], w_in[2 * INTER:]
    b_w, c_w, dt_w = bc[:STATE], bc[STATE:2 * STATE], bc[2 * STATE:]
    taps = np.concatenate([a['L0_attn_conv_w'], a['L0_attn_conv_b'][:, None]], 1)
    d_rows = np.repeat(a['L0_attn_D_param'], HEAD_P)[:, None]
    pad = np.zeros((INTER, 2), f)
    q = a['L1_attn_Wq'].T.reshape(KV_HEADS, REP, HEAD_D, D)
    out = {
        'x': a['L0_attn_hidden_states'].reshape(TOK, D),
        'w_up': rows(a['L0_ffn_W_up'].T), 'w_down': rows(a['L0_ffn_W_down'].T),
        'w_expert': rows(np.concatenate([a['L0_ffn_W_expert'], a['L0_ffn_W_gate'].T], 1)),
        'w_bcd': rows(np.concatenate([b_w, dt_w, c_w]).T),
        'bc_vec': np.concatenate([taps[INTER:], np.zeros((2 * STATE, 3), f)], 1).reshape(
            2, P, 8).transpose(1, 0, 2),
        'head_vec': np.stack([a['L0_attn_dt_bias'], a['L0_attn_A_log']], 1),
        'w_gate_x': blocks(gate, xs),
        'pair_vec': np.concatenate([taps[:INTER], d_rows, pad], 1).reshape(PAIRS, P, 8),
        'norm_w': a['L0_attn_norm_w'].reshape(KI, P).T, 'w_out': rows(a['L0_attn_W_out'].T),
        'w_gvr': rows(np.concatenate([a['L1_attn_Wg'], a['L1_attn_Wv'],
                                      a['L1_ffn_router_weight'].T], 1)),
        'w_qqk': blocks(q[:, 0].reshape(-1, D), q[:, 1].reshape(-1, D), a['L1_attn_Wk'].T),
        'w_c': rows(a['L1_attn_Wc']), 'b_c': a['L1_attn_bc'].reshape(1, D),
        'w_gate_up': blocks(np.concatenate([a['L1_ffn_sh_gate'], a['L1_ffn_r_gate']]),
                            np.concatenate([a['L1_ffn_sh_up'], a['L1_ffn_r_up']])),
        'w_mlp_down': rows(np.concatenate([a['L1_ffn_sh_down'].T, a['L1_ffn_r_down'].T])),
        'ident': np.eye(P, dtype=f),
        'causal': np.triu(np.ones((P, P), f)),
        'never': np.where(np.arange(P)[None, :] >= np.arange(P)[:, None], f(0), f(-1e30)),
    }
    return {n: np.ascontiguousarray(v) for n, v in out.items()}


class Memory:

    def __init__(self, d, out):
        self.x, self.out = d["x"], out
        self.w_up, self.w_down, self.w_expert = d["w_up"], d["w_down"], d["w_expert"]
        self.w_bcd, self.w_gate_x, self.pair_vec, self.w_out = (
            d["w_bcd"], d["w_gate_x"], d["pair_vec"], d["w_out"])
        self.w_gvr, self.w_qqk, self.w_c, self.b_c = d["w_gvr"], d["w_qqk"], d["w_c"], d["b_c"]
        self.w_gate_up, self.w_mlp_down = d["w_gate_up"], d["w_mlp_down"]


def build(nc, d, out, debug=()):
    with ExitStack() as stack:
        def sb(name, shape, dtype=F32):
            return stack.enter_context(nc.sbuf_tensor(name, shape, dtype))

        def dram(name, shape):
            return nc.dram_tensor(name, shape, F32, kind="ExternalOutput" if name in debug else "Internal").ap()

        m = Memory(d, out)
        m.gate_dram, m.x1_dram, m.s_dram = (dram(n, [TOK, D]) for n in ("gate_s", "x1_s", "s_s"))
        m.ell_dram = dram("ell_s", [PAIRS, 2, TOK])
        m.mixed_dram = dram("mixed_s", [PAIRS, P, TOK])
        m.log_gate_dram = dram("log_gate_s", [KV_HEADS, TOK])
        m.values_dram = dram("values_s", [TOK, KV_DIM])
        m.attended_dram = dram("attended_s", [TOK, Q_DIM])
        m.hidden_dram = dram("hidden_s", [BLOCKS, P, TOK])
        constants = ("ident", "causal", "never", "bc_vec", "head_vec", "norm_w")
        loaded = {n: sb(f"{n}_sb", list(d[n].shape)) for n in constants}
        m.ident, m.causal, m.never, m.bc_vec, m.head_vec, m.norm_w = (loaded[n] for n in constants)
        m.comb_w = sb("comb_w", [P, TILES])
        constants_loaded = nc.alloc_semaphore("constants_loaded")
        with nc.Block() as block:
            @block.sync
            def _(sync):
                for n in constants:
                    sync.dma_start(loaded[n][:], d[n]).then_inc(constants_loaded, 16)
                sync.wait_ge(constants_loaded, 16 * len(constants))

        with nc.sbuf_tensor("square_sum", [P, TOK], F32) as m.square_sum:
            with nc.sbuf_tensor("xn_hi", [P, KD, TOK], F32R) as m.xn_hi, \
                    nc.sbuf_tensor("xn_lo", [P, KD, TOK], F32R) as m.xn_lo:
                normalize(nc, "norm0", m.x, m)
                mixture(nc, m)
                with nc.sbuf_tensor("c_fm", [P, TOK], F32) as m.c_fm, \
                        nc.sbuf_tensor("b_tm", [P, TILES, P], F32) as m.b_tm, \
                        nc.sbuf_tensor("cb", [P, TILES, P], F32) as m.cb, \
                        nc.sbuf_tensor("times_tm", [P, 3 * TILES, HEADS], F32) as m.times_tm, \
                        nc.sbuf_tensor("chunk_decay", [P, HEADS, TILES], F32) as m.chunk_decay:
                    m.dt_tm, m.dt_end_tm, m.ell_tm = (m.times_tm[:, n * TILES:(n + 1) * TILES]
                                                      for n in range(3))
                    ssm_shared(nc, m)
                    ssm_heads(nc, m)
            ssm_output(nc, m)
        with nc.sbuf_tensor("xn1_hi", [P, KD, TOK], F32R) as m.xn_hi, \
                nc.sbuf_tensor("xn1_lo", [P, KD, TOK], F32R) as m.xn_lo:
            normalize(nc, "norm1", m.x1_dram, m)
            with nc.sbuf_tensor("log_gate_tm", [P, KV_HEADS, TILES], F32) as m.log_gate_tm:
                values_and_decays(nc, m)
                power_attention(nc, m)
            mlp_up(nc, m)
        attention_output(nc, m)
        mlp_down(nc, m)


def kernel(**inputs):
    import concourse.bacc as bacc
    from concourse.bass_utils import run_bass_kernel_spmd

    arrays = lay_out({n: inputs[n] for n in _INS})
    nc = bacc.Bacc("TRN2", target_bir_lowering=False, num_devices=1)
    d = {n: nc.dram_tensor(f"in_{n}", list(a.shape), F32, kind="ExternalInput").ap()
         for n, a in arrays.items()}
    out = nc.dram_tensor("out", [TOK, D], F32, kind="ExternalOutput").ap()
    build(nc, d, out)
    r = run_bass_kernel_spmd(nc, [{f"in_{n}": a for n, a in arrays.items()}], core_ids=[0])
    return r.results[0]["out"].reshape(B, SEQ, D)
```

```python
from contextlib import ExitStack

import concourse.bass as bass
from concourse import mybir

F32 = mybir.dt.float32
F32R = mybir.dt.float32r
ACT = mybir.ActivationFunctionType
ALU = mybir.AluOpType
AX = mybir.AxisListType

P = 128
B, SEQ, D = 4, 512, 512
TOK = B * SEQ
TILES = TOK // P
CH = SEQ // P
KD = D // P
LN_EPS = 1e-5

HEADS, HEAD_P, STATE, TAPS = 32, 64, 128, 4
INTER = HEADS * HEAD_P
PAIRS = INTER // P
KI = INTER // P
EXPERTS = 8
KV_HEADS, REP, HEAD_D = 8, 2, 128
Q_DIM, KV_DIM = KV_HEADS * REP * HEAD_D, KV_HEADS * HEAD_D
SHARED, ROUTED = 2048, 256
HIDDEN = SHARED + ROUTED
BLOCKS = HIDDEN // P


def three_passes(pe, out, left, right, ks, first=True, last=True):
    ks = list(ks)
    for k in ks:
        (l_hi, l_lo), (r_hi, r_lo) = left(k), right(k)
        pe.matmul(out, l_lo, r_hi, start=first and k == ks[0], stop=False)
        pe.matmul(out, l_hi, r_lo, start=False, stop=False)
        end = pe.matmul(out, l_hi, r_hi, start=False, stop=last and k == ks[-1])
    return end


class Scope:

    def __init__(self, nc, stage):
        self.nc, self.stage, self.stack, self.sems = nc, stage, ExitStack(), []

    def __enter__(self):
        self.stack.__enter__()
        return self

    def __exit__(self, *exc):
        self.stack.__exit__(*exc)
        if exc[0] is None:
            self.nc.clear_and_free_semaphores(self.sems)
            self.nc.all_engine_barrier()

    def sb(self, name, shape, dtype=F32):
        return self.stack.enter_context(self.nc.sbuf_tensor(f"{self.stage}_{name}", shape, dtype))

    def ps(self, name, shape):
        return self.stack.enter_context(self.nc.psum_tensor(f"{self.stage}_{name}", shape, F32))

    def sem(self, name):
        self.sems.append(self.nc.alloc_semaphore(f"{self.stage}_{name}"))
        return self.sems[-1]

    def block(self):
        return self.stack.enter_context(self.nc.Block())


def normalize(nc, stage, x_dram, m):
    G = 4
    x_g = x_dram.rearrange("(g j p) d -> g p j d", j=G, p=P)
    with Scope(nc, stage) as s:
        x = s.sb("x", [P, 2, G, D])
        xn = s.sb("xn", [P, G, D])
        stats = s.sb("stats", [P, G, 6])
        mv = s.sb("mean_var", [P, G, 2])
        var_eps = s.sb("var_eps", [P, G])
        std = s.sb("std", [P, G])
        rstd = s.sb("rstd", [P, G])
        turned = s.ps("turned", [P, G, KD, P])
        x_loaded = [s.sem(f"x_loaded{i}") for i in range(2)]
        stats_done = s.sem("stats_done")
        var_done = s.sem("var_done")
        std_done = s.sem("std_done")
        rstd_done = s.sem("rstd_done")
        xn_done = s.sem("xn_done")
        turned_done = s.sem("turned_done")
        hi_done = s.sem("hi_done")
        lo_done = s.sem("lo_done")
        block = s.block()

        @block.sync
        def _(sync):
            for g in range(TILES // G):
                if g >= 2:
                    sync.wait_ge(xn_done, G * (g - 1))
                sync.dma_start(x[:, g % 2], x_g[g]).then_inc(x_loaded[g % 2], 16)

        @block.vector
        def _(dve):
            for g in range(TILES // G):
                dve.wait_ge(x_loaded[g % 2], 16 * (g // 2 + 1))
                for j in range(G):
                    dve.bn_stats(stats[:, j], x[:, g % 2, j]).then_inc(stats_done, 1)
                for j in range(G):
                    dve.wait_ge(stats_done, G * g + j + 1)
                    dve.bn_aggr(mv[:, j], stats[:, j]).then_inc(var_done, 1)
                dve.wait_ge(var_done, (G + 1) * g + G)
                dve.tensor_scalar(var_eps[:, :], mv[:, :, 1], LN_EPS, None, ALU.add).then_inc(var_done, 1)
                dve.wait_ge(std_done, g + 1)
                dve.reciprocal(rstd[:, :], std[:, :]).then_inc(rstd_done, 1)
                dve.wait_ge(rstd_done, g + 1)
                for j in range(G):
                    if g >= 1:
                        dve.wait_ge(turned_done, G * (g - 1) + j + 1)
                    dve.tensor_scalar(xn[:, j], x[:, g % 2, j], mv[:, j, 0:1], rstd[:, j:j + 1],
                                      ALU.subtract, ALU.mult).then_inc(xn_done, 1)
                for j in range(G):
                    t = G * g + j
                    dve.wait_ge(hi_done, t + 1)
                    dve.tensor_tensor(m.xn_lo[:, :, t * P:(t + 1) * P], turned[:, j],
                                      m.xn_hi[:, :, t * P:(t + 1) * P].bitcast(F32),
                                      ALU.subtract).then_inc(lo_done, 1)

        @block.scalar
        def _(act):
            for g in range(TILES // G):
                act.wait_ge(var_done, (G + 1) * (g + 1))
                act.activation(std[:, :], var_eps[:, :], ACT.Sqrt).then_inc(std_done, 1)
                for j in range(G):
                    t = G * g + j
                    act.wait_ge(turned_done, t + 1)
                    act.activation(m.xn_hi[:, :, t * P:(t + 1) * P], turned[:, j],
                                   ACT.Copy).then_inc(hi_done, 1)

        @block.tensor
        def _(pe):
            for g in range(TILES // G):
                for j in range(G):
                    pe.wait_ge(xn_done, G * g + j + 1)
                    if g >= 1:
                        pe.wait_ge(lo_done, G * (g - 1) + j + 1)
                    for k in range(KD):
                        ins = pe.transpose(turned[:, j, k], xn[:, j, k * P:(k + 1) * P], m.ident[:, :])
                    ins.then_inc(turned_done, 1)


class Steps:

    def __init__(self, load, round_hi, keep_lo, done, n, ring):
        self.load, self.round_hi, self.keep_lo = load, round_hi, keep_lo
        self.done, self.n, self.ring = done, n, ring


def split_weights(s, name, pieces, widest, ring=3):
    raw = s.sb(f"{name}_raw", [P, ring, widest])
    loaded = [s.sem(f"{name}_loaded{i}") for i in range(ring)]
    hi_done, lo_done = s.sem(f"{name}_hi_done"), s.sem(f"{name}_lo_done")

    def width(n):
        return pieces[n][1].shape[-1]

    def load(sync, n):
        if n >= ring:
            sync.wait_ge(lo_done, n - ring + 1)
        sync.dma_start(raw[:, n % ring, 0:width(n)], pieces[n][0]).then_inc(loaded[n % ring], 16)

    def round_hi(act, n):
        _, hi, _, scale = pieces[n]
        act.wait_ge(loaded[n % ring], 16 * (n // ring + 1))
        act.activation(hi, raw[:, n % ring, 0:width(n)], ACT.Identity,
                       scale=1.0 if scale is None else scale).then_inc(hi_done, 1)

    def keep_lo(dve, n):
        _, hi, lo, scale = pieces[n]
        dve.wait_ge(hi_done, n + 1)
        if scale is None:
            dve.tensor_tensor(lo, raw[:, n % ring, 0:width(n)], hi.bitcast(F32),
                              ALU.subtract).then_inc(lo_done, 1)
        else:
            dve.scalar_tensor_tensor(out=lo, in0=raw[:, n % ring, 0:width(n)], scalar=scale,
                                     in1=hi.bitcast(F32), op0=ALU.mult,
                                     op1=ALU.subtract).then_inc(lo_done, 1)

    return Steps(load, round_hi, keep_lo, lo_done, len(pieces), ring)


def norm_and_mixture(nc, m):
    G = CH
    E_COLS = D + EXPERTS
    EH = E_COLS // 2
    with Scope(nc, "mix") as s:
        up = [s.sb(f"up_{x}", [P, KD, D], F32R) for x in ("hi", "lo")]
        down = [s.sb(f"down_{x}", [P, KD, D], F32R) for x in ("hi", "lo")]
        expert = [s.sb(f"expert_{x}", [P, KD, E_COLS], F32R) for x in ("hi", "lo")]
        h_hi = s.sb("h_hi", [P, 2, KD, SEQ], F32R)
        h_lo = s.sb("h_lo", [P, 2, KD, SEQ], F32R)
        top8 = s.sb("top8", [P, 2, 8])
        below = s.sb("below", [P, 2, 2])
        e2 = s.sb("e2", [P, 2, 2])
        esum = s.sb("esum", [P, 2])
        einv = s.sb("einv", [P, 2])
        rw = s.sb("rw", [P, 2, 2])
        rsum = s.sb("rsum", [P, 2])
        scaled = s.sb("scaled", [P, 2, D])
        total = s.sb("total", [P, CH, D])
        gate = m.b_tm[:, :, :].rearrange("p t n -> p (t n)").rearrange("p (c d) -> p c d", c=CH)
        gate_stored = m.gate_stored
        x, xn = s.sb("x", [P, 2, G, D]), s.sb("xn", [P, G, D])
        stats, mv = s.sb("stats", [P, G, 6]), s.sb("mean_var", [P, G, 2])
        var_eps, std, rstd = (s.sb(n, [P, G]) for n in ("var_eps", "std", "rstd"))
        up_ps = s.ps("up_ps", [P, 2, SEQ])
        sh_ps = s.ps("sh_ps", [P, 2, D])
        ex_ps = s.ps("ex_ps", [P, 2, 2, 512])
        turned = ex_ps[:, :, :, :].rearrange("p a b (k t) -> p (a b) k t", t=P)
        pieces = [(dram[k], w[0][:, k], w[1][:, k], None)
                  for dram, w in ((m.w_up, up), (m.w_down, down), (m.w_expert, expert))
                  for k in range(KD)]
        w = split_weights(s, "w", pieces, E_COLS)
        x_loaded = [[s.sem(f"x_loaded{q}_{j}") for j in range(G)] for q in range(2)]
        stats_done, var_done, std_done, rstd_done, xn_done, turned_done, hi_done, lo_done = (
            s.sem(n) for n in ("stats_done", "var_done", "std_done", "rstd_done", "xn_done",
                               "turned_done", "hi_done", "lo_done"))
        up_done = s.sem("up_done")
        h_hi_done = s.sem("h_hi_done")
        h_lo_done = s.sem("h_lo_done")
        ffn_done = s.sem("ffn_done")
        top_done = s.sem("top_done")
        below_done = s.sem("below_done")
        e2_done = s.sem("e2_done")
        rw_step = s.sem("rw_step")
        scaled_done = s.sem("scaled_done")
        total_done = s.sem("total_done")
        gate_done = s.sem("gate_done")
        block = s.block()
        gate_b = m.gate_dram.rearrange("(b c p) d -> b p c d", b=B, p=P)

        x_g = m.x.rearrange("(g j p) d -> g j p d", j=G, p=P)

        @block.sync
        def _(sync):
            def load(g):
                for j in range(G):
                    if g >= 2:
                        sync.wait_ge(xn_done, G * (g - 2) + j + 1)
                    sync.dma_start(x[:, g % 2, j], x_g[g, j]).then_inc(x_loaded[g % 2][j], 16)

            load(0)
            for tile, source in m.constants:
                sync.dma_start(tile[:], source).then_inc(m.constants_loaded, 16)
            for n in range(KD):
                w.load(sync, n)
            load(1)
            for n in range(KD, KD + w.ring):
                w.load(sync, n)
            load(2)
            load(3)
            for n in range(KD + w.ring, w.n):
                w.load(sync, n)
            sync.wait_ge(m.constants_loaded, 16 * len(m.constants))
            for b in range(B):
                sync.wait_ge(gate_done, b + 1)
                sync.dma_start(gate_b[b], gate[:, :, :]).then_inc(gate_stored, 16)

        @block.tensor
        def _(pe):
            def turn(g):
                for j in range(G):
                    pe.wait_ge(xn_done, G * g + j + 1)
                    if g >= 1:
                        pe.wait_ge(lo_done, G * (g - 1) + j + 1)
                    for k in range(KD):
                        end = pe.transpose(turned[:, j, k], xn[:, j, k * P:(k + 1) * P], m.ident[:, :])
                    end.then_inc(turned_done, 1)

            def up_product(b):
                pe.wait_ge(lo_done, G * (b + 1))
                for f in range(KD):
                    n = KD * b + f
                    if n >= 2:
                        pe.wait_ge(h_lo_done, n - 1)
                    for k in range(KD):
                        if n == 0:
                            pe.wait_ge(w.done, k + 1)
                        end = three_passes(
                            pe, up_ps[:, n % 2],
                            lambda k: [x[:, k, f * P:(f + 1) * P] for x in up],
                            lambda k: [x[:, k, b * SEQ:(b + 1) * SEQ] for x in (m.xn_hi, m.xn_lo)],
                            [k], first=k == 0, last=k == KD - 1)
                    end.then_inc(up_done, 1)

            def down_and_expert(b):
                for j in range(CH):
                    t = CH * b + j
                    pe.wait_ge(h_lo_done, KD * (b + 1))
                    if t == 0:
                        pe.wait_ge(w.done, w.n)
                        pe.wait_ge(lo_done, TILES)
                    if t >= 2:
                        pe.wait_ge(total_done, t - 1)
                    three_passes(pe, sh_ps[:, t % 2],
                                 lambda f: [x[:, b % 2, f, j * P:(j + 1) * P] for x in (h_hi, h_lo)],
                                 lambda f: [x[:, f] for x in down], range(KD))
                    for half in range(2):
                        end = three_passes(
                            pe, ex_ps[:, t % 2, half, 0:EH],
                            lambda k: [x[:, k, t * P:(t + 1) * P] for x in (m.xn_hi, m.xn_lo)],
                            lambda k: [x[:, k, half * EH:(half + 1) * EH] for x in expert], range(KD))
                    end.then_inc(ffn_done, 1)

            pe.wait_ge(m.constants_loaded, 16 * len(m.constants))
            turn(0)
            up_product(0)
            turn(1)
            up_product(1)
            turn(2)
            turn(3)
            down_and_expert(0)
            for b in range(1, B):
                if b + 1 < B:
                    up_product(b + 1)
                down_and_expert(b)

        @block.scalar
        def _(act):
            def relu_hi(b):
                for f in range(KD):
                    n = KD * b + f
                    act.wait_ge(up_done, n + 1)
                    if b >= 2:
                        act.wait_ge(ffn_done, CH * (b - 1))
                    act.activation(h_hi[:, b % 2, f], up_ps[:, n % 2], ACT.Relu).then_inc(h_hi_done, 1)

            def deviations(g):
                act.wait_ge(var_done, (G + 1) * (g + 1))
                act.activation(std[:, :], var_eps[:, :], ACT.Sqrt).then_inc(std_done, 1)

            def round_xn(g):
                for t in range(G * g, G * (g + 1)):
                    act.wait_ge(turned_done, t + 1)
                    act.activation(m.xn_hi[:, :, t * P:(t + 1) * P], turned[:, t % G],
                                   ACT.Copy).then_inc(hi_done, 1)

            deviations(0)
            for n in range(KD):
                w.round_hi(act, n)
            round_xn(0)
            deviations(1)
            relu_hi(0)
            round_xn(1)
            deviations(2)
            for n in range(KD, 2 * KD):
                w.round_hi(act, n)
            relu_hi(1)
            deviations(3)
            round_xn(2)
            for n in range(2 * KD, w.n):
                w.round_hi(act, n)
            round_xn(3)
            for b in range(B):
                if 1 <= b < B - 1:
                    relu_hi(b + 1)
                for j in range(CH):
                    t = CH * b + j
                    act.wait_ge(below_done, t + 1)
                    act.activation(e2[:, t % 2], below[:, t % 2], ACT.Exp).then_inc(e2_done, 1)
                    act.wait_ge(rw_step, 4 * (t + 1))
                    if t >= 2:
                        act.wait_ge(total_done, t - 1)
                    act.activation(scaled[:, t % 2, 0:EH], ex_ps[:, t % 2, 0, 0:EH], ACT.Copy,
                                   scale=rsum[:, t % 2:t % 2 + 1]).then_inc(scaled_done, 1)
                    act.activation(scaled[:, t % 2, EH:D], ex_ps[:, t % 2, 1, 0:D - EH], ACT.Copy,
                                   scale=rsum[:, t % 2:t % 2 + 1]).then_inc(scaled_done, 1)
                act.wait_ge(total_done, CH * (b + 1))
                if b >= 1:
                    act.wait_ge(gate_stored, 16 * b)
                act.activation(gate[:, :, :], total[:, :, :], ACT.Silu).then_inc(gate_done, 1)

        @block.vector
        def _(dve):
            def relu_lo(b):
                for f in range(KD):
                    n = KD * b + f
                    dve.wait_ge(h_hi_done, n + 1)
                    dve.scalar_tensor_tensor(out=h_lo[:, b % 2, f], in0=up_ps[:, n % 2], scalar=0.0,
                                             in1=h_hi[:, b % 2, f].bitcast(F32),
                                             op0=ALU.max, op1=ALU.subtract).then_inc(h_lo_done, 1)

            def variances(g):
                if g >= 1:
                    dve.wait_ge(xn_done, G * g)
                for j in range(G):
                    dve.wait_ge(x_loaded[g % 2][j], 16 * (g // 2 + 1))
                    dve.bn_stats(stats[:, j], x[:, g % 2, j]).then_inc(stats_done, 1)
                for j in range(G):
                    dve.wait_ge(stats_done, G * g + j + 1)
                    dve.bn_aggr(mv[:, j], stats[:, j]).then_inc(var_done, 1)
                dve.wait_ge(var_done, (G + 1) * g + G)
                dve.tensor_scalar(var_eps[:, :], mv[:, :, 1], LN_EPS, None, ALU.add).then_inc(var_done, 1)

            def scale(g):
                dve.wait_ge(std_done, g + 1)
                dve.reciprocal(rstd[:, :], std[:, :]).then_inc(rstd_done, 1)
                dve.wait_ge(rstd_done, g + 1)
                for j in range(G):
                    if g >= 1:
                        dve.wait_ge(turned_done, G * (g - 1) + j + 1)
                    dve.tensor_scalar(xn[:, j], x[:, g % 2, j], mv[:, j, 0:1], rstd[:, j:j + 1],
                                      ALU.subtract, ALU.mult).then_inc(xn_done, 1)

            def keep_xn_lo(g):
                for t in range(G * g, G * (g + 1)):
                    dve.wait_ge(hi_done, t + 1)
                    dve.tensor_tensor(m.xn_lo[:, :, t * P:(t + 1) * P], turned[:, t % G],
                                      m.xn_hi[:, :, t * P:(t + 1) * P].bitcast(F32),
                                      ALU.subtract).then_inc(lo_done, 1)

            variances(0)
            scale(0)
            keep_xn_lo(0)
            variances(1)
            scale(1)
            variances(2)
            relu_lo(0)
            keep_xn_lo(1)
            scale(2)
            variances(3)
            relu_lo(1)
            keep_xn_lo(2)
            scale(3)
            keep_xn_lo(3)
            for b in range(B):
                if 1 <= b < B - 1:
                    relu_lo(b + 1)
                for j in range(CH):
                    t, i = CH * b + j, (CH * b + j) % 2
                    dve.wait_ge(ffn_done, t + 1)
                    dve.max(top8[:, i], ex_ps[:, i, 1, D - EH:EH]).then_inc(top_done, 1)
                    dve.wait_ge(top_done, t + 1)
                    dve.tensor_scalar(below[:, i], top8[:, i, 0:2], top8[:, i, 0:1], None,
                                      ALU.subtract).then_inc(below_done, 1)
                    dve.wait_ge(e2_done, t + 1)
                    dve.tensor_tensor(esum[:, i:i + 1], e2[:, i, 0:1], e2[:, i, 1:2],
                                      ALU.add).then_inc(rw_step, 1)
                    dve.wait_ge(rw_step, 4 * t + 1)
                    dve.reciprocal(einv[:, i:i + 1], esum[:, i:i + 1]).then_inc(rw_step, 1)
                    dve.wait_ge(rw_step, 4 * t + 2)
                    dve.tensor_scalar(rw[:, i], e2[:, i], einv[:, i:i + 1], None,
                                      ALU.mult).then_inc(rw_step, 1)
                    dve.wait_ge(rw_step, 4 * t + 3)
                    dve.tensor_tensor(rsum[:, i:i + 1], rw[:, i, 0:1], rw[:, i, 1:2],
                                      ALU.add).then_inc(rw_step, 1)
                    dve.wait_ge(scaled_done, 2 * (t + 1))
                    if b >= 1 and j == 0:
                        dve.wait_ge(gate_done, b)
                    dve.tensor_tensor(total[:, j], scaled[:, i], sh_ps[:, i],
                                      ALU.add).then_inc(total_done, 1)

        @block.gpsimd
        def _(pool):
            for n in range(w.n):
                w.keep_lo(pool, n)


def ssm_shared(nc, m):
    with Scope(nc, "shared") as s:
        COLS = 2 * STATE + HEADS
        DT0, C0 = STATE, STATE + HEADS
        starts = {"dt": DT0, "B": 0, "C": C0}
        w_bcd = [s.sb(f"w_{x}", [P, KD, COLS], F32R) for x in ("hi", "lo")]
        raw = s.sb("raw", [P, 2, B, TAPS - 1 + SEQ])
        b_fm = s.sb("b_fm", [P, TOK])
        dtx = s.sb("dtx", [HEADS, TOK])
        dt_abs = s.sb("dt_abs", [HEADS, TOK])
        dt_exp = s.sb("dt_exp", [HEADS, TOK])
        dt_one = s.sb("dt_one", [HEADS, TOK])
        dt_err = s.sb("dt_err", [HEADS, TOK])
        dt = s.sb("dt", [HEADS, TOK])
        keep = m.cb[0:HEADS].rearrange("h t p -> h (t p)")
        ell = s.sb("ell", [HEADS, TILES, P])
        a_exp = s.sb("a_exp", [HEADS, 1])
        end_exp = s.sb("end_exp", [HEADS, TILES])
        diag = s.sb("diag", [HEADS, HEADS, TILES])
        ones = s.sb("ones", [HEADS, P])
        la, to_end, end_w, dt_end, dt_log = dt_abs, dt_exp, dt_one, dt_err, dt_one
        proj_ps = s.ps("proj_ps", [P, 3, SEQ])
        turn_ps = s.ps("turn_ps", [P, 4, 512])
        w = split_weights(s, "w", [(m.w_bcd[k], w_bcd[0][:, k], w_bcd[1][:, k], None)
                                   for k in range(KD)], COLS)
        proj_done, proj_read = s.sem("proj_done"), s.sem("proj_read")
        abs_done, exp_done, one_done = s.sem("abs_done"), s.sem("exp_done"), s.sem("one_done")
        log_done, err_done, log1p_done = s.sem("log_done"), s.sem("err_done"), s.sem("log1p_done")
        relu_done = s.sem("relu_done")
        dt_done, la_done, keep_done, ell_done = (s.sem("dt_done"), s.sem("la_done"),
                                                 s.sem("keep_done"), s.sem("ell_done"))
        a_done, to_end_done, end_w_done, dt_end_done = (s.sem("a_done"), s.sem("to_end_done"),
                                                        s.sem("end_w_done"), s.sem("dt_end_done"))
        end_exp_done, diag_done = s.sem("end_exp_done"), s.sem("diag_done")
        pad_done, conv_done, silu_done = s.sem("pad_done"), s.sem("conv_done"), s.sem("silu_done")
        turned, turned_read = s.sem("turned"), s.sem("turned_read")
        cb_done, ell_stored = s.sem("cb_done"), s.sem("ell_stored")
        block = s.block()

        N_TURN, N_CB, N_TABLE = TILES // 4, TILES // 4, 3
        CB0 = N_TURN
        TABLE0 = CB0 + N_CB

        @block.sync
        def _(sync):
            for n in range(w.n):
                w.load(sync, n)
            sync.wait_ge(ell_done, 1)
            sync.dma_start(m.ell_dram.rearrange("a h t -> (a h) t"), ell[:, :, :].rearrange("h t p -> h (t p)")).then_inc(ell_stored, 16)
            sync.wait_ge(ell_stored, 16)

        @block.tensor
        def _(pe):
            for n, (kind, b) in enumerate([(k, b) for k in ("dt", "B", "C") for b in range(B)]):
                if n >= 3:
                    pe.wait_ge(proj_read, n - 2)
                c0 = starts[kind]
                for k in range(KD):
                    if n == 0:
                        pe.wait_ge(w.done, k + 1)
                    end = three_passes(pe, proj_ps[:, n % 3],
                                       lambda k: [x[:, k, c0:c0 + P] for x in w_bcd],
                                       lambda k: [x[:, k, b * SEQ:(b + 1) * SEQ]
                                                  for x in (m.xn_hi, m.xn_lo)],
                                       [k], first=k == 0, last=k == KD - 1)
                end.then_inc(proj_done, 1)
            pe.wait_ge(silu_done, 1)
            for n in range(N_TURN):
                for j in range(4):
                    t = 4 * n + j
                    end = pe.transpose(turn_ps[:, n, j * P:(j + 1) * P], b_fm[:, t * P:(t + 1) * P],
                                       m.ident[:, :])
                end.then_inc(turned, 1)
            pe.wait_ge(silu_done, 2)
            for n in range(N_CB):
                pe.wait_ge(turned_read, n + 1)
                for j in range(4):
                    t = 4 * n + j
                    end = pe.matmul(turn_ps[:, n, j * P:(j + 1) * P], b_fm[:, t * P:(t + 1) * P],
                                    m.c_fm[:, t * P:(t + 1) * P], start=True, stop=True)
                end.then_inc(turned, 1)
            for n, (table, ready) in enumerate(((dt, dt_done), (None, ell_done), (dt_end, dt_end_done))):
                pe.wait_ge(ready, 1)
                pe.wait_ge(cb_done, n + 1)
                for t in range(TILES):
                    src = ell[:, t] if table is None else table[:, t * P:(t + 1) * P]
                    end = pe.transpose(turn_ps[:, n, t * HEADS:(t + 1) * HEADS], src,
                                       m.ident[0:HEADS, 0:HEADS])
                end.then_inc(turned, 1)
            pe.wait_ge(diag_done, 1)
            pe.wait_ge(cb_done, N_CB)
            pe.matmul(turn_ps[:, N_TABLE, :], ones[:, :], diag[:, :, :].rearrange("h g t -> h (g t)"),
                      start=True, stop=True).then_inc(turned, 1)

        @block.scalar
        def _(act):
            for n in range(w.n):
                w.round_hi(act, n)
            act.activation(a_exp[:, :], m.head_vec[:, 1:2], ACT.Exp).then_inc(a_done, 1)
            for b in range(B):
                act.wait_ge(proj_done, b + 1)
                act.activation(dtx[:, b * SEQ:(b + 1) * SEQ], proj_ps[0:HEADS, b % 3], ACT.Identity,
                               bias=m.head_vec[:, 0:1]).then_inc(proj_read, 1)
            act.wait_ge(proj_read, B)
            act.activation(dt_abs[:, :], dtx[:, :], ACT.Abs).then_inc(abs_done, 1)
            act.wait_ge(abs_done, 1)
            act.activation(dt_exp[:, :], dt_abs[:, :], ACT.Exp, scale=-1.0).then_inc(exp_done, 1)
            for n in range(B, 3 * B):
                kind, b = (n - B) // B, n % B
                act.wait_ge(proj_done, n + 1)
                act.activation(raw[:, kind, b, TAPS - 1:], proj_ps[:, n % 3],
                               ACT.Copy).then_inc(proj_read, 1)
                if n == 2 * B - 1:
                    act.wait_ge(err_done, 1)
                    act.activation(dt_log[:, :], dt_one[:, :], ACT.Ln).then_inc(log_done, 1)
            for kind, dest in enumerate((b_fm, m.c_fm)):
                act.wait_ge(conv_done, TAPS * (kind + 1))
                act.activation(dest[:, :], dest[:, :], ACT.Silu).then_inc(silu_done, 1)
            act.wait_ge(m.gate_stored, 16 * B)
            for n in range(N_TURN):
                act.wait_ge(turned, n + 1)
                act.activation(m.b_tm[:, 4 * n:4 * n + 4], turn_ps[:, n, :].rearrange(
                    "p (t n) -> p t n", n=P), ACT.Copy).then_inc(turned_read, 1)
            act.wait_ge(to_end_done, 1)
            act.activation(end_w[:, :], to_end[:, :], ACT.Exp).then_inc(end_w_done, 1)
            act.activation(end_exp[:, :], ell[:, :, P - 1], ACT.Exp).then_inc(end_exp_done, 1)
            for n, dest in enumerate((m.dt_tm, m.ell_tm, m.dt_end_tm)):
                act.wait_ge(turned, TABLE0 + n + 1)
                act.activation(dest, turn_ps[:, n, :].rearrange("p (t h) -> p t h", h=HEADS),
                               ACT.Copy).then_inc(turned_read, 1)
            act.wait_ge(turned, TABLE0 + N_TABLE + 1)
            act.activation(m.chunk_decay[:, :, :], turn_ps[:, N_TABLE, :].rearrange(
                "p (h t) -> p h t", t=TILES), ACT.Copy).then_inc(turned_read, 1)

        @block.vector
        def _(dve):
            for n in range(w.n):
                w.keep_lo(dve, n)
            dve.wait_ge(exp_done, 1)
            dve.tensor_scalar(dt_one[:, :], dt_exp[:, :], 1.0, None, ALU.add).then_inc(one_done, 1)
            dve.wait_ge(one_done, 1)
            dve.scalar_tensor_tensor(out=dt_err[:, :], in0=dt_one[:, :], scalar=1.0, in1=dt_exp[:, :],
                                     op0=ALU.subtract, op1=ALU.subtract).then_inc(err_done, 1)
            dve.wait_ge(pad_done, 2)
            for kind in range(2):
                dve.wait_ge(proj_read, B * (kind + 2))
                vec = m.bc_vec[:, kind]
                conv = (b_fm, m.c_fm)[kind][:, :].rearrange("p (b t) -> p b t", b=B)
                dve.tensor_scalar(conv, raw[:, kind, :, 0:SEQ], vec[:, 0:1], vec[:, TAPS:TAPS + 1],
                                  ALU.mult, ALU.add).then_inc(conv_done, 1)
                for j in range(1, TAPS):
                    dve.wait_ge(conv_done, TAPS * kind + j)
                    dve.scalar_tensor_tensor(out=conv, in0=raw[:, kind, :, j:j + SEQ],
                                             scalar=vec[:, j:j + 1], in1=conv,
                                             op0=ALU.mult, op1=ALU.add).then_inc(conv_done, 1)
            dve.wait_ge(la_done, 1)
            dve.wait_ge(keep_done, 2)
            dve.tensor_tensor_scan(ell[:, :, :].rearrange("h t p -> h (t p)"), keep[:, :], la[:, :], 0.0,
                                   ALU.mult, ALU.add).then_inc(ell_done, 1)
            dve.wait_ge(ell_done, 1)
            dve.tensor_tensor(to_end[:, :].rearrange("h (t p) -> h t p", p=P),
                              ell[:, :, P - 1:P].broadcast_to([HEADS, TILES, P]), ell[:, :, :],
                              ALU.subtract).then_inc(to_end_done, 1)
            for n in range(N_CB):
                dve.wait_ge(turned, CB0 + n + 1)
                dve.tensor_tensor(m.cb[:, 4 * n:4 * n + 4], turn_ps[:, n, :].rearrange(
                    "p (t n) -> p t n", n=P),
                    m.causal[:, :].rearrange("p (o n) -> p o n", o=1).broadcast_to([P, 4, P]),
                    ALU.mult).then_inc(cb_done, 1)
            dve.wait_ge(end_w_done, 1)
            dve.tensor_tensor(dt_end[:, :], end_w[:, :], dt[:, :], ALU.mult).then_inc(dt_end_done, 1)
            dve.wait_ge(end_exp_done, 1)
            dve.tensor_tensor(diag[:, :, :],
                              m.ident[0:HEADS, 0:HEADS].rearrange("h (g o) -> h g o", o=1).broadcast_to(
                                  [HEADS, HEADS, TILES]),
                              end_exp[:, :].rearrange("h (o t) -> h o t", o=1).broadcast_to(
                                  [HEADS, HEADS, TILES]), ALU.mult).then_inc(diag_done, 1)

        @block.gpsimd
        def _(pool):
            pool.memset(ones[:, :], 1.0).then_inc(pad_done, 1)
            pool.memset(raw[:, :, :, 0:TAPS - 1], 0.0).then_inc(pad_done, 1)
            pool.memset(keep[:, :], 1.0).then_inc(keep_done, 1)
            pool.wait_ge(keep_done, 1)
            pool.memset(keep[:, :].rearrange("h (t p) -> h t p", p=P)[:, :, 0:1], 0.0).then_inc(keep_done, 1)
            pool.wait_ge(abs_done, 1)
            pool.tensor_scalar(dt[:, :], dtx[:, :], 0.0, None, ALU.max).then_inc(relu_done, 1)
            pool.wait_ge(err_done, 1)
            pool.wait_ge(log_done, 1)
            pool.tensor_tensor(dt_log[:, :], dt_log[:, :], dt_err[:, :], ALU.subtract).then_inc(log1p_done, 1)
            pool.wait_ge(log1p_done, 1)
            pool.wait_ge(relu_done, 1)
            pool.tensor_tensor(dt[:, :], dt[:, :], dt_log[:, :], ALU.add).then_inc(dt_done, 1)
            pool.wait_ge(dt_done, 1)
            pool.wait_ge(a_done, 1)
            pool.tensor_scalar(la[:, :], dt[:, :], a_exp[:, 0:1], -1.0, ALU.mult, ALU.mult).then_inc(la_done, 1)


def row_of(eng, dram, n):
    size = 1
    for d in dram.shape[1:]:
        size *= d
    start = n * size if isinstance(n, int) else eng.snap(n * size)
    names = " ".join(f"d{k}" for k in range(len(dram.shape)))
    return dram.rearrange(f"{names} -> ({names})")[bass.ds(start, size)]


def columns_of(eng, n, size):
    return bass.ds(n * size if isinstance(n, int) else eng.snap(n * size), size)


def wait_all(eng, *waits):
    values = [v if isinstance(v, int) else eng.snap(v) for _, v in waits]
    for (sem, _), v in zip(waits, values):
        eng.wait_ge(sem, v)


def opening(i, r, upto):
    return isinstance(i, int) and i == 0 and r < upto


def each_unit(eng, body, units, steps, lead, tail):
    turns = units // steps
    for r in range(lead):
        body(0, r)
    with eng.Fori(0, turns - 1) as i:
        for r in range(lead, lead + steps):
            body(i, r)
    for r in range(lead, steps + tail):
        body(turns - 1, r)


def ssm_heads(nc, m):
    STEPS, UNITS, LEAD, TAIL = 2 * B, PAIRS * B, 6, 4
    LAST = UNITS // STEPS - 1
    with Scope(nc, "heads") as s:
        w_raw = s.sb("w_raw", [P, KD, 2, P])
        w_hi = s.sb("w_hi", [P, 2, KD, 2, P], F32R)
        w_lo = s.sb("w_lo", [P, 2, KD, 2, P], F32R)
        vec = s.sb("vec", [P, 2, 8])
        times = s.sb("times", [P, 2, 3, TILES, 2])
        decay = s.sb("decay", [P, 2, 2, TILES])
        ell_row = s.sb("ell_row", [P, 2, 2, SEQ])
        ell_exp = s.sb("ell_exp", [P, 4, SEQ - P])
        silu_gate = s.sb("silu_gate", [P, 8, SEQ])
        raw = s.sb("raw", [P, 2, TAPS - 1 + SEQ])
        x = s.sb("x", [P, 4, SEQ])
        x_dt = s.sb("x_dt", [P, 2, CH, P])
        x_end = s.sb("x_end", [P, 2, CH - 1, P])
        mix = s.sb("mix", [P, 4, 2, SEQ])
        state = s.sb("state", [P, 2, CH - 1, P])
        carried = s.sb("carried", [P, 4, SEQ - P])
        y = s.sb("y", [P, 4, SEQ])
        g = s.sb("g", [P, 2, SEQ])
        gate_ps = s.ps("gate_ps", [P, SEQ])
        x_ps = s.ps("x_ps", [P, SEQ])
        turn_ps = s.ps("turn_ps", [P, CH, P])
        state_ps = s.ps("state_ps", [P, CH, P])
        inner_ps = s.ps("inner_ps", [P, 2, SEQ])
        outer_ps = s.ps("outer_ps", [P, 2, SEQ])
        w_loaded, vec_loaded = s.sem("w_loaded"), s.sem("vec_loaded")
        w_hi_done, w_lo_done = s.sem("w_hi_done"), s.sem("w_lo_done")
        row_loaded = [s.sem(f"row_loaded{q}") for q in range(2)]
        ell_loaded = [s.sem(f"ell_loaded{q}") for q in range(4)]
        times_done, pad_done = s.sem("times_done"), s.sem("pad_done")
        gate_mm, x_mm, turn_mm, state_mm, y_mm = (s.sem("gate_mm"), s.sem("x_mm"), s.sem("turn_mm"),
                                                  s.sem("state_mm"), s.sem("y_mm"))
        gate_done, raw_done, conv_step, x_done = (s.sem("gate_done"), s.sem("raw_done"),
                                                  s.sem("conv_step"), s.sem("x_done"))
        ell_exp_done, diff_exp_done = s.sem("ell_exp_done"), s.sem("diff_exp_done")
        x_dt_done, x_end_done, diff_done = s.sem("x_dt_done"), s.sem("x_end_done"), s.sem("diff_done")
        mix_done, state_step, y_step = s.sem("mix_done"), s.sem("state_step"), s.sem("y_step")
        y_done, g_done = s.sem("y_done"), s.sem("g_done")
        g_stored = [s.sem(f"g_stored{q}") for q in range(2)]
        block = s.block()

        def missing(i, r):
            return opening(i, r, 0) or (isinstance(i, int) and i == LAST and r >= STEPS)

        def nth(i, r, ring=1):
            return i * (STEPS // ring) + r // ring + 1

        def pair_of(i, r):
            return i * 2 + r // B

        def ell_rows(sync, i, r):
            rows, b = row_of(sync, m.ell_dram, pair_of(i, r)), r % B
            return rows.rearrange("(o h t) -> o h t", o=1, h=2)[:, :, b * SEQ:(b + 1) * SEQ]

        @block.sync
        def _(sync):
            def load_weights(i, r):
                pair = pair_of(i, r)
                weights = row_of(sync, m.w_gate_x, pair)
                if not opening(i, r, 1):
                    sync.wait_ge(w_lo_done, pair)
                sync.dma_start(w_raw[:, :, :, :].rearrange("p k c n -> p (k c n)"),
                               weights.rearrange("(p n) -> p n", p=P)).then_inc(w_loaded, 16)

            def load_vectors(i, r):
                q, vectors = (r // B) % 2, row_of(sync, m.pair_vec, pair_of(i, r))
                if not opening(i, r, 2 * B):
                    sync.wait_ge(y_step, nth(i, r - B - 1) * 2)
                sync.dma_start(vec[:, q], vectors.rearrange("(p n) -> p n", p=P)).then_inc(
                    vec_loaded, 16)

            def load_row(i, r):
                if missing(i, r):
                    return
                rows = ell_rows(sync, i, r)
                if not opening(i, r, 2):
                    sync.wait_ge(diff_done, nth(i, r - 2))
                sync.dma_start(ell_row[:, r % 2], rows.broadcast_to([P, 2, SEQ])).then_inc(
                    row_loaded[r % 2], 16)

            def load_ell(i, r):
                if missing(i, r):
                    return
                rows = ell_rows(sync, i, r)
                if not opening(i, r, 4):
                    sync.wait_ge(y_step, nth(i, r - 4) * 2)
                for h in range(2):
                    sync.dma_start(ell_exp[h * HEAD_P:(h + 1) * HEAD_P, r % 4],
                                   rows[:, h, P:SEQ].broadcast_to([HEAD_P, SEQ - P])).then_inc(
                        ell_loaded[r % 4], 16)

            def body(i, r):
                load_ell(i, r)
                load_row(i, r + 2)
                if r % B == 1 and not missing(i, r + B - 1):
                    load_weights(i, r + B - 1)
                if r % B == 2 and not missing(i, r + B - 2):
                    load_vectors(i, r + B - 2)
                if not missing(i, r - 4):
                    q, b = r % 2, r % B
                    mixed = row_of(sync, m.mixed_dram, pair_of(i, r - 4)).rearrange("(p t) -> p t", p=P)
                    sync.wait_ge(g_done, nth(i, r - 4))
                    sync.dma_start(mixed[:, b * SEQ:(b + 1) * SEQ], g[:, q]).then_inc(g_stored[q], 16)

            load_weights(0, 0)
            load_vectors(0, 0)
            load_row(0, 0)
            load_row(0, 1)
            each_unit(sync, body, UNITS, STEPS, 4, TAIL)
            for q in range(2):
                sync.wait_ge(g_stored[q], 16 * UNITS // 2)

        @block.tensor
        def _(pe):
            def project(i, r, kind, out):
                q, b = (r // B) % 2, r % B
                if b == 0:
                    pe.wait_ge(w_lo_done, pair_of(i, r) + 1)
                return three_passes(pe, out, lambda k: [x[:, q, k, kind] for x in (w_hi, w_lo)],
                                    lambda k: [x[:, k, b * SEQ:(b + 1) * SEQ]
                                               for x in (m.xn_hi, m.xn_lo)], range(KD))

            def outputs(i, r):
                b, q = r % B, r % 2
                pe.wait_ge(mix_done, nth(i, r))
                pe.wait_ge(x_dt_done, nth(i, r))
                pe.wait_ge(state_step, nth(i, r) * 5)
                if not opening(i, r, 2):
                    pe.wait_ge(y_step, nth(i, r - 2) * 2)
                for c in range(CH):
                    for h in range(2):
                        pe.matmul(inner_ps[h * HEAD_P:(h + 1) * HEAD_P, q, c * P:(c + 1) * P],
                                  x_dt[:, q, c, h * HEAD_P:(h + 1) * HEAD_P],
                                  mix[:, r % 4, h, c * P:(c + 1) * P], start=True, stop=True)
                for c in range(1, CH):
                    end = pe.matmul(outer_ps[:, q, c * P:(c + 1) * P], state[:, q, c - 1],
                                    m.c_fm[:, (CH * b + c) * P:(CH * b + c + 1) * P],
                                    start=True, stop=True)
                end.then_inc(y_mm, 1)

            def body(i, r):
                if not missing(i, r):
                    if not opening(i, r, 1):
                        pe.wait_ge(gate_done, nth(i, r - 1))
                    project(i, r, 0, gate_ps[:, :]).then_inc(gate_mm, 1)
                    if not opening(i, r, 1):
                        pe.wait_ge(raw_done, nth(i, r - 1))
                    project(i, r, 1, x_ps[:, :]).then_inc(x_mm, 1)
                if not missing(i, r - 1):
                    pe.wait_ge(x_done, nth(i, r - 1))
                    if not opening(i, r, 2):
                        pe.wait_ge(x_end_done, nth(i, r - 2))
                    for c in range(CH):
                        end = pe.transpose(turn_ps[:, c], x[:, (r - 1) % 4, c * P:(c + 1) * P],
                                           m.ident[:, :])
                    end.then_inc(turn_mm, 1)
                if not missing(i, r - 2):
                    outputs(i, r - 2)
                if not missing(i, r - 1):
                    b, q = (r - 1) % B, (r - 1) % 2
                    pe.wait_ge(x_end_done, nth(i, r - 1))
                    if not opening(i, r, 2):
                        pe.wait_ge(state_step, nth(i, r - 2) * 5)
                    for c in range(CH - 1):
                        end = pe.matmul(state_ps[:, c], m.b_tm[:, CH * b + c], x_end[:, q, c],
                                        start=True, stop=True)
                    end.then_inc(state_mm, 1)

            each_unit(pe, body, UNITS, STEPS, LEAD, TAIL)

        @block.scalar
        def _(act):
            def round_weights(i, r):
                q = (r // B) % 2
                act.wait_ge(w_loaded, 16 * (pair_of(i, r) + 1))
                if not opening(i, r, 2 * B):
                    act.wait_ge(x_mm, nth(i, r - B - 1))
                act.activation(w_hi[:, q], w_raw[:, :, :, :], ACT.Copy).then_inc(w_hi_done, 1)

            def diff_exp(i, r):
                if missing(i, r):
                    return
                act.wait_ge(diff_done, nth(i, r))
                act.activation(mix[:, r % 4], mix[:, r % 4], ACT.Exp).then_inc(diff_exp_done, 1)

            def ell_exps(i, r):
                if missing(i, r):
                    return
                act.wait_ge(ell_loaded[r % 4], 32 * nth(i, r, 4))
                act.activation(ell_exp[:, r % 4], ell_exp[:, r % 4], ACT.Exp).then_inc(ell_exp_done, 1)

            def body(i, r):
                if not missing(i, r):
                    act.wait_ge(gate_mm, nth(i, r))
                    if not opening(i, r, 6):
                        act.wait_ge(g_done, nth(i, r - 6))
                    act.activation(silu_gate[:, r % 8], gate_ps[:, :], ACT.Silu).then_inc(gate_done, 1)
                    act.wait_ge(x_mm, nth(i, r))
                    if not opening(i, r, 2):
                        act.wait_ge(conv_step, nth(i, r - 2) * 4)
                    act.activation(raw[:, r % 2, TAPS - 1:], x_ps[:, :], ACT.Copy).then_inc(raw_done, 1)
                if r % 2 == 0:
                    diff_exp(i, r - 1)
                    diff_exp(i, r)
                    ell_exps(i, r - 1)
                    ell_exps(i, r)
                if not missing(i, r):
                    act.wait_ge(conv_step, nth(i, r) * 4)
                    act.activation(x[:, r % 4], x[:, r % 4], ACT.Silu).then_inc(x_done, 1)
                if r % B == 2 and not missing(i, r + B - 2):
                    round_weights(i, r + B - 2)

            round_weights(0, 0)
            act.wait_ge(pad_done, 1)
            each_unit(act, body, UNITS, STEPS, LEAD, TAIL)

        @block.vector
        def _(dve):
            def take_times(i, r):
                q, pair = (r // B) % 2, pair_of(i, r)
                dve.tensor_copy(times[:, q].rearrange("p a t h -> p (a t) h"),
                                m.times_tm[:, :, bass.ds(pair * 2, 2)]).then_inc(times_done, 1)
                dve.tensor_copy(decay[:, q], m.chunk_decay[:, bass.ds(pair * 2, 2), :]).then_inc(
                    times_done, 1)

            def outputs(i, r):
                if missing(i, r):
                    return
                q, pq = r % 2, (r // B) % 2
                dve.wait_ge(y_mm, nth(i, r))
                if not opening(i, r, 3):
                    dve.wait_ge(g_done, nth(i, r - 3))
                dve.scalar_tensor_tensor(out=y[:, r % 4], in0=x[:, r % 4], scalar=vec[:, pq, 5:6],
                                         in1=inner_ps[:, q], op0=ALU.mult, op1=ALU.add).then_inc(y_step, 1)
                dve.wait_ge(ell_exp_done, nth(i, r))
                dve.tensor_tensor(carried[:, r % 4], outer_ps[:, q, P:SEQ], ell_exp[:, r % 4],
                                  ALU.mult).then_inc(y_step, 1)

            def differences(i, r):
                if missing(i, r):
                    return
                b, q, pq = r % B, r % 2, (r // B) % 2
                if b == 0:
                    take_times(i, r)
                dve.wait_ge(row_loaded[q], 16 * nth(i, r, 2))
                dve.wait_ge(times_done, 2 * (pair_of(i, r) + 1))
                if not opening(i, r, 4):
                    dve.wait_ge(y_mm, nth(i, r - 4))
                for h in range(2):
                    for c in range(CH):
                        cols, t = slice(c * P, (c + 1) * P), CH * b + c
                        end = dve.tensor_scalar(mix[:, r % 4, h, cols], ell_row[:, q, h, cols],
                                                times[:, pq, 2, t, h:h + 1], 0.0,
                                                ALU.subtract, ALU.min)
                end.then_inc(diff_done, 1)

            def weigh(i, r):
                if missing(i, r):
                    return
                b, q, pq = r % B, r % 2, (r // B) % 2
                dve.wait_ge(turn_mm, nth(i, r))
                if not opening(i, r, 2):
                    dve.wait_ge(y_mm, nth(i, r - 2))
                for out, done, n, cs in ((x_end, x_end_done, 1, CH - 1), (x_dt, x_dt_done, 0, CH)):
                    dve.tensor_tensor(
                        out[:, q].rearrange("p c (h e) -> p c h e", h=2),
                        turn_ps[:, 0:cs].rearrange("p c (h e) -> p c h e", h=2),
                        times[:, pq, n, CH * b:CH * b + cs].rearrange(
                            "p c (h o) -> p c h o", o=1).broadcast_to([P, cs, 2, HEAD_P]),
                        ALU.mult).then_inc(done, 1)

            def convolve(i, r):
                if missing(i, r):
                    return
                q, pq = r % 2, (r // B) % 2
                if r % B == 0:
                    dve.wait_ge(vec_loaded, 16 * (pair_of(i, r) + 1))
                dve.wait_ge(raw_done, nth(i, r))
                if not opening(i, r, 4):
                    dve.wait_ge(turn_mm, nth(i, r - 4))
                dve.tensor_scalar(x[:, r % 4], raw[:, q, 0:SEQ], vec[:, pq, 0:1],
                                  vec[:, pq, TAPS:TAPS + 1], ALU.mult, ALU.add).then_inc(conv_step, 1)
                for j in range(1, TAPS):
                    dve.wait_ge(conv_step, nth(i, r) * 4 - 4 + j)
                    dve.scalar_tensor_tensor(out=x[:, r % 4], in0=raw[:, q, j:j + SEQ],
                                             scalar=vec[:, pq, j:j + 1], in1=x[:, r % 4],
                                             op0=ALU.mult, op1=ALU.add).then_inc(conv_step, 1)

            def states(i, r):
                if missing(i, r):
                    return
                b, q, pq = r % B, r % 2, (r // B) % 2
                dve.wait_ge(state_mm, nth(i, r))
                if not opening(i, r, 2):
                    dve.wait_ge(y_mm, nth(i, r - 2))
                dve.tensor_copy(state[:, q, 0], state_ps[:, 0]).then_inc(state_step, 1)
                for c in range(1, CH - 1):
                    dve.wait_ge(state_step, nth(i, r) * 5 - 6 + 2 * c)
                    for h in range(2):
                        cols = slice(h * HEAD_P, (h + 1) * HEAD_P)
                        dve.scalar_tensor_tensor(
                            out=state[:, q, c, cols], in0=state[:, q, c - 1, cols],
                            scalar=decay[:, pq, h, CH * b + c:CH * b + c + 1],
                            in1=state_ps[:, c, cols], op0=ALU.mult, op1=ALU.add).then_inc(state_step, 1)

            def body(i, r):
                outputs(i, r - 3)
                differences(i, r + 1)
                weigh(i, r - 1)
                convolve(i, r)
                states(i, r - 1)

            dve.memset(raw[:, :, 0:TAPS - 1], 0.0).then_inc(pad_done, 1)
            differences(0, 0)
            each_unit(dve, body, UNITS, STEPS, LEAD, TAIL)

        @block.gpsimd
        def _(pool):
            def keep_lo(i, r):
                q = (r // B) % 2
                pool.wait_ge(w_hi_done, pair_of(i, r) + 1)
                pool.tensor_tensor(w_lo[:, q], w_raw[:, :, :, :], w_hi[:, q].bitcast(F32),
                                   ALU.subtract).then_inc(w_lo_done, 1)

            def weigh(i, r):
                if missing(i, r):
                    return
                b = r % B
                pool.wait_ge(diff_exp_done, nth(i, r))
                cells = mix[:, r % 4].rearrange("p h (c t) -> p h c t", c=CH)
                pool.tensor_tensor(cells, cells, m.cb[:, CH * b:CH * (b + 1)].rearrange(
                    "p (o c) t -> p o c t", o=1).broadcast_to([P, 2, CH, P]), ALU.mult).then_inc(mix_done, 1)

            def body(i, r):
                if r % B == 3 and not missing(i, r + 1):
                    keep_lo(i, r + 1)
                if not missing(i, r - 4):
                    q, y_q = r % 2, r % 4
                    pool.wait_ge(y_step, nth(i, r - 4) * 2)
                    pool.tensor_tensor(y[:, y_q, P:SEQ], y[:, y_q, P:SEQ], carried[:, y_q],
                                       ALU.add).then_inc(y_done, 1)
                    pool.wait_ge(y_done, nth(i, r - 4))
                    if not opening(i, r, 6):
                        pool.wait_ge(g_stored[q], 16 * nth(i, r - 6, 2))
                    pool.tensor_tensor(g[:, q], y[:, y_q], silu_gate[:, (r - 4) % 8], ALU.mult).then_inc(g_done, 1)
                if r % 2 == 0:
                    weigh(i, r - 1)
                    weigh(i, r)

            keep_lo(0, 0)
            each_unit(pool, body, UNITS, STEPS, LEAD, TAIL)


def ssm_output(nc, m):
    STEPS, LEAD, TAIL = 4, 3, 1
    LAST = TILES // STEPS - 1
    with Scope(nc, "ssm_out") as s:
        w_out = [s.sb(f"w_{x}", [P, KI, D], F32R) for x in ("hi", "lo")]
        w = split_weights(s, "w", [(m.w_out[k], w_out[0][:, k], w_out[1][:, k], m.norm_w[:, k:k + 1])
                                   for k in range(KI)], D)
        ones = s.sb("ones", [P, 2])
        mean_sq, rms, inv_rms = (s.sb(n, [P, 2, 1]) for n in ("mean_sq", "rms", "inv_rms"))
        mixed = s.sb("mixed", [P, 2, KI, P])
        hi, lo = s.sb("mixed_hi", [P, 2, KI, P], F32R), s.sb("mixed_lo", [P, 2, KI, P], F32R)
        square, square_sum = s.sb("square", [P, KI, P]), s.sb("square_sum", [P, 2, P])
        x, gate = s.sb("x", [P, 4, D]), s.sb("gate", [P, 4, D])
        gated, x1 = s.sb("gated", [P, 2, D]), s.sb("x1", [P, 2, D])
        out_ps = s.ps("out_ps", [P, 2, D])
        sq_ps = s.ps("sq_ps", [P, 2, 512])
        ones_done, square_done, square_sum_done, sq_mm, mean_done, rms_done, inv_done = (
            s.sem(n) for n in ("ones_done", "square_done", "square_sum_done", "sq_mm", "mean_done",
                               "rms_done", "inv_done"))
        mixed_loaded = [s.sem(f"mixed_loaded{q}") for q in range(2)]
        rows_loaded = [s.sem(f"rows_loaded{q}") for q in range(2)]
        hi_done, lo_done, out_mm, gated_done, x1_done = (
            s.sem(n) for n in ("hi_done", "lo_done", "out_mm", "gated_done", "x1_done"))
        x1_stored = [s.sem(f"x1_stored{q}") for q in range(2)]
        block = s.block()
        x_t, gate_t, x1_t = (d.rearrange("(n p) d -> n p d", p=P) for d in (m.x, m.gate_dram, m.x1_dram))
        mixed_p = m.mixed_dram.rearrange("k p t -> p k t")

        def missing(i, r):
            return opening(i, r, 0) or (isinstance(i, int) and i == LAST and r >= STEPS)

        def nth(i, r, ring=1):
            return i * (STEPS // ring) + r // ring + 1

        @block.sync
        def _(sync):
            def load(i, r):
                q, t = r % 2, i * STEPS + r
                tokens = columns_of(sync, t, P)
                x_rows, gate_rows = (row_of(sync, d, t).rearrange("(p d) -> p d", p=P)
                                     for d in (x_t, gate_t))
                if not opening(i, r, 2):
                    sync.wait_ge(lo_done, nth(i, r - 2))
                    sync.wait_ge(square_done, nth(i, r - 2))
                sync.dma_start(mixed[:, q], mixed_p[:, :, tokens]).then_inc(mixed_loaded[q], 16)
                if not opening(i, r, 4):
                    sync.wait_ge(x1_done, nth(i, r - 4))
                sync.dma_start(x[:, r % 4], x_rows).then_inc(rows_loaded[q], 16)
                sync.dma_start(gate[:, r % 4], gate_rows).then_inc(rows_loaded[q], 16)

            def body(i, r):
                if not missing(i, r + 2):
                    load(i, r + 2)
                if not missing(i, r - 1):
                    rows = row_of(sync, x1_t, i * STEPS + r - 1).rearrange("(p d) -> p d", p=P)
                    sync.wait_ge(x1_done, nth(i, r - 1))
                    sync.dma_start(rows, x1[:, (r - 1) % 2]).then_inc(x1_stored[(r - 1) % 2], 16)

            load(0, 0)
            for n in range(w.ring):
                w.load(sync, n)
            load(0, 1)
            for n in range(w.ring, w.n):
                w.load(sync, n)
            each_unit(sync, body, TILES, STEPS, 2, TAIL)
            for q in range(2):
                sync.wait_ge(x1_stored[q], 16 * TILES // 2)

        @block.tensor
        def _(pe):
            def body(i, r):
                if missing(i, r):
                    return
                q = r % 2
                pe.wait_ge(lo_done, nth(i, r))
                if not opening(i, r, 2):
                    pe.wait_ge(gated_done, nth(i, r - 2))
                for k in range(KI):
                    if opening(i, r, 1):
                        pe.wait_ge(w.done, k + 1)
                    three_passes(pe, out_ps[:, q], lambda k: (hi[:, q, k], lo[:, q, k]),
                                 lambda k: [x[:, k] for x in w_out], [k],
                                 first=k == 0, last=k == KI - 1)
                pe.wait_ge(square_sum_done, nth(i, r))
                pe.matmul(sq_ps[:, q, 0:2], square_sum[:, q], ones[:, :], start=True,
                          stop=True).then_inc(out_mm, 1)

            pe.wait_ge(ones_done, 1)
            each_unit(pe, body, TILES, STEPS, LEAD, TAIL)

        @block.scalar
        def _(act):
            def split(i, r):
                q = r % 2
                act.wait_ge(mixed_loaded[q], 16 * nth(i, r, 2))
                if not opening(i, r, 2):
                    act.wait_ge(out_mm, nth(i, r - 2))
                act.activation(hi[:, q], mixed[:, q], ACT.Copy).then_inc(hi_done, 1)

            def squares(i, r):
                if not opening(i, r, 1):
                    act.wait_ge(square_sum_done, nth(i, r - 1))
                act.activation(square[:, :, :], mixed[:, r % 2], ACT.Square).then_inc(square_done, 1)

            def body(i, r):
                if not missing(i, r):
                    if not opening(i, r, 1):
                        split(i, r)
                    squares(i, r)
                if not missing(i, r - 1):
                    q = (r - 1) % 2
                    act.wait_ge(mean_done, nth(i, r - 1))
                    act.activation(rms[:, q], mean_sq[:, q], ACT.Sqrt).then_inc(rms_done, 1)

            split(0, 0)
            for n in range(w.n):
                w.round_hi(act, n)
            each_unit(act, body, TILES, STEPS, LEAD, TAIL)

        @block.vector
        def _(dve):
            def split(i, r):
                q = r % 2
                dve.wait_ge(hi_done, nth(i, r))
                dve.tensor_tensor(lo[:, q], mixed[:, q], hi[:, q].bitcast(F32),
                                  ALU.subtract).then_inc(lo_done, 1)

            def sum_squares(i, r):
                dve.wait_ge(square_done, nth(i, r))
                dve.tensor_reduce(square_sum[:, r % 2], square[:, :, :].rearrange("p k t -> p t k"),
                                  AX.X, ALU.add).then_inc(square_sum_done, 1)

            def mean(i, r):
                q = r % 2
                dve.wait_ge(out_mm, nth(i, r))
                dve.tensor_scalar(mean_sq[:, q], sq_ps[:, q, 0:1], 1.0 / INTER, LN_EPS, ALU.mult,
                                  ALU.add).then_inc(mean_done, 1)

            def finish(i, r):
                q = r % 2
                dve.wait_ge(rms_done, nth(i, r))
                dve.reciprocal(inv_rms[:, q], rms[:, q]).then_inc(inv_done, 1)
                wait_all(dve, (inv_done, nth(i, r)), (rows_loaded[q], 32 * nth(i, r, 2)),
                         *[(x1_stored[q], 16 * nth(i, r - 2, 2))][:not opening(i, r, 2)])
                dve.scalar_tensor_tensor(out=gated[:, q], in0=out_ps[:, q],
                                         scalar=inv_rms[:, q], in1=gate[:, r % 4],
                                         op0=ALU.mult, op1=ALU.mult).then_inc(gated_done, 1)
                dve.wait_ge(gated_done, nth(i, r))
                dve.tensor_tensor(x1[:, q], gated[:, q], x[:, r % 4], ALU.add).then_inc(x1_done, 1)

            def body(i, r):
                if not missing(i, r):
                    if not opening(i, r, 1):
                        split(i, r)
                    sum_squares(i, r)
                if not missing(i, r - 1):
                    mean(i, r - 1)
                    finish(i, r - 1)

            dve.memset(ones[:, :], 1.0).then_inc(ones_done, 1)
            split(0, 0)
            for n in range(w.n):
                w.keep_lo(dve, n)
            each_unit(dve, body, TILES, STEPS, LEAD, TAIL)


def values_and_decays(nc, m):
    V0 = KV_HEADS
    COLS = KV_HEADS + KV_DIM + EXPERTS
    PARTS = 4
    W = (KV_DIM + EXPERTS) // PARTS
    GATE_OFFSET = 6.906768
    with Scope(nc, "values") as s:
        w_all = [s.sb(f"w_{x}", [P, KD, COLS], F32R) for x in ("hi", "lo")]
        w = split_weights(s, "w", [(m.w_gvr[k], w_all[0][:, k], w_all[1][:, k], None)
                                   for k in range(KD)], COLS)
        v = s.sb("v", [P, 2, PARTS, W])
        z, z_abs, z_exp, z_one, z_err, log_g, keep, total = (
            s.sb(n, [KV_HEADS, TOK]) for n in ("z", "z_abs", "z_exp", "z_one", "z_err", "log_g",
                                               "keep", "total"))
        top8 = s.sb("top8", [P, TILES, 8])
        below, e2, rw = (s.sb(n, [P, TILES, 2]) for n in ("below", "e2", "rw"))
        esum, einv = s.sb("esum", [P, TILES, 1]), s.sb("einv", [P, TILES, 1])
        g_ps = s.ps("g_ps", [P, SEQ])
        v_ps = s.ps("v_ps", [P, 6, 512])
        turn_ps = s.ps("turn_ps", [P, TILES, KV_HEADS])
        g_mm, z_done, abs_done, exp_done, one_done, log_done, err_done, log1p_done = (
            s.sem(n) for n in ("g_mm", "z_done", "abs_done", "exp_done", "one_done", "log_done",
                               "err_done", "log1p_done"))
        log_g_done, keep_done, total_done, turned, turned_read, total_stored = (
            s.sem(n) for n in ("log_g_done", "keep_done", "total_done", "turned", "turned_read",
                               "total_stored"))
        v_mm, v_read, top_done, below_done, e2_done, rw_step = (
            s.sem(n) for n in ("v_mm", "v_read", "top_done", "below_done", "e2_done", "rw_step"))
        v_stored = [s.sem(f"v_stored{q}") for q in range(2)]
        block = s.block()
        values_t = m.values_dram.rearrange("(n p) d -> n p d", p=P)

        @block.sync
        def _(sync):
            for n in range(w.n):
                w.load(sync, n)
            for t in range(TILES):
                sync.wait_ge(v_read, PARTS * (t + 1))
                sync.dma_start(values_t[t], v[:, t % 2].rearrange("p a w -> p (a w)")[:, 0:KV_DIM]
                               ).then_inc(v_stored[t % 2], 16)
                if t == 1:
                    sync.wait_ge(total_done, 1)
                    sync.dma_start(m.log_gate_dram, total[:, :]).then_inc(total_stored, 16)
            sync.wait_ge(total_stored, 16)
            for q in range(2):
                sync.wait_ge(v_stored[q], 16 * TILES // 2)

        @block.tensor
        def _(pe):
            for b in range(B):
                if b >= 1:
                    pe.wait_ge(z_done, b)
                for k in range(KD):
                    if b == 0:
                        pe.wait_ge(w.done, k + 1)
                    end = three_passes(pe, g_ps[:, :], lambda k: [x[:, k, 0:P] for x in w_all],
                                       lambda k: [x[:, k, b * SEQ:(b + 1) * SEQ]
                                                  for x in (m.xn_hi, m.xn_lo)],
                                       [k], first=k == 0, last=k == KD - 1)
                end.then_inc(g_mm, 1)
            for t in range(TILES):
                if t == TILES // 2:
                    pe.wait_ge(total_done, 1)
                    for n in range(TILES):
                        end = pe.transpose(turn_ps[:, n], total[:, n * P:(n + 1) * P],
                                           m.ident[0:KV_HEADS, 0:KV_HEADS])
                    end.then_inc(turned, 1)
                for a in range(PARTS):
                    n = PARTS * t + a
                    if n >= 6:
                        pe.wait_ge(v_read, n - 5)
                    three_passes(pe, v_ps[:, n % 6, 0:W],
                                 lambda k: [x[:, k, t * P:(t + 1) * P] for x in (m.xn_hi, m.xn_lo)],
                                 lambda k: [x[:, k, V0 + a * W:V0 + (a + 1) * W] for x in w_all],
                                 range(KD)).then_inc(v_mm, 1)

        @block.scalar
        def _(act):
            for n in range(w.n):
                w.round_hi(act, n)
            act.wait_ge(z_done, B)
            act.activation(z_abs[:, :], z[:, :], ACT.Abs).then_inc(abs_done, 1)
            act.wait_ge(abs_done, 1)
            act.activation(z_exp[:, :], z_abs[:, :], ACT.Exp, scale=-1.0).then_inc(exp_done, 1)
            act.wait_ge(one_done, 1)
            act.activation(log_g[:, :], z_one[:, :], ACT.Ln).then_inc(log_done, 1)
            for t in range(TILES):
                if t >= 2:
                    act.wait_ge(v_stored[t % 2], 16 * (t // 2))
                    act.wait_ge(top_done, t - 1)
                for a in range(PARTS):
                    n = PARTS * t + a
                    act.wait_ge(v_mm, n + 1)
                    act.activation(v[:, t % 2, a], v_ps[:, n % 6, 0:W], ACT.Copy).then_inc(v_read, 1)
            act.wait_ge(turned, 1)
            act.activation(m.log_gate_tm[:, :, :].rearrange("p h t -> p t h"), turn_ps[:, :, :],
                           ACT.Copy).then_inc(turned_read, 1)
            act.wait_ge(below_done, 1)
            act.activation(e2[:, :, :], below[:, :, :], ACT.Exp).then_inc(e2_done, 1)
            act.wait_ge(turned_read, 1)

        @block.vector
        def _(dve):
            for n in range(w.n):
                w.keep_lo(dve, n)
            dve.memset(keep[:, :], 1.0).then_inc(keep_done, 1)
            dve.wait_ge(keep_done, 1)
            dve.memset(keep[:, :].rearrange("h (b t) -> h b t", b=B)[:, :, 0:1], 0.0).then_inc(keep_done, 1)
            for b in range(B):
                dve.wait_ge(g_mm, b + 1)
                dve.tensor_scalar(z[:, b * SEQ:(b + 1) * SEQ], g_ps[0:KV_HEADS], GATE_OFFSET, None,
                                  ALU.add).then_inc(z_done, 1)
            dve.wait_ge(exp_done, 1)
            dve.tensor_scalar(z_one[:, :], z_exp[:, :], 1.0, None, ALU.add).then_inc(one_done, 1)
            dve.wait_ge(one_done, 1)
            dve.scalar_tensor_tensor(out=z_err[:, :], in0=z_one[:, :], scalar=1.0, in1=z_exp[:, :],
                                     op0=ALU.subtract, op1=ALU.subtract).then_inc(err_done, 1)
            wait_all(dve, (err_done, 1), (log_done, 1))
            dve.tensor_tensor(log_g[:, :], log_g[:, :], z_err[:, :], ALU.subtract).then_inc(log1p_done, 1)
            dve.wait_ge(log1p_done, 1)
            dve.scalar_tensor_tensor(out=log_g[:, :], in0=z[:, :], scalar=0.0, in1=log_g[:, :],
                                     op0=ALU.min, op1=ALU.subtract).then_inc(log_g_done, 1)
            wait_all(dve, (log_g_done, 1), (keep_done, 2))
            dve.tensor_tensor_scan(total[:, :], keep[:, :], log_g[:, :], 0.0, ALU.mult,
                                   ALU.add).then_inc(total_done, 1)
            for t in range(TILES):
                dve.wait_ge(v_read, PARTS * (t + 1))
                dve.max(top8[:, t], v[:, t % 2, PARTS - 1, W - EXPERTS:W]).then_inc(top_done, 1)
            dve.wait_ge(top_done, TILES)
            dve.tensor_tensor(below[:, :, :], top8[:, :, 0:2],
                              top8[:, :, 0:1].broadcast_to([P, TILES, 2]), ALU.subtract).then_inc(below_done, 1)
            dve.wait_ge(e2_done, 1)
            dve.tensor_tensor(esum[:, :, :], e2[:, :, 0:1], e2[:, :, 1:2], ALU.add).then_inc(rw_step, 1)
            dve.wait_ge(rw_step, 1)
            dve.reciprocal(einv[:, :, :], esum[:, :, :]).then_inc(rw_step, 1)
            dve.wait_ge(rw_step, 2)
            dve.tensor_tensor(rw[:, :, :], e2[:, :, :], einv[:, :, :].broadcast_to([P, TILES, 2]),
                              ALU.mult).then_inc(rw_step, 1)
            dve.wait_ge(rw_step, 3)
            dve.tensor_tensor(m.comb_w[:, :].rearrange("p (t o) -> p t o", o=1), rw[:, :, 0:1],
                              rw[:, :, 1:2], ALU.add).then_inc(rw_step, 1)
            dve.wait_ge(rw_step, 4)


def power_attention(nc, m):
    STEPS, UNITS, LEAD, TAIL = 2 * B, KV_HEADS * B, 6, 2
    LAST = UNITS // STEPS - 1
    WIDTH = [SEQ - j * P for j in range(CH)]
    AT = [0, 512, 1024, 896]
    COLS = sum(WIDTH)
    VC = HEAD_D + 2
    SCALE = HEAD_D ** -0.5
    with Scope(nc, "attn") as s:
        w_raw = s.sb("w_raw", [P, KD, 3, P])
        w_hi = s.sb("w_hi", [P, 2, KD, 3, P], F32R)
        w_lo = s.sb("w_lo", [P, 2, KD, 3, P], F32R)
        gate_row = s.sb("gate_row", [P, 2, SEQ])
        gate_cols = s.sb("gate_cols", [P, 2, TILES])
        v = s.sb("v", [P, 2, CH, VC])
        qk = s.sb("qk", [P, 2, 3, SEQ])
        decay = s.sb("decay", [P, 2, COLS])
        a = s.sb("a", [P, 2, COLS])
        norm, inv = s.sb("norm", [P, 2, CH]), s.sb("inv", [P, 2, CH])
        y = s.sb("y", [P, 2, CH, REP, HEAD_D])
        proj_ps = s.ps("proj_ps", [P, 3, SEQ])
        score_ps = s.ps("score_ps", [P, 3 * 512])
        out_ps = s.ps("out_ps", [P, 2, 512])
        w_loaded, w_hi_done, w_lo_done = s.sem("w_loaded"), s.sem("w_hi_done"), s.sem("w_lo_done")
        rows_loaded = [s.sem(f"rows_loaded{q}") for q in range(2)]
        v_loaded = [s.sem(f"v_loaded{q}") for q in range(2)]
        ones_done, cols_done, proj_mm, qk_done = (
            s.sem(n) for n in ("ones_done", "cols_done", "proj_mm", "qk_done"))
        score_mm, square_done, diff_done, decay_done, a_done = (
            s.sem(n) for n in ("score_mm", "square_done", "diff_done", "decay_done", "a_done"))
        out_mm, norm_done, inv_done, y_done = (
            s.sem(n) for n in ("out_mm", "norm_done", "inv_done", "y_done"))
        y_stored = [s.sem(f"y_stored{q}") for q in range(2)]
        block = s.block()

        def missing(i, r):
            return opening(i, r, 0) or (isinstance(i, int) and i == LAST and r >= STEPS)

        def nth(i, r, ring=1):
            return i * (STEPS // ring) + r // ring + 1

        def head_of(i, r):
            return i * 2 + r // B

        @block.sync
        def _(sync):
            def load_weights(i, r):
                weights = row_of(sync, m.w_qqk, head_of(i, r)).rearrange("(p n) -> p n", p=P)
                wait_all(sync, *[(w_lo_done, head_of(i, r))][:not opening(i, r, 1)])
                sync.dma_start(w_raw[:, :, :, :].rearrange("p k c n -> p (k c n)"),
                               weights).then_inc(w_loaded, 16)

            def body(i, r):
                b, q = r % B, r % 2
                if not missing(i, r):
                    row = row_of(sync, m.log_gate_dram, head_of(i, r))
                    values = m.values_dram.rearrange("(b c p) e -> b p c e", b=B, p=P)[
                        b][:, :, columns_of(sync, head_of(i, r), HEAD_D)]
                    if not opening(i, r, 2):
                        sync.wait_ge(diff_done, nth(i, r - 2))
                    sync.dma_start(gate_row[:, q], row.rearrange("(o t) -> o t", o=1)[
                        :, b * SEQ:(b + 1) * SEQ].broadcast_to([P, SEQ])).then_inc(rows_loaded[q], 16)
                    if not opening(i, r, 2):
                        sync.wait_ge(out_mm, 2 * nth(i, r - 2))
                    sync.dma_start(v[:, q, :, 0:HEAD_D], values).then_inc(v_loaded[q], 16)
                if r % B == 1 and not missing(i, r + B - 1):
                    load_weights(i, r + B - 1)
                if not missing(i, r - 2):
                    out = m.attended_dram.rearrange("(b c p) e -> b p c e", b=B, p=P)[
                        (r - 2) % B][:, :, columns_of(sync, head_of(i, r - 2), REP * HEAD_D)]
                    wait_all(sync, (y_done, 2 * nth(i, r - 2)))
                    sync.dma_start(out, y[:, q].rearrange("p c r e -> p c (r e)")).then_inc(
                        y_stored[q], 16)

            load_weights(0, 0)
            each_unit(sync, body, UNITS, STEPS, 4, TAIL)
            for q in range(2):
                sync.wait_ge(y_stored[q], 16 * UNITS // 2)

        @block.tensor
        def _(pe):
            def project(i, r, kind):
                if missing(i, r):
                    return
                q, b = (r // B) % 2, r % B
                if b == 0 and kind == 0:
                    wait_all(pe, (w_lo_done, head_of(i, r) + 1))
                if not opening(i, r, 1):
                    wait_all(pe, (qk_done, 3 * nth(i, r) - 5 + kind))
                three_passes(pe, proj_ps[:, kind], lambda k: [x[:, q, k, kind] for x in (w_hi, w_lo)],
                             lambda k: [x[:, k, b * SEQ:(b + 1) * SEQ] for x in (m.xn_hi, m.xn_lo)],
                             range(KD)).then_inc(proj_mm, 1)

            def scores(i, r, h):
                if missing(i, r):
                    return
                q = r % 2
                wait_all(pe, (qk_done, 3 * nth(i, r)),
                         *[(square_done, 2 * nth(i, r) - 2 + h)][:h or not opening(i, r, 1)])
                for j in range(CH):
                    end = pe.matmul(score_ps[:, AT[j]:AT[j] + WIDTH[j]], qk[:, q, 2, j * P:(j + 1) * P],
                                    qk[:, q, h, j * P:SEQ], start=True, stop=True)
                end.then_inc(score_mm, 1)

            def outputs(i, r, h):
                if missing(i, r):
                    return
                q = r % 2
                wait_all(pe, (a_done, 2 * nth(i, r) - 1 + h), (v_loaded[q], 16 * nth(i, r, 2)),
                         *[(y_done, 2 * nth(i, r) - 2 + h)][:h or not opening(i, r, 1)])
                for c in range(CH):
                    for j in range(c + 1):
                        at = AT[j] + (c - j) * P
                        end = pe.matmul(out_ps[:, c // 2, (c % 2) * VC:(c % 2 + 1) * VC],
                                        a[:, h, at:at + P], v[:, q, j], start=j == 0, stop=j == c)
                end.then_inc(out_mm, 1)

            def body(i, r):
                project(i, r, 0)
                scores(i, r - 1, 0)
                project(i, r, 1)
                outputs(i, r - 2, 1)
                scores(i, r - 1, 1)
                project(i, r, 2)
                outputs(i, r - 1, 0)

            pe.wait_ge(ones_done, 1)
            each_unit(pe, body, UNITS, STEPS, LEAD, TAIL)

        @block.scalar
        def _(act):
            def round_weights(i, r):
                q = (r // B) % 2
                wait_all(act, (w_loaded, 16 * (head_of(i, r) + 1)),
                         *[(proj_mm, 3 * nth(i, r - B - 1))][:not opening(i, r, 2 * B)])
                act.activation(w_hi[:, q], w_raw[:, :, :, :], ACT.Copy).then_inc(w_hi_done, 1)

            def take(i, r, kind):
                if missing(i, r):
                    return
                wait_all(act, (proj_mm, 3 * nth(i, r) - 2 + kind),
                         *[(score_mm, 2 * nth(i, r - 2))][:not opening(i, r, 2)])
                act.activation(qk[:, r % 2, kind], proj_ps[:, kind], ACT.Copy).then_inc(qk_done, 1)

            def square(i, r, h):
                if missing(i, r):
                    return
                wait_all(act, (score_mm, 2 * nth(i, r) - 1 + h),
                         *[(out_mm, 2 * nth(i, r - 1) - 1 + h)][:not opening(i, r, 1)])
                act.activation(a[:, h], score_ps[:, 0:COLS], ACT.Square,
                               scale=SCALE).then_inc(square_done, 1)

            def body(i, r):
                take(i, r, 0)
                square(i, r - 1, 0)
                take(i, r, 1)
                square(i, r - 1, 1)
                take(i, r, 2)
                if not missing(i, r):
                    wait_all(act, (diff_done, nth(i, r)))
                    act.activation(decay[:, r % 2], decay[:, r % 2], ACT.Exp).then_inc(decay_done, 1)
                if r % B == 2 and not missing(i, r + B - 2):
                    round_weights(i, r + B - 2)

            round_weights(0, 0)
            each_unit(act, body, UNITS, STEPS, LEAD, TAIL)

        @block.vector
        def _(dve):
            def keep_lo(i, r):
                q = (r // B) % 2
                wait_all(dve, (w_hi_done, head_of(i, r) + 1))
                dve.tensor_tensor(w_lo[:, q], w_raw[:, :, :, :], w_hi[:, q].bitcast(F32),
                                  ALU.subtract).then_inc(w_lo_done, 1)

            def take_columns(i, r):
                dve.tensor_copy(gate_cols[:, (r // B) % 2].rearrange("p (o t) -> p o t", o=1),
                                m.log_gate_tm[:, bass.ds(head_of(i, r), 1), :]).then_inc(cols_done, 1)

            def weigh(i, r, h):
                if missing(i, r):
                    return
                wait_all(dve, (square_done, 2 * nth(i, r) - 1 + h), (decay_done, nth(i, r)))
                dve.tensor_tensor(a[:, h], a[:, h], decay[:, r % 2], ALU.mult).then_inc(a_done, 1)

            def divide(i, r, h):
                if missing(i, r):
                    return
                q = r % 2
                n = 2 * nth(i, r) - 1 + h
                wait_all(dve, (out_mm, n), *[(y_stored[q], 16 * nth(i, r - 2, 2))][:not opening(i, r, 2)])
                heads = out_ps[:, :, 0:2 * VC].rearrange("p a (c e) -> p a c e", c=2)
                dve.tensor_scalar(norm[:, h].rearrange("p (a c) -> p a c", a=2), heads[:, :, :, HEAD_D],
                                  1e-6, None, ALU.add).then_inc(norm_done, 1)
                wait_all(dve, (norm_done, n))
                dve.reciprocal(inv[:, h], norm[:, h]).then_inc(inv_done, 1)
                wait_all(dve, (inv_done, n))
                dve.tensor_tensor(
                    y[:, q, :, h].rearrange("p (a c) e -> p a c e", a=2), heads[:, :, :, 0:HEAD_D],
                    inv[:, h].rearrange("p (a c o) -> p a c o", a=2, o=1).broadcast_to(
                        [P, 2, 2, HEAD_D]), ALU.mult).then_inc(y_done, 1)

            def body(i, r):
                if not missing(i, r):
                    b, q = r % B, r % 2
                    if b == 0:
                        take_columns(i, r)
                    wait_all(dve, (rows_loaded[q], 16 * nth(i, r, 2)), (cols_done, head_of(i, r) + 1))
                    for j in range(CH):
                        col = gate_cols[:, (r // B) % 2, CH * b + j:CH * b + j + 1]
                        end = dve.scalar_tensor_tensor(
                            out=decay[:, q, AT[j]:AT[j] + P], in0=gate_row[:, q, j * P:(j + 1) * P],
                            scalar=col, in1=m.never[:, :], op0=ALU.subtract, op1=ALU.min)
                        if j < CH - 1:
                            end = dve.tensor_scalar(
                                decay[:, q, AT[j] + P:AT[j] + WIDTH[j]], gate_row[:, q, (j + 1) * P:SEQ],
                                col, 0.0, ALU.subtract, ALU.min)
                    end.then_inc(diff_done, 1)
                weigh(i, r - 1, 0)
                divide(i, r - 2, 1)
                weigh(i, r - 1, 1)
                divide(i, r - 1, 0)
                if r % B == 2 and not missing(i, r + B - 2):
                    keep_lo(i, r + B - 2)

            dve.memset(v[:, :, :, HEAD_D:VC], 1.0).then_inc(ones_done, 1)
            keep_lo(0, 0)
            each_unit(dve, body, UNITS, STEPS, LEAD, TAIL)


def mlp_up(nc, m):
    STEPS, UNITS, LEAD, TAIL = 2 * B, BLOCKS * B, 6, 2
    LAST = UNITS // STEPS - 1
    with Scope(nc, "mlp_up") as s:
        w_raw = s.sb("w_raw", [P, KD, 2, P])
        w_hi = s.sb("w_hi", [P, 2, KD, 2, P], F32R)
        w_lo = s.sb("w_lo", [P, 2, KD, 2, P], F32R)
        silu_gate, hidden = s.sb("silu_gate", [P, 2, SEQ]), s.sb("hidden", [P, 2, SEQ])
        gate_ps, up_ps = s.ps("gate_ps", [P, 2, SEQ]), s.ps("up_ps", [P, 2, SEQ])
        w_loaded, w_hi_done, w_lo_done, gate_mm, up_mm, gate_done, hidden_done = (
            s.sem(n) for n in ("w_loaded", "w_hi_done", "w_lo_done", "gate_mm", "up_mm", "gate_done",
                               "hidden_done"))
        stored = [s.sem(f"stored{q}") for q in range(2)]
        block = s.block()

        def missing(i, r):
            return opening(i, r, 0) or (isinstance(i, int) and i == LAST and r >= STEPS)

        def nth(i, r, ring=1):
            return i * (STEPS // ring) + r // ring + 1

        def block_of(i, r):
            return i * 2 + r // B

        @block.sync
        def _(sync):
            def load_weights(i, r):
                weights = row_of(sync, m.w_gate_up, block_of(i, r)).rearrange("(p n) -> p n", p=P)
                wait_all(sync, *[(w_lo_done, block_of(i, r))][:not opening(i, r, 1)])
                sync.dma_start(w_raw[:, :, :, :].rearrange("p k c n -> p (k c n)"),
                               weights).then_inc(w_loaded, 16)

            def body(i, r):
                if r % B == 1 and not missing(i, r + B - 1):
                    load_weights(i, r + B - 1)
                if not missing(i, r - 1):
                    q, b = (r - 1) % 2, (r - 1) % B
                    out = row_of(sync, m.hidden_dram, block_of(i, r - 1)).rearrange("(p t) -> p t", p=P)
                    wait_all(sync, (hidden_done, nth(i, r - 1)))
                    sync.dma_start(out[:, b * SEQ:(b + 1) * SEQ], hidden[:, q]).then_inc(stored[q], 16)

            load_weights(0, 0)
            each_unit(sync, body, UNITS, STEPS, 4, TAIL)
            for q in range(2):
                sync.wait_ge(stored[q], 16 * UNITS // 2)

        @block.tensor
        def _(pe):
            def body(i, r):
                if missing(i, r):
                    return
                q, w_q, b = r % 2, (r // B) % 2, r % B
                if b == 0:
                    wait_all(pe, (w_lo_done, block_of(i, r) + 1))
                for kind, (ps, mm) in enumerate(((gate_ps, gate_mm), (up_ps, up_mm))):
                    if kind == 0 and not opening(i, r, 2):
                        wait_all(pe, (hidden_done, nth(i, r - 2)))
                    three_passes(pe, ps[:, q], lambda k: [x[:, w_q, k, kind] for x in (w_hi, w_lo)],
                                 lambda k: [x[:, k, b * SEQ:(b + 1) * SEQ] for x in (m.xn_hi, m.xn_lo)],
                                 range(KD)).then_inc(mm, 1)

            each_unit(pe, body, UNITS, STEPS, LEAD, TAIL)

        @block.scalar
        def _(act):
            def round_weights(i, r):
                q = (r // B) % 2
                wait_all(act, (w_loaded, 16 * (block_of(i, r) + 1)),
                         *[(up_mm, nth(i, r - B - 1))][:not opening(i, r, 2 * B)])
                act.activation(w_hi[:, q], w_raw[:, :, :, :], ACT.Copy).then_inc(w_hi_done, 1)

            def body(i, r):
                if not missing(i, r):
                    wait_all(act, (gate_mm, nth(i, r)),
                             *[(hidden_done, nth(i, r - 2))][:not opening(i, r, 2)])
                    act.activation(silu_gate[:, r % 2], gate_ps[:, r % 2], ACT.Silu).then_inc(gate_done, 1)
                if r % B == 2 and not missing(i, r + B - 2):
                    round_weights(i, r + B - 2)

            round_weights(0, 0)
            each_unit(act, body, UNITS, STEPS, LEAD, TAIL)

        @block.vector
        def _(dve):
            def keep_lo(i, r):
                q = (r // B) % 2
                wait_all(dve, (w_hi_done, block_of(i, r) + 1))
                dve.tensor_tensor(w_lo[:, q], w_raw[:, :, :, :], w_hi[:, q].bitcast(F32),
                                  ALU.subtract).then_inc(w_lo_done, 1)

            def body(i, r):
                q = r % 2
                if not missing(i, r):
                    wait_all(dve, (gate_done, nth(i, r)), (up_mm, nth(i, r)),
                             *[(stored[q], 16 * nth(i, r - 2, 2))][:not opening(i, r, 2)])
                    dve.tensor_tensor(hidden[:, q], silu_gate[:, q], up_ps[:, q],
                                      ALU.mult).then_inc(hidden_done, 1)
                if r % B == 2 and not missing(i, r + B - 2):
                    keep_lo(i, r + B - 2)

            keep_lo(0, 0)
            each_unit(dve, body, UNITS, STEPS, LEAD, TAIL)


def attention_output(nc, m):
    STEPS, LEAD, TAIL = 4, 3, 1
    LAST = TILES // STEPS - 1
    QUARTER = KI // 4
    with Scope(nc, "attn_out") as s:
        w_c = [s.sb(f"w_{x}", [P, KI, D], F32R) for x in ("hi", "lo")]
        w = split_weights(s, "w", [(m.w_c[k], w_c[0][:, k], w_c[1][:, k], None) for k in range(KI)], D)
        bias = s.sb("bias", [P, D])
        y = s.sb("y", [P, 2, KI, P])
        hi, lo = s.sb("y_hi", [P, 2, KI, P], F32R), s.sb("y_lo", [P, 2, KI, P], F32R)
        out = s.sb("out", [P, 2, D])
        turn_ps = s.ps("turn_ps", [P, 4, QUARTER, P])
        out_ps = s.ps("out_ps", [P, 2, D])
        bias_loaded = s.sem("bias_loaded")
        y_loaded = [s.sem(f"y_loaded{q}") for q in range(2)]
        turned, hi_done, lo_done, out_mm, out_done = (
            s.sem(n) for n in ("turned", "hi_done", "lo_done", "out_mm", "out_done"))
        stored = [s.sem(f"stored{q}") for q in range(2)]
        block = s.block()
        y_t = m.attended_dram.rearrange("(n p) d -> n p d", p=P)
        s_t = m.s_dram.rearrange("(n p) d -> n p d", p=P)

        def missing(i, r):
            return opening(i, r, 0) or (isinstance(i, int) and i == LAST and r >= STEPS)

        def nth(i, r, ring=1):
            return i * (STEPS // ring) + r // ring + 1

        @block.sync
        def _(sync):
            def load(i, r):
                q = r % 2
                rows = row_of(sync, y_t, i * STEPS + r).rearrange("(p d) -> p d", p=P)
                if not opening(i, r, 2):
                    sync.wait_ge(turned, 4 * nth(i, r - 2))
                sync.dma_start(y[:, q].rearrange("p k e -> p (k e)"), rows).then_inc(y_loaded[q], 16)

            def body(i, r):
                if not missing(i, r + 2):
                    load(i, r + 2)
                if not missing(i, r - 1):
                    q = (r - 1) % 2
                    rows = row_of(sync, s_t, i * STEPS + r - 1).rearrange("(p d) -> p d", p=P)
                    wait_all(sync, (out_done, nth(i, r - 1)))
                    sync.dma_start(rows, out[:, q]).then_inc(stored[q], 16)

            load(0, 0)
            for n in range(w.ring):
                w.load(sync, n)
            load(0, 1)
            sync.dma_start(bias[:, :], m.b_c.broadcast_to([P, D])).then_inc(bias_loaded, 16)
            for n in range(w.ring, w.n):
                w.load(sync, n)
            each_unit(sync, body, TILES, STEPS, 2, TAIL)
            for q in range(2):
                sync.wait_ge(stored[q], 16 * TILES // 2)

        @block.tensor
        def _(pe):
            def turn(i, r):
                if missing(i, r):
                    return
                q = r % 2
                for a in range(4):
                    wait_all(pe, *[(y_loaded[q], 16 * nth(i, r, 2))][:a == 0],
                             *[(lo_done, 4 * nth(i, r) - 7 + a)][:not opening(i, r, 1)])
                    for k in range(QUARTER):
                        end = pe.transpose(turn_ps[:, a, k], y[:, q, a * QUARTER + k], m.ident[:, :])
                    end.then_inc(turned, 1)

            def body(i, r):
                turn(i, r + 1)
                if missing(i, r):
                    return
                q = r % 2
                wait_all(pe, *[(out_done, nth(i, r - 2))][:not opening(i, r, 2)])
                for k in range(KI):
                    if k % QUARTER == 0:
                        wait_all(pe, (lo_done, 4 * nth(i, r) - 3 + k // QUARTER))
                    if opening(i, r, 1):
                        pe.wait_ge(w.done, k + 1)
                    end = three_passes(pe, out_ps[:, q], lambda k: (hi[:, q, k], lo[:, q, k]),
                                       lambda k: [x[:, k] for x in w_c], [k],
                                       first=k == 0, last=k == KI - 1)
                end.then_inc(out_mm, 1)

            turn(0, 0)
            each_unit(pe, body, TILES, STEPS, LEAD, TAIL)

        @block.scalar
        def _(act):
            def body(i, r):
                if missing(i, r):
                    return
                q = r % 2
                for a in range(4):
                    wait_all(act, (turned, 4 * nth(i, r) - 3 + a),
                             *[(out_mm, nth(i, r - 2))][:not opening(i, r, 2)])
                    act.activation(hi[:, q, a * QUARTER:(a + 1) * QUARTER], turn_ps[:, a],
                                   ACT.Copy).then_inc(hi_done, 1)

            body(0, 0)
            for n in range(w.n):
                w.round_hi(act, n)
            each_unit(act, lambda i, r: None if opening(i, r, 1) else body(i, r), TILES, STEPS, LEAD, TAIL)

        @block.vector
        def _(dve):
            def split(i, r):
                q = r % 2
                for a in range(4):
                    cols = slice(a * QUARTER, (a + 1) * QUARTER)
                    wait_all(dve, (hi_done, 4 * nth(i, r) - 3 + a))
                    dve.tensor_tensor(lo[:, q, cols], turn_ps[:, a], hi[:, q, cols].bitcast(F32),
                                      ALU.subtract).then_inc(lo_done, 1)

            def body(i, r):
                if not missing(i, r) and not opening(i, r, 1):
                    split(i, r)
                if not missing(i, r - 1):
                    q = (r - 1) % 2
                    wait_all(dve, (out_mm, nth(i, r - 1)), (bias_loaded, 16),
                             *[(stored[q], 16 * nth(i, r - 3, 2))][:not opening(i, r, 3)])
                    dve.tensor_tensor(out[:, q], out_ps[:, q], bias[:, :], ALU.add).then_inc(out_done, 1)

            split(0, 0)
            for n in range(w.n):
                w.keep_lo(dve, n)
            each_unit(dve, body, TILES, STEPS, LEAD, TAIL)


def mlp_down(nc, m):
    STEPS, LEAD, TAIL = 4, 3, 1
    LAST = TILES // STEPS - 1
    KS = SHARED // P
    with Scope(nc, "mlp_down") as s:
        w_down = [s.sb(f"w_{x}", [P, BLOCKS, D], F32R) for x in ("hi", "lo")]
        w = split_weights(s, "w", [(m.w_mlp_down[k], w_down[0][:, k], w_down[1][:, k], None)
                                   for k in range(BLOCKS)], D)
        h = s.sb("h", [P, 2, BLOCKS, P])
        hi, lo = s.sb("h_hi", [P, 2, BLOCKS, P], F32R), s.sb("h_lo", [P, 2, BLOCKS, P], F32R)
        x1, mixer = s.sb("x1", [P, 4, D]), s.sb("mixer", [P, 4, D])
        routed, total, gate, out = (s.sb(n, [P, 2, D]) for n in ("routed", "total", "gate", "out"))
        shared_ps, routed_ps = s.ps("shared_ps", [P, 2, D]), s.ps("routed_ps", [P, 2, D])
        h_loaded = [s.sem(f"h_loaded{q}") for q in range(2)]
        rows_loaded = [s.sem(f"rows_loaded{q}") for q in range(2)]
        hi_done, lo_done, shared_mm, routed_done, total_done, gate_done, gated_done, out_done = (
            s.sem(n) for n in ("hi_done", "lo_done", "shared_mm", "routed_done", "total_done",
                               "gate_done", "gated_done", "out_done"))
        stored = [s.sem(f"stored{q}") for q in range(2)]
        block = s.block()
        x1_t, s_t, out_t = (d.rearrange("(n p) d -> n p d", p=P) for d in (m.x1_dram, m.s_dram, m.out))
        hidden_p = m.hidden_dram.rearrange("k p t -> p k t")

        def missing(i, r):
            return opening(i, r, 0) or (isinstance(i, int) and i == LAST and r >= STEPS)

        def nth(i, r, ring=1):
            return i * (STEPS // ring) + r // ring + 1

        @block.sync
        def _(sync):
            def load(i, r):
                q, t = r % 2, i * STEPS + r
                tokens = columns_of(sync, t, P)
                rows = [row_of(sync, d, t).rearrange("(p d) -> p d", p=P) for d in (x1_t, s_t)]
                if not opening(i, r, 2):
                    sync.wait_ge(lo_done, nth(i, r - 2))
                sync.dma_start(h[:, q], hidden_p[:, :, tokens]).then_inc(h_loaded[q], 16)
                if not opening(i, r, 4):
                    sync.wait_ge(out_done, nth(i, r - 4))
                for tile, source in zip((x1, mixer), rows):
                    sync.dma_start(tile[:, r % 4], source).then_inc(rows_loaded[q], 16)

            def body(i, r):
                if not missing(i, r + 2):
                    load(i, r + 2)
                if not missing(i, r - 1):
                    q = (r - 1) % 2
                    rows = row_of(sync, out_t, i * STEPS + r - 1).rearrange("(p d) -> p d", p=P)
                    wait_all(sync, (out_done, nth(i, r - 1)))
                    sync.dma_start(rows, out[:, q]).then_inc(stored[q], 16)

            load(0, 0)
            for n in range(w.ring):
                w.load(sync, n)
            load(0, 1)
            for n in range(w.ring, w.n):
                w.load(sync, n)
            each_unit(sync, body, TILES, STEPS, 2, TAIL)
            for q in range(2):
                sync.wait_ge(stored[q], 16 * TILES // 2)

        @block.tensor
        def _(pe):
            def body(i, r):
                if missing(i, r):
                    return
                q = r % 2
                wait_all(pe, (lo_done, nth(i, r)), *[(total_done, nth(i, r - 2))][:not opening(i, r, 2)])
                for ps, ks in ((shared_ps, range(KS)), (routed_ps, range(KS, BLOCKS))):
                    for k in ks:
                        if opening(i, r, 1):
                            pe.wait_ge(w.done, k + 1)
                        end = three_passes(pe, ps[:, q], lambda k: (hi[:, q, k], lo[:, q, k]),
                                           lambda k: [x[:, k] for x in w_down], [k],
                                           first=k == ks[0], last=k == ks[-1])
                end.then_inc(shared_mm, 1)

            each_unit(pe, body, TILES, STEPS, LEAD, TAIL)

        @block.scalar
        def _(act):
            def split(i, r):
                if missing(i, r):
                    return
                q = r % 2
                wait_all(act, (h_loaded[q], 16 * nth(i, r, 2)),
                         *[(shared_mm, nth(i, r - 2))][:not opening(i, r, 2)])
                act.activation(hi[:, q], h[:, q], ACT.Copy).then_inc(hi_done, 1)

            def body(i, r):
                if not opening(i, r, 1):
                    split(i, r)
                if not missing(i, r - 1):
                    q, t = (r - 1) % 2, i * STEPS + r - 1
                    wait_all(act, (shared_mm, nth(i, r - 1)))
                    act.activation(routed[:, q], routed_ps[:, q], ACT.Copy,
                                   scale=m.comb_w[:, bass.ds(t, 1)]).then_inc(routed_done, 1)
                    wait_all(act, (total_done, nth(i, r - 1)))
                    act.activation(gate[:, q], total[:, q], ACT.Silu).then_inc(gate_done, 1)

            split(0, 0)
            for n in range(w.n):
                w.round_hi(act, n)
            each_unit(act, body, TILES, STEPS, LEAD, TAIL)

        @block.vector
        def _(dve):
            def split(i, r):
                q = r % 2
                wait_all(dve, (hi_done, nth(i, r)))
                dve.tensor_tensor(lo[:, q], h[:, q], hi[:, q].bitcast(F32), ALU.subtract).then_inc(lo_done, 1)

            def finish(i, r):
                q = r % 2
                wait_all(dve, (routed_done, nth(i, r)),
                         *[(gate_done, nth(i, r - 2))][:not opening(i, r, 2)])
                dve.tensor_tensor(total[:, q], routed[:, q], shared_ps[:, q], ALU.add).then_inc(total_done, 1)
                wait_all(dve, (gate_done, nth(i, r)), (rows_loaded[q], 32 * nth(i, r, 2)),
                         *[(stored[q], 16 * nth(i, r - 2, 2))][:not opening(i, r, 2)])
                dve.tensor_tensor(gate[:, q], gate[:, q], mixer[:, r % 4], ALU.mult).then_inc(gated_done, 1)
                wait_all(dve, (gated_done, nth(i, r)))
                dve.tensor_tensor(out[:, q], gate[:, q], x1[:, r % 4], ALU.add).then_inc(out_done, 1)

            def body(i, r):
                if not missing(i, r) and not opening(i, r, 1):
                    split(i, r)
                if not missing(i, r - 1):
                    finish(i, r - 1)

            split(0, 0)
            for n in range(w.n):
                w.keep_lo(dve, n)
            each_unit(dve, body, TILES, STEPS, LEAD, TAIL)


_INS = ['L0_attn_hidden_states', 'L0_attn_W_in', 'L0_attn_conv_w', 'L0_attn_conv_b', 'L0_attn_dt_bias',
        'L0_attn_A_log', 'L0_attn_D_param', 'L0_attn_norm_w', 'L0_attn_W_out', 'L0_ffn_W_up',
        'L0_ffn_W_down', 'L0_ffn_W_gate', 'L0_ffn_W_expert', 'L1_attn_Wq', 'L1_attn_Wk', 'L1_attn_Wv',
        'L1_attn_Wg', 'L1_attn_Wc', 'L1_attn_bc', 'L1_ffn_router_weight', 'L1_ffn_sh_gate',
        'L1_ffn_sh_up', 'L1_ffn_sh_down', 'L1_ffn_r_gate', 'L1_ffn_r_up', 'L1_ffn_r_down']


def lay_out(i):
    import numpy as np
    a = {n: np.asarray(v) for n, v in i.items()}
    f = np.float32

    def rows(w):
        return w.reshape(-1, P, w.shape[1])

    def blocks(*parts):
        w = np.stack([p.reshape(-1, P, KD, P) for p in parts])
        return w.transpose(1, 4, 3, 0, 2)

    w_in = a['L0_attn_W_in']
    gate, xs, bc = w_in[:INTER], w_in[INTER:2 * INTER], w_in[2 * INTER:]
    b_w, c_w, dt_w = bc[:STATE], bc[STATE:2 * STATE], bc[2 * STATE:]
    taps = np.concatenate([a['L0_attn_conv_w'], a['L0_attn_conv_b'][:, None]], 1)
    d_rows = np.repeat(a['L0_attn_D_param'], HEAD_P)[:, None]
    pad = np.zeros((INTER, 2), f)
    q = a['L1_attn_Wq'].T.reshape(KV_HEADS, REP, HEAD_D, D)
    out = {
        'x': a['L0_attn_hidden_states'].reshape(TOK, D),
        'w_up': rows(a['L0_ffn_W_up'].T), 'w_down': rows(a['L0_ffn_W_down'].T),
        'w_expert': rows(np.concatenate([a['L0_ffn_W_expert'], a['L0_ffn_W_gate'].T], 1)),
        'w_bcd': rows(np.concatenate([b_w, dt_w, c_w]).T),
        'bc_vec': np.concatenate([taps[INTER:], np.zeros((2 * STATE, 3), f)], 1).reshape(
            2, P, 8).transpose(1, 0, 2),
        'head_vec': np.stack([a['L0_attn_dt_bias'], a['L0_attn_A_log']], 1),
        'w_gate_x': blocks(gate, xs),
        'pair_vec': np.concatenate([taps[:INTER], d_rows, pad], 1).reshape(PAIRS, P, 8),
        'norm_w': a['L0_attn_norm_w'].reshape(KI, P).T, 'w_out': rows(a['L0_attn_W_out'].T),
        'w_gvr': rows(np.concatenate([a['L1_attn_Wg'], a['L1_attn_Wv'],
                                      a['L1_ffn_router_weight'].T], 1)),
        'w_qqk': blocks(q[:, 0].reshape(-1, D), q[:, 1].reshape(-1, D), a['L1_attn_Wk'].T),
        'w_c': rows(a['L1_attn_Wc']), 'b_c': a['L1_attn_bc'].reshape(1, D),
        'w_gate_up': blocks(np.concatenate([a['L1_ffn_sh_gate'], a['L1_ffn_r_gate']]),
                            np.concatenate([a['L1_ffn_sh_up'], a['L1_ffn_r_up']])),
        'w_mlp_down': rows(np.concatenate([a['L1_ffn_sh_down'].T, a['L1_ffn_r_down'].T])),
        'ident': np.eye(P, dtype=f),
        'causal': np.triu(np.ones((P, P), f)),
        'never': np.where(np.arange(P)[None, :] >= np.arange(P)[:, None], f(0), f(-1e30)),
    }
    return {n: np.ascontiguousarray(v) for n, v in out.items()}


class Memory:

    def __init__(self, d, out):
        self.x, self.out = d["x"], out
        self.w_up, self.w_down, self.w_expert = d["w_up"], d["w_down"], d["w_expert"]
        self.w_bcd, self.w_gate_x, self.pair_vec, self.w_out = (
            d["w_bcd"], d["w_gate_x"], d["pair_vec"], d["w_out"])
        self.w_gvr, self.w_qqk, self.w_c, self.b_c = d["w_gvr"], d["w_qqk"], d["w_c"], d["b_c"]
        self.w_gate_up, self.w_mlp_down = d["w_gate_up"], d["w_mlp_down"]


def build(nc, d, out, debug=()):
    with ExitStack() as stack:
        def sb(name, shape, dtype=F32):
            return stack.enter_context(nc.sbuf_tensor(name, shape, dtype))

        def dram(name, shape):
            return nc.dram_tensor(name, shape, F32, kind="ExternalOutput" if name in debug else "Internal").ap()

        m = Memory(d, out)
        m.gate_dram, m.x1_dram, m.s_dram = (dram(n, [TOK, D]) for n in ("gate_s", "x1_s", "s_s"))
        m.ell_dram = dram("ell_s", [PAIRS, 2, TOK])
        m.mixed_dram = dram("mixed_s", [PAIRS, P, TOK])
        m.log_gate_dram = dram("log_gate_s", [KV_HEADS, TOK])
        m.values_dram = dram("values_s", [TOK, KV_DIM])
        m.attended_dram = dram("attended_s", [TOK, Q_DIM])
        m.hidden_dram = dram("hidden_s", [BLOCKS, P, TOK])
        constants = ("ident", "causal", "never", "bc_vec", "head_vec", "norm_w")
        loaded = {n: sb(f"{n}_sb", list(d[n].shape)) for n in constants}
        m.ident, m.causal, m.never, m.bc_vec, m.head_vec, m.norm_w = (loaded[n] for n in constants)
        m.comb_w = sb("comb_w", [P, TILES])
        m.constants = [(loaded[n], d[n]) for n in constants]
        m.constants_loaded = nc.alloc_semaphore("constants_loaded")
        m.gate_stored = nc.alloc_semaphore("gate_stored")
        with nc.sbuf_tensor("xn_hi", [P, KD, TOK], F32R) as m.xn_hi, \
                nc.sbuf_tensor("xn_lo", [P, KD, TOK], F32R) as m.xn_lo, \
                nc.sbuf_tensor("b_tm", [P, TILES, P], F32) as m.b_tm:
            norm_and_mixture(nc, m)
            with nc.sbuf_tensor("c_fm", [P, TOK], F32) as m.c_fm, \
                    nc.sbuf_tensor("cb", [P, TILES, P], F32) as m.cb, \
                    nc.sbuf_tensor("times_tm", [P, 3 * TILES, HEADS], F32) as m.times_tm, \
                    nc.sbuf_tensor("chunk_decay", [P, HEADS, TILES], F32) as m.chunk_decay:
                m.dt_tm, m.dt_end_tm, m.ell_tm = (m.times_tm[:, n * TILES:(n + 1) * TILES]
                                                  for n in range(3))
                ssm_shared(nc, m)
                ssm_heads(nc, m)
        ssm_output(nc, m)
        with nc.sbuf_tensor("xn1_hi", [P, KD, TOK], F32R) as m.xn_hi, \
                nc.sbuf_tensor("xn1_lo", [P, KD, TOK], F32R) as m.xn_lo:
            normalize(nc, "norm1", m.x1_dram, m)
            with nc.sbuf_tensor("log_gate_tm", [P, KV_HEADS, TILES], F32) as m.log_gate_tm:
                values_and_decays(nc, m)
                power_attention(nc, m)
            mlp_up(nc, m)
        attention_output(nc, m)
        mlp_down(nc, m)


def kernel(**inputs):
    import concourse.bacc as bacc
    from concourse.bass_utils import run_bass_kernel_spmd

    arrays = lay_out({n: inputs[n] for n in _INS})
    nc = bacc.Bacc("TRN2", target_bir_lowering=False, num_devices=1)
    d = {n: nc.dram_tensor(f"in_{n}", list(a.shape), F32, kind="ExternalInput").ap()
         for n, a in arrays.items()}
    out = nc.dram_tensor("out", [TOK, D], F32, kind="ExternalOutput").ap()
    build(nc, d, out)
    r = run_bass_kernel_spmd(nc, [{f"in_{n}": a for n, a in arrays.items()}], core_ids=[0])
    return r.results[0]["out"].reshape(B, SEQ, D)
```

```python
from contextlib import ExitStack, contextmanager

import concourse.bass as bass
from concourse import mybir

F32 = mybir.dt.float32
F32R = mybir.dt.float32r
ACT = mybir.ActivationFunctionType
ALU = mybir.AluOpType
AX = mybir.AxisListType

P = 128
B, SEQ, D = 4, 512, 512
TOK = B * SEQ
TILES = TOK // P
CH = SEQ // P
KD = D // P
LN_EPS = 1e-5

HEADS, HEAD_P, STATE, TAPS = 32, 64, 128, 4
INTER = HEADS * HEAD_P
PAIRS = INTER // P
KI = INTER // P
EXPERTS = 8
KV_HEADS, REP, HEAD_D = 8, 2, 128
Q_DIM, KV_DIM = KV_HEADS * REP * HEAD_D, KV_HEADS * HEAD_D
SHARED, ROUTED = 2048, 256
HIDDEN = SHARED + ROUTED
BLOCKS = HIDDEN // P


def three_passes(pe, out, left, right, ks, first=True, last=True):
    ks = list(ks)
    for k in ks:
        (l_hi, l_lo), (r_hi, r_lo) = left(k), right(k)
        pe.matmul(out, l_lo, r_hi, start=first and k == ks[0], stop=False)
        pe.matmul(out, l_hi, r_lo, start=False, stop=False)
        end = pe.matmul(out, l_hi, r_hi, start=False, stop=last and k == ks[-1])
    return end


class Scope:

    def __init__(self, nc, stage):
        self.nc, self.stage, self.stack, self.sems = nc, stage, ExitStack(), []

    def __enter__(self):
        self.stack.__enter__()
        return self

    def __exit__(self, *exc):
        self.stack.__exit__(*exc)
        if exc[0] is None:
            self.nc.clear_and_free_semaphores(self.sems)
            self.nc.all_engine_barrier()

    def sb(self, name, shape, dtype=F32):
        return self.stack.enter_context(self.nc.sbuf_tensor(f"{self.stage}_{name}", shape, dtype))

    def ps(self, name, shape):
        return self.stack.enter_context(self.nc.psum_tensor(f"{self.stage}_{name}", shape, F32))

    def sem(self, name):
        self.sems.append(self.nc.alloc_semaphore(f"{self.stage}_{name}"))
        return self.sems[-1]

    def block(self):
        return self.stack.enter_context(self.nc.Block())


class Steps:

    def __init__(self, load, round_hi, keep_lo, done, n, ring):
        self.load, self.round_hi, self.keep_lo = load, round_hi, keep_lo
        self.done, self.n, self.ring = done, n, ring


def first_piece(dram, w):
    flat = "p k c n -> p (k c n)"
    return dram[0].rearrange(flat), w[0][:, 0].rearrange(flat), w[1][:, 0].rearrange(flat), None


def split_weights(s, name, pieces, widest, ring=3, raw=None):
    raw = s.sb(f"{name}_raw", [P, ring, widest]) if raw is None else raw
    loaded = [s.sem(f"{name}_loaded{i}") for i in range(ring)]
    hi_done, lo_done = s.sem(f"{name}_hi_done"), s.sem(f"{name}_lo_done")

    def width(n):
        return pieces[n][1].shape[-1]

    def load(sync, n):
        if n >= ring:
            sync.wait_ge(lo_done, n - ring + 1)
        sync.dma_start(raw[:, n % ring, 0:width(n)], pieces[n][0]).then_inc(loaded[n % ring], 16)

    def round_hi(act, n):
        _, hi, _, scale = pieces[n]
        act.wait_ge(loaded[n % ring], 16 * (n // ring + 1))
        act.activation(hi, raw[:, n % ring, 0:width(n)], ACT.Identity,
                       scale=1.0 if scale is None else scale).then_inc(hi_done, 1)

    def keep_lo(dve, n):
        _, hi, lo, scale = pieces[n]
        dve.wait_ge(hi_done, n + 1)
        if scale is None:
            dve.tensor_tensor(lo, raw[:, n % ring, 0:width(n)], hi.bitcast(F32),
                              ALU.subtract).then_inc(lo_done, 1)
        else:
            dve.scalar_tensor_tensor(out=lo, in0=raw[:, n % ring, 0:width(n)], scalar=scale,
                                     in1=hi.bitcast(F32), op0=ALU.mult,
                                     op1=ALU.subtract).then_inc(lo_done, 1)

    return Steps(load, round_hi, keep_lo, lo_done, len(pieces), ring)


def norm_and_mixture(nc, m):
    G = CH
    E_COLS = D + EXPERTS
    EH = E_COLS // 2
    with Scope(nc, "mix") as s:
        up = [s.sb(f"up_{x}", [P, KD, D], F32R) for x in ("hi", "lo")]
        down = [s.sb(f"down_{x}", [P, KD, D], F32R) for x in ("hi", "lo")]
        expert = [s.sb(f"expert_{x}", [P, KD, E_COLS], F32R) for x in ("hi", "lo")]
        h_hi = s.sb("h_hi", [P, 2, KD, SEQ], F32R)
        h_lo = s.sb("h_lo", [P, 2, KD, SEQ], F32R)
        top8 = s.sb("top8", [P, 2, 8])
        below = s.sb("below", [P, 2, 2])
        e2 = s.sb("e2", [P, 2, 2])
        esum = s.sb("esum", [P, 2])
        einv = s.sb("einv", [P, 2])
        rw = s.sb("rw", [P, 2, 2])
        rsum = s.sb("rsum", [P, 2])
        scaled = s.sb("scaled", [P, 2, D])
        total = s.sb("total", [P, CH, D])
        gate = m.b_tm[:, :, :].rearrange("p t n -> p (t n)").rearrange("p (c d) -> p c d", c=CH)
        gate_stored = m.gate_stored
        x, xn = s.sb("x", [P, 2, G, D]), s.sb("xn", [P, G, D])
        stats, mv = s.sb("stats", [P, G, 6]), s.sb("mean_var", [P, G, 2])
        var_eps, std, rstd = (s.sb(n, [P, G]) for n in ("var_eps", "std", "rstd"))
        up_ps = s.ps("up_ps", [P, 2, SEQ])
        sh_ps = s.ps("sh_ps", [P, 2, D])
        ex_ps = s.ps("ex_ps", [P, 2, 2, 512])
        turned = ex_ps[:, :, :, :].rearrange("p a b (k t) -> p (a b) k t", t=P)
        pieces = [(dram[k], w[0][:, k], w[1][:, k], None)
                  for dram, w in ((m.w_up, up), (m.w_down, down), (m.w_expert, expert))
                  for k in range(KD)]
        w = split_weights(s, "w", pieces, E_COLS, 4)
        EARLY, LATE = range(KD // 2), range(KD // 2, KD)
        x_loaded = [[s.sem(f"x_loaded{q}_{j}") for j in range(G)] for q in range(2)]
        stats_done, var_done, std_done, rstd_done, xn_done, turned_done, hi_done, lo_done = (
            s.sem(n) for n in ("stats_done", "var_done", "std_done", "rstd_done", "xn_done",
                               "turned_done", "hi_done", "lo_done"))
        up_done = s.sem("up_done")
        h_hi_done = s.sem("h_hi_done")
        h_lo_done = s.sem("h_lo_done")
        ffn_done = s.sem("ffn_done")
        top_done = s.sem("top_done")
        below_done = s.sem("below_done")
        e2_done = s.sem("e2_done")
        rw_step = s.sem("rw_step")
        scaled_done = s.sem("scaled_done")
        total_done = s.sem("total_done")
        gate_done = s.sem("gate_done")
        block = s.block()
        gate_b = m.gate_dram.rearrange("(b c p) d -> b p c d", b=B, p=P)

        x_g = m.x.rearrange("(g j p) d -> g j p d", j=G, p=P)

        @block.sync
        def _(sync):
            def load(g):
                for j in range(G):
                    if g >= 2:
                        sync.wait_ge(xn_done, G * (g - 2) + j + 1)
                    sync.dma_start(x[:, g % 2, j], x_g[g, j]).then_inc(x_loaded[g % 2][j], 16)

            load(0)
            for tile, source in m.constants:
                sync.dma_start(tile[:], source).then_inc(m.constants_loaded, 16)
            for n in range(KD):
                w.load(sync, n)
            load(1)
            for n in range(KD, KD + w.ring):
                w.load(sync, n)
            load(2)
            load(3)
            for n in range(KD + w.ring, w.n):
                w.load(sync, n)
            sync.wait_ge(m.constants_loaded, 16 * len(m.constants))
            for b in range(B):
                sync.wait_ge(gate_done, b + 1)
                sync.dma_start(gate_b[b], gate[:, :, :]).then_inc(gate_stored, 16)

        @block.tensor
        def _(pe):
            def turn(g):
                for j in range(G):
                    pe.wait_ge(xn_done, G * g + j + 1)
                    if g >= 1:
                        pe.wait_ge(lo_done, G * (g - 1) + j + 1)
                    for k in range(KD):
                        end = pe.transpose(turned[:, j, k], xn[:, j, k * P:(k + 1) * P], m.ident[:, :])
                    end.then_inc(turned_done, 1)

            def up_product(b, blocks=range(KD)):
                pe.wait_ge(lo_done, G * (b + 1))
                for f in blocks:
                    n = KD * b + f
                    if n >= 2:
                        pe.wait_ge(h_lo_done, n - 1)
                    for k in range(KD):
                        if n == 0:
                            pe.wait_ge(w.done, k + 1)
                        end = three_passes(
                            pe, up_ps[:, n % 2],
                            lambda k: [x[:, k, f * P:(f + 1) * P] for x in up],
                            lambda k: [x[:, k, b * SEQ:(b + 1) * SEQ] for x in (m.xn_hi, m.xn_lo)],
                            [k], first=k == 0, last=k == KD - 1)
                    end.then_inc(up_done, 1)

            def down_and_expert(b):
                for j in range(CH):
                    t = CH * b + j
                    pe.wait_ge(h_lo_done, KD * (b + 1))
                    if t == 0:
                        pe.wait_ge(w.done, 2 * KD)
                    if t >= 2:
                        pe.wait_ge(total_done, t - 1)
                    three_passes(pe, sh_ps[:, t % 2],
                                 lambda f: [x[:, b % 2, f, j * P:(j + 1) * P] for x in (h_hi, h_lo)],
                                 lambda f: [x[:, f] for x in down], range(KD))
                    if t == 0:
                        pe.wait_ge(w.done, w.n)
                        pe.wait_ge(lo_done, TILES)
                    for half in range(2):
                        end = three_passes(
                            pe, ex_ps[:, t % 2, half, 0:EH],
                            lambda k: [x[:, k, t * P:(t + 1) * P] for x in (m.xn_hi, m.xn_lo)],
                            lambda k: [x[:, k, half * EH:(half + 1) * EH] for x in expert], range(KD))
                    end.then_inc(ffn_done, 1)

            pe.wait_ge(m.constants_loaded, 16 * len(m.constants))
            turn(0)
            for b in range(2):
                up_product(b, EARLY)
                turn(b + 1)
                up_product(b, LATE)
            turn(3)
            down_and_expert(0)
            for b in range(1, B):
                if b + 1 < B:
                    up_product(b + 1)
                down_and_expert(b)

        @block.scalar
        def _(act):
            def relu_hi(b, blocks=range(KD)):
                for f in blocks:
                    n = KD * b + f
                    act.wait_ge(up_done, n + 1)
                    if b >= 2:
                        act.wait_ge(ffn_done, CH * (b - 1))
                    act.activation(h_hi[:, b % 2, f], up_ps[:, n % 2], ACT.Relu).then_inc(h_hi_done, 1)

            def deviations(g):
                act.wait_ge(var_done, (G + 1) * (g + 1))
                act.activation(std[:, :], var_eps[:, :], ACT.Sqrt).then_inc(std_done, 1)

            def round_xn(g, tiles=range(G)):
                for t in [G * g + j for j in tiles]:
                    act.wait_ge(turned_done, t + 1)
                    act.activation(m.xn_hi[:, :, t * P:(t + 1) * P], turned[:, t % G],
                                   ACT.Copy).then_inc(hi_done, 1)

            def silu(b):
                act.wait_ge(total_done, CH * (b + 1))
                if b >= 1:
                    act.wait_ge(gate_stored, 16 * b)
                act.activation(gate[:, :, :], total[:, :, :], ACT.Silu).then_inc(gate_done, 1)

            deviations(0)
            for j in range(G):
                w.round_hi(act, j)
                round_xn(0, [j])
            deviations(1)
            for b in range(2):
                relu_hi(b, EARLY)
                round_xn(b + 1)
                deviations(b + 2)
                relu_hi(b, LATE)
                for n in range(KD * (b + 1), KD * (b + 2)):
                    w.round_hi(act, n)
            round_xn(3)
            for b in range(B):
                if 1 <= b < B - 1:
                    relu_hi(b + 1)
                if b >= 1:
                    silu(b - 1)
                for j in range(CH):
                    t = CH * b + j
                    act.wait_ge(below_done, t + 1)
                    act.activation(e2[:, t % 2], below[:, t % 2], ACT.Exp).then_inc(e2_done, 1)
                    act.wait_ge(rw_step, 4 * (t + 1))
                    if t >= 2:
                        act.wait_ge(total_done, t - 1)
                    act.activation(scaled[:, t % 2, 0:EH], ex_ps[:, t % 2, 0, 0:EH], ACT.Copy,
                                   scale=rsum[:, t % 2:t % 2 + 1]).then_inc(scaled_done, 1)
                    act.activation(scaled[:, t % 2, EH:D], ex_ps[:, t % 2, 1, 0:D - EH], ACT.Copy,
                                   scale=rsum[:, t % 2:t % 2 + 1]).then_inc(scaled_done, 1)
            silu(B - 1)

        @block.vector
        def _(dve):
            def relu_lo(b, blocks=range(KD)):
                for f in blocks:
                    n = KD * b + f
                    dve.wait_ge(h_hi_done, n + 1)
                    dve.scalar_tensor_tensor(out=h_lo[:, b % 2, f], in0=up_ps[:, n % 2], scalar=0.0,
                                             in1=h_hi[:, b % 2, f].bitcast(F32),
                                             op0=ALU.max, op1=ALU.subtract).then_inc(h_lo_done, 1)

            def variances(g):
                if g >= 1:
                    dve.wait_ge(xn_done, G * g)
                for j in range(G):
                    dve.wait_ge(x_loaded[g % 2][j], 16 * (g // 2 + 1))
                    dve.bn_stats(stats[:, j], x[:, g % 2, j]).then_inc(stats_done, 1)
                for j in range(G):
                    dve.wait_ge(stats_done, G * g + j + 1)
                    dve.bn_aggr(mv[:, j], stats[:, j]).then_inc(var_done, 1)
                dve.wait_ge(var_done, (G + 1) * g + G)
                dve.tensor_scalar(var_eps[:, :], mv[:, :, 1], LN_EPS, None, ALU.add).then_inc(var_done, 1)

            def scale(g):
                dve.wait_ge(std_done, g + 1)
                dve.reciprocal(rstd[:, :], std[:, :]).then_inc(rstd_done, 1)
                dve.wait_ge(rstd_done, g + 1)
                for j in range(G):
                    if g >= 1:
                        dve.wait_ge(turned_done, G * (g - 1) + j + 1)
                    dve.tensor_scalar(xn[:, j], x[:, g % 2, j], mv[:, j, 0:1], rstd[:, j:j + 1],
                                      ALU.subtract, ALU.mult).then_inc(xn_done, 1)

            def keep_xn_lo(g):
                for t in range(G * g, G * (g + 1)):
                    dve.wait_ge(hi_done, t + 1)
                    dve.tensor_tensor(m.xn_lo[:, :, t * P:(t + 1) * P], turned[:, t % G],
                                      m.xn_hi[:, :, t * P:(t + 1) * P].bitcast(F32),
                                      ALU.subtract).then_inc(lo_done, 1)

            variances(0)
            scale(0)
            keep_xn_lo(0)
            variances(1)
            scale(1)
            for b in range(2):
                relu_lo(b, EARLY)
                keep_xn_lo(b + 1)
                variances(b + 2)
                scale(b + 2)
                relu_lo(b, LATE)
            keep_xn_lo(3)
            for b in range(B):
                if 1 <= b < B - 1:
                    relu_lo(b + 1)
                for j in range(CH):
                    t, i = CH * b + j, (CH * b + j) % 2
                    dve.wait_ge(ffn_done, t + 1)
                    dve.max(top8[:, i], ex_ps[:, i, 1, D - EH:EH]).then_inc(top_done, 1)
                    dve.wait_ge(top_done, t + 1)
                    dve.tensor_scalar(below[:, i], top8[:, i, 0:2], top8[:, i, 0:1], None,
                                      ALU.subtract).then_inc(below_done, 1)
                    dve.wait_ge(e2_done, t + 1)
                    dve.tensor_tensor(esum[:, i:i + 1], e2[:, i, 0:1], e2[:, i, 1:2],
                                      ALU.add).then_inc(rw_step, 1)
                    dve.wait_ge(rw_step, 4 * t + 1)
                    dve.reciprocal(einv[:, i:i + 1], esum[:, i:i + 1]).then_inc(rw_step, 1)
                    dve.wait_ge(rw_step, 4 * t + 2)
                    dve.tensor_scalar(rw[:, i], e2[:, i], einv[:, i:i + 1], None,
                                      ALU.mult).then_inc(rw_step, 1)
                    dve.wait_ge(rw_step, 4 * t + 3)
                    dve.tensor_tensor(rsum[:, i:i + 1], rw[:, i, 0:1], rw[:, i, 1:2],
                                      ALU.add).then_inc(rw_step, 1)
                    dve.wait_ge(scaled_done, 2 * (t + 1))
                    if b >= 1 and j == 0:
                        dve.wait_ge(gate_done, b)
                    dve.tensor_tensor(total[:, j], scaled[:, i], sh_ps[:, i],
                                      ALU.add).then_inc(total_done, 1)

        @block.gpsimd
        def _(pool):
            for n in range(w.n):
                w.keep_lo(pool, n)


def ssm_shared(nc, m):
    with Scope(nc, "shared") as s:
        COLS = 2 * STATE + HEADS
        DT0, C0 = STATE, STATE + HEADS
        starts = {"dt": DT0, "B": 0, "C": C0}
        w_bcd = [s.sb(f"w_{x}", [P, KD, COLS], F32R) for x in ("hi", "lo")]
        raw = s.sb("raw", [P, 2, B, TAPS - 1 + SEQ])
        b_fm = s.sb("b_fm", [P, TOK])
        dtx = s.sb("dtx", [HEADS, TOK])
        dt_abs = s.sb("dt_abs", [HEADS, TOK])
        dt_exp = s.sb("dt_exp", [HEADS, TOK])
        dt_one = s.sb("dt_one", [HEADS, TOK])
        dt_err = s.sb("dt_err", [HEADS, TOK])
        dt = s.sb("dt", [HEADS, TOK])
        keep = m.cb[0:HEADS].rearrange("h t p -> h (t p)")
        ell = s.sb("ell", [HEADS, TILES, P])
        a_exp = s.sb("a_exp", [HEADS, 1])
        end_exp = s.sb("end_exp", [HEADS, TILES])
        diag = s.sb("diag", [HEADS, HEADS, TILES])
        ones = s.sb("ones", [HEADS, P])
        la, to_end, end_w, dt_end, dt_log = dt_abs, dt_exp, dt_one, dt_err, dt_one
        proj_ps = s.ps("proj_ps", [P, 3, SEQ])
        turn_ps = s.ps("turn_ps", [P, 4, 512])
        w = split_weights(s, "w", [(m.w_bcd[k], w_bcd[0][:, k], w_bcd[1][:, k], None)
                                   for k in range(KD)], COLS, KD,
                          raw[:, :, :, :].rearrange("p k b t -> p (k b t)")[:, 0:KD * COLS].rearrange(
                              "p (n c) -> p n c", n=KD))
        nxt = split_weights(s, "next", [first_piece(m.w_gate_x, m.w_heads)], KD * 2 * P, 1,
                            b_fm[:, 0:KD * 2 * P].rearrange("p (o n) -> p o n", o=1))
        proj_done, proj_read = s.sem("proj_done"), s.sem("proj_read")
        abs_done, exp_done, one_done = s.sem("abs_done"), s.sem("exp_done"), s.sem("one_done")
        log_done, err_done, log1p_done = s.sem("log_done"), s.sem("err_done"), s.sem("log1p_done")
        relu_done = s.sem("relu_done")
        dt_done, la_done, keep_done, ell_done = (s.sem("dt_done"), s.sem("la_done"),
                                                 s.sem("keep_done"), s.sem("ell_done"))
        a_done, to_end_done, end_w_done, dt_end_done = (s.sem("a_done"), s.sem("to_end_done"),
                                                        s.sem("end_w_done"), s.sem("dt_end_done"))
        end_exp_done, diag_done = s.sem("end_exp_done"), s.sem("diag_done")
        pad_done, conv_done, silu_done = s.sem("pad_done"), s.sem("conv_done"), s.sem("silu_done")
        turned, turned_read = s.sem("turned"), s.sem("turned_read")
        cb_done, ell_stored = s.sem("cb_done"), s.sem("ell_stored")
        block = s.block()

        N_TURN, N_CB, N_TABLE = TILES // 4, TILES // 4, 3
        CB0 = N_TURN
        TABLE0 = CB0 + N_CB

        @block.sync
        def _(sync):
            for n in range(w.n):
                w.load(sync, n)
            nxt.load(sync, 0)
            sync.wait_ge(ell_done, 1)
            sync.dma_start(m.ell_dram.rearrange("a h t -> (a h) t"), ell[:, :, :].rearrange("h t p -> h (t p)")).then_inc(ell_stored, 16)
            sync.wait_ge(ell_stored, 16)

        @block.tensor
        def _(pe):
            for n, (kind, b) in enumerate([(k, b) for k in ("dt", "B", "C") for b in range(B)]):
                if n >= 3:
                    pe.wait_ge(proj_read, n - 2)
                c0 = starts[kind]
                for k in range(KD):
                    if n == 0:
                        pe.wait_ge(w.done, k + 1)
                    end = three_passes(pe, proj_ps[:, n % 3],
                                       lambda k: [x[:, k, c0:c0 + P] for x in w_bcd],
                                       lambda k: [x[:, k, b * SEQ:(b + 1) * SEQ]
                                                  for x in (m.xn_hi, m.xn_lo)],
                                       [k], first=k == 0, last=k == KD - 1)
                end.then_inc(proj_done, 1)
            for n in range(N_TURN):
                pe.wait_ge(silu_done, n // 2 + 1)
                for j in range(4):
                    t = 4 * n + j
                    end = pe.transpose(turn_ps[:, n, j * P:(j + 1) * P], b_fm[:, t * P:(t + 1) * P],
                                       m.ident[:, :])
                end.then_inc(turned, 1)
            for n in range(N_CB):
                pe.wait_ge(silu_done, 2 + n // 2 + 1)
                pe.wait_ge(turned_read, n + 1)
                for j in range(4):
                    t = 4 * n + j
                    end = pe.matmul(turn_ps[:, n, j * P:(j + 1) * P], b_fm[:, t * P:(t + 1) * P],
                                    m.c_fm[:, t * P:(t + 1) * P], start=True, stop=True)
                end.then_inc(turned, 1)
            for n, (table, ready) in enumerate(((dt, dt_done), (None, ell_done), (dt_end, dt_end_done))):
                pe.wait_ge(ready, 1)
                pe.wait_ge(cb_done, n + 1)
                for t in range(TILES):
                    src = ell[:, t] if table is None else table[:, t * P:(t + 1) * P]
                    end = pe.transpose(turn_ps[:, n, t * HEADS:(t + 1) * HEADS], src,
                                       m.ident[0:HEADS, 0:HEADS])
                end.then_inc(turned, 1)
            pe.wait_ge(diag_done, 1)
            pe.wait_ge(cb_done, N_CB)
            pe.matmul(turn_ps[:, N_TABLE, :], ones[:, :], diag[:, :, :].rearrange("h g t -> h (g t)"),
                      start=True, stop=True).then_inc(turned, 1)

        @block.scalar
        def _(act):
            for n in range(w.n):
                w.round_hi(act, n)
            act.activation(a_exp[:, :], m.head_vec[:, 1:2], ACT.Exp).then_inc(a_done, 1)
            nxt.round_hi(act, 0)
            for b in range(B):
                act.wait_ge(proj_done, b + 1)
                act.activation(dtx[:, b * SEQ:(b + 1) * SEQ], proj_ps[0:HEADS, b % 3], ACT.Identity,
                               bias=m.head_vec[:, 0:1]).then_inc(proj_read, 1)
            act.wait_ge(proj_read, B)
            act.activation(dt_abs[:, :], dtx[:, :], ACT.Abs).then_inc(abs_done, 1)
            act.wait_ge(abs_done, 1)
            act.activation(dt_exp[:, :], dt_abs[:, :], ACT.Exp, scale=-1.0).then_inc(exp_done, 1)
            for n in range(B, 3 * B):
                kind, b = (n - B) // B, n % B
                act.wait_ge(proj_done, n + 1)
                act.activation(raw[:, kind, b, TAPS - 1:], proj_ps[:, n % 3],
                               ACT.Copy).then_inc(proj_read, 1)
                if n == 2 * B - 1:
                    act.wait_ge(err_done, 1)
                    act.activation(dt_log[:, :], dt_one[:, :], ACT.Ln).then_inc(log_done, 1)
            for n in range(4):
                half = (b_fm, m.c_fm)[n // 2][:, TOK // 2 * (n % 2):TOK // 2 * (n % 2 + 1)]
                act.wait_ge(conv_done, TAPS * (n + 1))
                act.activation(half, half, ACT.Silu).then_inc(silu_done, 1)
            act.wait_ge(m.gate_stored, 16 * B)
            for n in range(N_TURN):
                act.wait_ge(turned, n + 1)
                act.activation(m.b_tm[:, 4 * n:4 * n + 4], turn_ps[:, n, :].rearrange(
                    "p (t n) -> p t n", n=P), ACT.Copy).then_inc(turned_read, 1)
            act.wait_ge(to_end_done, 1)
            act.activation(end_w[:, :], to_end[:, :], ACT.Exp).then_inc(end_w_done, 1)
            act.activation(end_exp[:, :], ell[:, :, P - 1], ACT.Exp).then_inc(end_exp_done, 1)
            for n, dest in enumerate((m.dt_tm, m.ell_tm, m.dt_end_tm)):
                act.wait_ge(turned, TABLE0 + n + 1)
                act.activation(dest, turn_ps[:, n, :].rearrange("p (t h) -> p t h", h=HEADS),
                               ACT.Copy).then_inc(turned_read, 1)
            act.wait_ge(turned, TABLE0 + N_TABLE + 1)
            act.activation(m.chunk_decay[:, :, :], turn_ps[:, N_TABLE, :].rearrange(
                "p (h t) -> p h t", t=TILES), ACT.Copy).then_inc(turned_read, 1)

        @block.vector
        def _(dve):
            for n in range(w.n):
                w.keep_lo(dve, n)
            dve.wait_ge(exp_done, 1)
            dve.tensor_scalar(dt_one[:, :], dt_exp[:, :], 1.0, None, ALU.add).then_inc(one_done, 1)
            dve.wait_ge(one_done, 1)
            dve.scalar_tensor_tensor(out=dt_err[:, :], in0=dt_one[:, :], scalar=1.0, in1=dt_exp[:, :],
                                     op0=ALU.subtract, op1=ALU.subtract).then_inc(err_done, 1)
            dve.wait_ge(pad_done, 2)
            dve.wait_ge(nxt.done, 1)
            for n in range(4):
                kind, seqs = n // 2, slice(B // 2 * (n % 2), B // 2 * (n % 2 + 1))
                dve.wait_ge(proj_read, B + B // 2 * (n + 1))
                vec = m.bc_vec[:, kind]
                conv = (b_fm, m.c_fm)[kind][:, :].rearrange("p (b t) -> p b t", b=B)[:, seqs]
                dve.tensor_scalar(conv, raw[:, kind, seqs, 0:SEQ], vec[:, 0:1], vec[:, TAPS:TAPS + 1],
                                  ALU.mult, ALU.add).then_inc(conv_done, 1)
                for j in range(1, TAPS):
                    dve.wait_ge(conv_done, TAPS * n + j)
                    dve.scalar_tensor_tensor(out=conv, in0=raw[:, kind, seqs, j:j + SEQ],
                                             scalar=vec[:, j:j + 1], in1=conv,
                                             op0=ALU.mult, op1=ALU.add).then_inc(conv_done, 1)
            dve.wait_ge(la_done, 1)
            dve.wait_ge(keep_done, 2)
            dve.tensor_tensor_scan(ell[:, :, :].rearrange("h t p -> h (t p)"), keep[:, :], la[:, :], 0.0,
                                   ALU.mult, ALU.add).then_inc(ell_done, 1)
            dve.wait_ge(ell_done, 1)
            dve.tensor_tensor(to_end[:, :].rearrange("h (t p) -> h t p", p=P),
                              ell[:, :, P - 1:P].broadcast_to([HEADS, TILES, P]), ell[:, :, :],
                              ALU.subtract).then_inc(to_end_done, 1)
            for n in range(N_CB):
                dve.wait_ge(turned, CB0 + n + 1)
                dve.tensor_tensor(m.cb[:, 4 * n:4 * n + 4], turn_ps[:, n, :].rearrange(
                    "p (t n) -> p t n", n=P),
                    m.causal[:, :].rearrange("p (o n) -> p o n", o=1).broadcast_to([P, 4, P]),
                    ALU.mult).then_inc(cb_done, 1)
            dve.wait_ge(end_w_done, 1)
            dve.tensor_tensor(dt_end[:, :], end_w[:, :], dt[:, :], ALU.mult).then_inc(dt_end_done, 1)
            dve.wait_ge(end_exp_done, 1)
            dve.tensor_tensor(diag[:, :, :],
                              m.ident[0:HEADS, 0:HEADS].rearrange("h (g o) -> h g o", o=1).broadcast_to(
                                  [HEADS, HEADS, TILES]),
                              end_exp[:, :].rearrange("h (o t) -> h o t", o=1).broadcast_to(
                                  [HEADS, HEADS, TILES]), ALU.mult).then_inc(diag_done, 1)

        @block.gpsimd
        def _(pool):
            nxt.keep_lo(pool, 0)
            pool.memset(ones[:, :], 1.0).then_inc(pad_done, 1)
            pool.wait_ge(w.done, w.n)
            pool.memset(raw[:, :, :, 0:TAPS - 1], 0.0).then_inc(pad_done, 1)
            pool.memset(keep[:, :], 1.0).then_inc(keep_done, 1)
            pool.wait_ge(keep_done, 1)
            pool.memset(keep[:, :].rearrange("h (t p) -> h t p", p=P)[:, :, 0:1], 0.0).then_inc(keep_done, 1)
            pool.wait_ge(abs_done, 1)
            pool.tensor_scalar(dt[:, :], dtx[:, :], 0.0, None, ALU.max).then_inc(relu_done, 1)
            pool.wait_ge(err_done, 1)
            pool.wait_ge(log_done, 1)
            pool.tensor_tensor(dt_log[:, :], dt_log[:, :], dt_err[:, :], ALU.subtract).then_inc(log1p_done, 1)
            pool.wait_ge(log1p_done, 1)
            pool.wait_ge(relu_done, 1)
            pool.tensor_tensor(dt[:, :], dt[:, :], dt_log[:, :], ALU.add).then_inc(dt_done, 1)
            pool.wait_ge(dt_done, 1)
            pool.wait_ge(a_done, 1)
            pool.tensor_scalar(la[:, :], dt[:, :], a_exp[:, 0:1], -1.0, ALU.mult, ALU.mult).then_inc(la_done, 1)


def row_of(eng, dram, n):
    size = 1
    for d in dram.shape[1:]:
        size *= d
    start = n * size if isinstance(n, int) else eng.snap(n * size)
    names = " ".join(f"d{k}" for k in range(len(dram.shape)))
    return dram.rearrange(f"{names} -> ({names})")[bass.ds(start, size)]


def columns_of(eng, n, size):
    return bass.ds(n * size if isinstance(n, int) else eng.snap(n * size), size)


def wait_all(eng, *waits):
    values = [v if isinstance(v, int) else eng.snap(v) for _, v in waits]
    for (sem, _), v in zip(waits, values):
        eng.wait_ge(sem, v)


def opening(i, r, upto):
    return isinstance(i, int) and i == 0 and r < upto


def each_unit(eng, body, units, steps, lead, tail):
    turns = units // steps
    for r in range(lead):
        body(0, r)
    with eng.Fori(0, turns - 1) as i:
        for r in range(lead, lead + steps):
            body(i, r)
    for r in range(lead, steps + tail):
        body(turns - 1, r)


def ssm_heads(nc, m):
    STEPS, UNITS, LEAD, TAIL = 2 * B, PAIRS * B, 6, 4
    LAST = UNITS // STEPS - 1
    with Scope(nc, "heads") as s:
        w_raw = s.sb("w_raw", [P, KD, 2, P])
        w_hi, w_lo = m.w_heads
        vec = s.sb("vec", [P, 2, 8])
        times = s.sb("times", [P, 2, 3, TILES, 2])
        decay = s.sb("decay", [P, 2, 2, TILES])
        ell_row = s.sb("ell_row", [P, 2, 2, SEQ])
        ell_exp = s.sb("ell_exp", [P, 4, SEQ - P])
        silu_gate = s.sb("silu_gate", [P, 8, SEQ])
        raw = s.sb("raw", [P, 2, TAPS - 1 + SEQ])
        x = s.sb("x", [P, 4, SEQ])
        x_dt = s.sb("x_dt", [P, 2, CH, P])
        x_end = s.sb("x_end", [P, 2, CH - 1, P])
        mix = s.sb("mix", [P, 4, 2, SEQ])
        state = s.sb("state", [P, 2, CH - 1, P])
        carried = s.sb("carried", [P, 4, SEQ - P])
        y = s.sb("y", [P, 4, SEQ])
        g = s.sb("g", [P, 2, SEQ])
        gate_ps = s.ps("gate_ps", [P, SEQ])
        x_ps = s.ps("x_ps", [P, SEQ])
        turn_ps = s.ps("turn_ps", [P, CH, P])
        state_ps = s.ps("state_ps", [P, CH, P])
        inner_ps = s.ps("inner_ps", [P, 2, SEQ])
        outer_ps = s.ps("outer_ps", [P, 2, SEQ])
        w_loaded, vec_loaded = s.sem("w_loaded"), s.sem("vec_loaded")
        w_hi_done, w_lo_done = s.sem("w_hi_done"), s.sem("w_lo_done")
        row_loaded = [s.sem(f"row_loaded{q}") for q in range(2)]
        ell_loaded = [s.sem(f"ell_loaded{q}") for q in range(4)]
        times_done, pad_done = s.sem("times_done"), s.sem("pad_done")
        gate_mm, x_mm, turn_mm, state_mm, y_mm = (s.sem("gate_mm"), s.sem("x_mm"), s.sem("turn_mm"),
                                                  s.sem("state_mm"), s.sem("y_mm"))
        gate_done, raw_done, conv_step, x_done = (s.sem("gate_done"), s.sem("raw_done"),
                                                  s.sem("conv_step"), s.sem("x_done"))
        ell_exp_done, diff_exp_done = s.sem("ell_exp_done"), s.sem("diff_exp_done")
        x_dt_done, x_end_done, diff_done = s.sem("x_dt_done"), s.sem("x_end_done"), s.sem("diff_done")
        mix_done, state_step, y_step = s.sem("mix_done"), s.sem("state_step"), s.sem("y_step")
        y_done, g_done = s.sem("y_done"), s.sem("g_done")
        g_stored = [s.sem(f"g_stored{q}") for q in range(2)]
        block = s.block()

        def missing(i, r):
            return opening(i, r, 0) or (isinstance(i, int) and i == LAST and r >= STEPS)

        def nth(i, r, ring=1):
            return i * (STEPS // ring) + r // ring + 1

        def pair_of(i, r):
            return i * 2 + r // B

        def ell_rows(sync, i, r):
            rows, b = row_of(sync, m.ell_dram, pair_of(i, r)), r % B
            return rows.rearrange("(o h t) -> o h t", o=1, h=2)[:, :, b * SEQ:(b + 1) * SEQ]

        @block.sync
        def _(sync):
            def load_weights(i, r):
                pair = pair_of(i, r)
                weights = row_of(sync, m.w_gate_x, pair)
                if not opening(i, r, 2 * B):
                    sync.wait_ge(w_lo_done, pair - 1)
                sync.dma_start(w_raw[:, :, :, :].rearrange("p k c n -> p (k c n)"),
                               weights.rearrange("(p n) -> p n", p=P)).then_inc(w_loaded, 16)

            def load_vectors(i, r):
                q, vectors = (r // B) % 2, row_of(sync, m.pair_vec, pair_of(i, r))
                if not opening(i, r, 2 * B):
                    sync.wait_ge(y_step, nth(i, r - B - 1) * 2)
                sync.dma_start(vec[:, q], vectors.rearrange("(p n) -> p n", p=P)).then_inc(
                    vec_loaded, 16)

            def load_row(i, r):
                if missing(i, r):
                    return
                rows = ell_rows(sync, i, r)
                if not opening(i, r, 2):
                    sync.wait_ge(diff_done, nth(i, r - 2))
                sync.dma_start(ell_row[:, r % 2], rows.broadcast_to([P, 2, SEQ])).then_inc(
                    row_loaded[r % 2], 16)

            def load_ell(i, r):
                if missing(i, r):
                    return
                rows = ell_rows(sync, i, r)
                if not opening(i, r, 4):
                    sync.wait_ge(y_step, nth(i, r - 4) * 2)
                for h in range(2):
                    sync.dma_start(ell_exp[h * HEAD_P:(h + 1) * HEAD_P, r % 4],
                                   rows[:, h, P:SEQ].broadcast_to([HEAD_P, SEQ - P])).then_inc(
                        ell_loaded[r % 4], 16)

            def body(i, r):
                load_ell(i, r)
                load_row(i, r + 2)
                if r % B == 1 and not missing(i, r + B - 1):
                    load_weights(i, r + B - 1)
                if r % B == 2 and not missing(i, r + B - 2):
                    load_vectors(i, r + B - 2)
                if not missing(i, r - 4):
                    q, b = r % 2, r % B
                    mixed = row_of(sync, m.mixed_dram, pair_of(i, r - 4)).rearrange("(p t) -> p t", p=P)
                    sync.wait_ge(g_done, nth(i, r - 4))
                    sync.dma_start(mixed[:, b * SEQ:(b + 1) * SEQ], g[:, q]).then_inc(g_stored[q], 16)

            load_vectors(0, 0)
            load_row(0, 0)
            load_row(0, 1)
            each_unit(sync, body, UNITS, STEPS, 4, TAIL)
            for q in range(2):
                sync.wait_ge(g_stored[q], 16 * UNITS // 2)

        @block.tensor
        def _(pe):
            def project(i, r, kind, out):
                q, b = (r // B) % 2, r % B
                if b == 0 and not opening(i, r, 1):
                    pe.wait_ge(w_lo_done, pair_of(i, r))
                return three_passes(pe, out, lambda k: [x[:, q, k, kind] for x in (w_hi, w_lo)],
                                    lambda k: [x[:, k, b * SEQ:(b + 1) * SEQ]
                                               for x in (m.xn_hi, m.xn_lo)], range(KD))

            def outputs(i, r):
                b, q = r % B, r % 2
                pe.wait_ge(mix_done, nth(i, r))
                pe.wait_ge(x_dt_done, nth(i, r))
                pe.wait_ge(state_step, nth(i, r) * 5)
                if not opening(i, r, 2):
                    pe.wait_ge(y_step, nth(i, r - 2) * 2)
                for c in range(CH):
                    for h in range(2):
                        pe.matmul(inner_ps[h * HEAD_P:(h + 1) * HEAD_P, q, c * P:(c + 1) * P],
                                  x_dt[:, q, c, h * HEAD_P:(h + 1) * HEAD_P],
                                  mix[:, r % 4, h, c * P:(c + 1) * P], start=True, stop=True)
                for c in range(1, CH):
                    end = pe.matmul(outer_ps[:, q, c * P:(c + 1) * P], state[:, q, c - 1],
                                    m.c_fm[:, (CH * b + c) * P:(CH * b + c + 1) * P],
                                    start=True, stop=True)
                end.then_inc(y_mm, 1)

            def body(i, r):
                if not missing(i, r):
                    if not opening(i, r, 1):
                        pe.wait_ge(gate_done, nth(i, r - 1))
                    project(i, r, 0, gate_ps[:, :]).then_inc(gate_mm, 1)
                    if not opening(i, r, 1):
                        pe.wait_ge(raw_done, nth(i, r - 1))
                    project(i, r, 1, x_ps[:, :]).then_inc(x_mm, 1)
                if not missing(i, r - 1):
                    pe.wait_ge(x_done, nth(i, r - 1))
                    if not opening(i, r, 2):
                        pe.wait_ge(x_end_done, nth(i, r - 2))
                    for c in range(CH):
                        end = pe.transpose(turn_ps[:, c], x[:, (r - 1) % 4, c * P:(c + 1) * P],
                                           m.ident[:, :])
                    end.then_inc(turn_mm, 1)
                if not missing(i, r - 2):
                    outputs(i, r - 2)
                if not missing(i, r - 1):
                    b, q = (r - 1) % B, (r - 1) % 2
                    pe.wait_ge(x_end_done, nth(i, r - 1))
                    if not opening(i, r, 2):
                        pe.wait_ge(state_step, nth(i, r - 2) * 5)
                    for c in range(CH - 1):
                        end = pe.matmul(state_ps[:, c], m.b_tm[:, CH * b + c], x_end[:, q, c],
                                        start=True, stop=True)
                    end.then_inc(state_mm, 1)

            each_unit(pe, body, UNITS, STEPS, LEAD, TAIL)

        @block.scalar
        def _(act):
            def round_weights(i, r):
                q = (r // B) % 2
                act.wait_ge(w_loaded, 16 * pair_of(i, r))
                if not opening(i, r, 2 * B):
                    act.wait_ge(x_mm, nth(i, r - B - 1))
                act.activation(w_hi[:, q], w_raw[:, :, :, :], ACT.Copy).then_inc(w_hi_done, 1)

            def diff_exp(i, r):
                if missing(i, r):
                    return
                act.wait_ge(diff_done, nth(i, r))
                act.activation(mix[:, r % 4], mix[:, r % 4], ACT.Exp).then_inc(diff_exp_done, 1)

            def ell_exps(i, r):
                if missing(i, r):
                    return
                act.wait_ge(ell_loaded[r % 4], 32 * nth(i, r, 4))
                act.activation(ell_exp[:, r % 4], ell_exp[:, r % 4], ACT.Exp).then_inc(ell_exp_done, 1)

            def body(i, r):
                if not missing(i, r):
                    act.wait_ge(gate_mm, nth(i, r))
                    if not opening(i, r, 6):
                        act.wait_ge(g_done, nth(i, r - 6))
                    act.activation(silu_gate[:, r % 8], gate_ps[:, :], ACT.Silu).then_inc(gate_done, 1)
                    act.wait_ge(x_mm, nth(i, r))
                    if not opening(i, r, 2):
                        act.wait_ge(conv_step, nth(i, r - 2) * 4)
                    act.activation(raw[:, r % 2, TAPS - 1:], x_ps[:, :], ACT.Copy).then_inc(raw_done, 1)
                if r % 2 == 0:
                    diff_exp(i, r - 1)
                    diff_exp(i, r)
                    ell_exps(i, r - 1)
                    ell_exps(i, r)
                if not missing(i, r):
                    act.wait_ge(conv_step, nth(i, r) * 4)
                    act.activation(x[:, r % 4], x[:, r % 4], ACT.Silu).then_inc(x_done, 1)
                if r % B == 2 and not missing(i, r + B - 2):
                    round_weights(i, r + B - 2)

            act.wait_ge(pad_done, 1)
            each_unit(act, body, UNITS, STEPS, LEAD, TAIL)

        @block.vector
        def _(dve):
            def take_times(i, r):
                q, pair = (r // B) % 2, pair_of(i, r)
                dve.tensor_copy(times[:, q].rearrange("p a t h -> p (a t) h"),
                                m.times_tm[:, :, bass.ds(pair * 2, 2)]).then_inc(times_done, 1)
                dve.tensor_copy(decay[:, q], m.chunk_decay[:, bass.ds(pair * 2, 2), :]).then_inc(
                    times_done, 1)

            def outputs(i, r):
                if missing(i, r):
                    return
                q, pq = r % 2, (r // B) % 2
                dve.wait_ge(y_mm, nth(i, r))
                if not opening(i, r, 3):
                    dve.wait_ge(g_done, nth(i, r - 3))
                dve.scalar_tensor_tensor(out=y[:, r % 4], in0=x[:, r % 4], scalar=vec[:, pq, 5:6],
                                         in1=inner_ps[:, q], op0=ALU.mult, op1=ALU.add).then_inc(y_step, 1)
                dve.wait_ge(ell_exp_done, nth(i, r))
                dve.tensor_tensor(carried[:, r % 4], outer_ps[:, q, P:SEQ], ell_exp[:, r % 4],
                                  ALU.mult).then_inc(y_step, 1)

            def differences(i, r):
                if missing(i, r):
                    return
                b, q, pq = r % B, r % 2, (r // B) % 2
                if b == 0:
                    take_times(i, r)
                dve.wait_ge(row_loaded[q], 16 * nth(i, r, 2))
                dve.wait_ge(times_done, 2 * (pair_of(i, r) + 1))
                if not opening(i, r, 4):
                    dve.wait_ge(y_mm, nth(i, r - 4))
                for h in range(2):
                    for c in range(CH):
                        cols, t = slice(c * P, (c + 1) * P), CH * b + c
                        end = dve.tensor_scalar(mix[:, r % 4, h, cols], ell_row[:, q, h, cols],
                                                times[:, pq, 2, t, h:h + 1], 0.0,
                                                ALU.subtract, ALU.min)
                end.then_inc(diff_done, 1)

            def weigh(i, r):
                if missing(i, r):
                    return
                b, q, pq = r % B, r % 2, (r // B) % 2
                dve.wait_ge(turn_mm, nth(i, r))
                if not opening(i, r, 2):
                    dve.wait_ge(y_mm, nth(i, r - 2))
                for out, done, n, cs in ((x_end, x_end_done, 1, CH - 1), (x_dt, x_dt_done, 0, CH)):
                    dve.tensor_tensor(
                        out[:, q].rearrange("p c (h e) -> p c h e", h=2),
                        turn_ps[:, 0:cs].rearrange("p c (h e) -> p c h e", h=2),
                        times[:, pq, n, CH * b:CH * b + cs].rearrange(
                            "p c (h o) -> p c h o", o=1).broadcast_to([P, cs, 2, HEAD_P]),
                        ALU.mult).then_inc(done, 1)

            def convolve(i, r):
                if missing(i, r):
                    return
                q, pq = r % 2, (r // B) % 2
                if r % B == 0:
                    dve.wait_ge(vec_loaded, 16 * (pair_of(i, r) + 1))
                dve.wait_ge(raw_done, nth(i, r))
                if not opening(i, r, 4):
                    dve.wait_ge(turn_mm, nth(i, r - 4))
                dve.tensor_scalar(x[:, r % 4], raw[:, q, 0:SEQ], vec[:, pq, 0:1],
                                  vec[:, pq, TAPS:TAPS + 1], ALU.mult, ALU.add).then_inc(conv_step, 1)
                for j in range(1, TAPS):
                    dve.wait_ge(conv_step, nth(i, r) * 4 - 4 + j)
                    dve.scalar_tensor_tensor(out=x[:, r % 4], in0=raw[:, q, j:j + SEQ],
                                             scalar=vec[:, pq, j:j + 1], in1=x[:, r % 4],
                                             op0=ALU.mult, op1=ALU.add).then_inc(conv_step, 1)

            def states(i, r):
                if missing(i, r):
                    return
                b, q, pq = r % B, r % 2, (r // B) % 2
                dve.wait_ge(state_mm, nth(i, r))
                if not opening(i, r, 2):
                    dve.wait_ge(y_mm, nth(i, r - 2))
                dve.tensor_copy(state[:, q, 0], state_ps[:, 0]).then_inc(state_step, 1)
                for c in range(1, CH - 1):
                    dve.wait_ge(state_step, nth(i, r) * 5 - 6 + 2 * c)
                    for h in range(2):
                        cols = slice(h * HEAD_P, (h + 1) * HEAD_P)
                        dve.scalar_tensor_tensor(
                            out=state[:, q, c, cols], in0=state[:, q, c - 1, cols],
                            scalar=decay[:, pq, h, CH * b + c:CH * b + c + 1],
                            in1=state_ps[:, c, cols], op0=ALU.mult, op1=ALU.add).then_inc(state_step, 1)

            def body(i, r):
                outputs(i, r - 3)
                differences(i, r + 1)
                weigh(i, r - 1)
                convolve(i, r)
                states(i, r - 1)

            dve.memset(raw[:, :, 0:TAPS - 1], 0.0).then_inc(pad_done, 1)
            differences(0, 0)
            each_unit(dve, body, UNITS, STEPS, LEAD, TAIL)

        @block.gpsimd
        def _(pool):
            def keep_lo(i, r):
                q = (r // B) % 2
                pool.wait_ge(w_hi_done, pair_of(i, r))
                pool.tensor_tensor(w_lo[:, q], w_raw[:, :, :, :], w_hi[:, q].bitcast(F32),
                                   ALU.subtract).then_inc(w_lo_done, 1)

            def weigh(i, r):
                if missing(i, r):
                    return
                b = r % B
                pool.wait_ge(diff_exp_done, nth(i, r))
                cells = mix[:, r % 4].rearrange("p h (c t) -> p h c t", c=CH)
                pool.tensor_tensor(cells, cells, m.cb[:, CH * b:CH * (b + 1)].rearrange(
                    "p (o c) t -> p o c t", o=1).broadcast_to([P, 2, CH, P]), ALU.mult).then_inc(mix_done, 1)

            def body(i, r):
                if r % B == 3 and not missing(i, r + 1):
                    keep_lo(i, r + 1)
                if not missing(i, r - 4):
                    q, y_q = r % 2, r % 4
                    pool.wait_ge(y_step, nth(i, r - 4) * 2)
                    pool.tensor_tensor(y[:, y_q, P:SEQ], y[:, y_q, P:SEQ], carried[:, y_q],
                                       ALU.add).then_inc(y_done, 1)
                    pool.wait_ge(y_done, nth(i, r - 4))
                    if not opening(i, r, 6):
                        pool.wait_ge(g_stored[q], 16 * nth(i, r - 6, 2))
                    pool.tensor_tensor(g[:, q], y[:, y_q], silu_gate[:, (r - 4) % 8], ALU.mult).then_inc(g_done, 1)
                if r % 2 == 0:
                    weigh(i, r - 1)
                    weigh(i, r)

            each_unit(pool, body, UNITS, STEPS, LEAD, TAIL)


def ssm_output(nc, m):
    STEPS, LEAD, TAIL = 4, 3, 2
    LAST = TILES // STEPS - 1
    with Scope(nc, "ssm_out") as s:
        w_out = [s.sb(f"w_{x}", [P, KI, D], F32R) for x in ("hi", "lo")]
        rows = s.sb("rows", [P, 6, D])
        gated, x1, xn = rows[:, 0:2], rows[:, 2:4], rows[:, 4:6]
        w = split_weights(s, "w", [(m.w_out[k], w_out[0][:, k], w_out[1][:, k], m.norm_w[:, k:k + 1])
                                   for k in range(KI)], D, 6, rows)
        ones = s.sb("ones", [P, 2])
        mean_sq, rms, inv_rms = (s.sb(n, [P, 2, 1]) for n in ("mean_sq", "rms", "inv_rms"))
        mixed = s.sb("mixed", [P, 2, KI, P])
        hi, lo = s.sb("mixed_hi", [P, 2, KI, P], F32R), s.sb("mixed_lo", [P, 2, KI, P], F32R)
        square_sum = s.sb("square_sum", [P, 2, P])
        x, gate = s.sb("x", [P, 2, D]), s.sb("gate", [P, 2, D])
        stats, mv = s.sb("stats", [P, 2, 6]), s.sb("mean_var", [P, 2, 2])
        var_eps, std, rstd = (s.sb(n, [P, 2, 1]) for n in ("var_eps", "std", "rstd"))
        out_ps = s.ps("out_ps", [P, 2, D])
        sq_ps = s.ps("sq_ps", [P, 2, 512])
        turned = s.ps("turned", [P, 2, KD, P])
        ones_done, square_done, square_sum_done, mean_done, rms_done, inv_done = (
            s.sem(n) for n in ("ones_done", "square_done", "square_sum_done", "mean_done",
                               "rms_done", "inv_done"))
        mixed_loaded = [s.sem(f"mixed_loaded{q}") for q in range(2)]
        rows_loaded = [s.sem(f"rows_loaded{q}") for q in range(2)]
        hi_done, lo_done, out_mm, gated_done, x1_done = (
            s.sem(n) for n in ("hi_done", "lo_done", "out_mm", "gated_done", "x1_done"))
        stats_done, var_done, eps_done, std_done, rstd_done, xn_done, turned_done, xn_hi_done, xn_lo_done = (
            s.sem(n) for n in ("stats_done", "var_done", "eps_done", "std_done", "rstd_done",
                               "xn_done", "turned_done", "xn_hi_done", "xn_lo_done"))
        x1_stored = [s.sem(f"x1_stored{q}") for q in range(2)]
        block = s.block()
        x_t, gate_t, x1_t = (d.rearrange("(n p) d -> n p d", p=P) for d in (m.x, m.gate_dram, m.x1_dram))
        mixed_p = m.mixed_dram.rearrange("k p t -> p k t")
        PARTS = [slice(a, a + KI // 4) for a in range(0, KI, KI // 4)]
        part_loaded = [s.sem(f"part_loaded{a}") for a in range(3)] + [mixed_loaded[0]]
        part_hi_done, part_lo_done = s.sem("part_hi_done"), s.sem("part_lo_done")

        def missing(i, r):
            return opening(i, r, 0) or (isinstance(i, int) and i == LAST and r >= STEPS)

        def nth(i, r, ring=1):
            return i * (STEPS // ring) + r // ring + 1

        def tokens_of(i, r):
            return bass.ds((i * STEPS + r) * P, P)

        @block.sync
        def _(sync):
            def load(i, r):
                q, tokens = r % 2, columns_of(sync, i * STEPS + r, P)
                if not opening(i, r, 2):
                    sync.wait_ge(square_sum_done, nth(i, r - 2))
                sync.dma_start(mixed[:, q], mixed_p[:, :, tokens]).then_inc(mixed_loaded[q], 16)

            def load_rows(i, r):
                q = r % 2
                for tile, source in ((x, x_t), (gate, gate_t)):
                    rows = row_of(sync, source, i * STEPS + r).rearrange("(p d) -> p d", p=P)
                    sync.dma_start(tile[:, q], rows).then_inc(rows_loaded[q], 16)

            def body(i, r):
                if not missing(i, r + 2):
                    load(i, r + 2)
                if not missing(i, r - 1):
                    rows = row_of(sync, x1_t, i * STEPS + r - 1).rearrange("(p d) -> p d", p=P)
                    sync.wait_ge(x1_done, nth(i, r - 1))
                    sync.dma_start(rows, x1[:, (r - 1) % 2]).then_inc(x1_stored[(r - 1) % 2], 16)
                    if not missing(i, r + 1):
                        load_rows(i, r + 1)

            for a, part in enumerate(PARTS):
                sync.dma_start(mixed[:, 0, part], mixed_p[:, part, 0:P]).then_inc(part_loaded[a], 16)
                for n in range(part.start, part.stop):
                    w.load(sync, n)
                if a == 1:
                    load(0, 1)
            load_rows(0, 0)
            load_rows(0, 1)
            each_unit(sync, body, TILES, STEPS, 2, TAIL)
            for q in range(2):
                sync.wait_ge(x1_stored[q], 16 * TILES // 2)

        @block.tensor
        def _(pe):
            def turn(i, r):
                if missing(i, r):
                    return
                q = r % 2
                pe.wait_ge(xn_done, nth(i, r))
                if not opening(i, r, 2):
                    pe.wait_ge(xn_lo_done, nth(i, r - 2))
                for k in range(KD):
                    end = pe.transpose(turned[:, q, k], xn[:, q, k * P:(k + 1) * P], m.ident[:, :])
                end.then_inc(turned_done, 1)

            def product(i, r):
                if missing(i, r):
                    return
                q = r % 2
                if not opening(i, r, 1):
                    pe.wait_ge(lo_done, nth(i, r))
                if not opening(i, r, 2):
                    pe.wait_ge(gated_done, nth(i, r - 2))
                for k in range(KI):
                    if opening(i, r, 1):
                        pe.wait_ge(w.done, k + 1)
                        if k < PARTS[-1].start:
                            pe.wait_ge(part_lo_done, k // 4 + 1)
                        else:
                            pe.wait_ge(lo_done, 1)
                    three_passes(pe, out_ps[:, q], lambda k: (hi[:, q, k], lo[:, q, k]),
                                 lambda k: [x[:, k] for x in w_out], [k],
                                 first=k == 0, last=k == KI - 1)
                pe.wait_ge(square_sum_done, nth(i, r))
                pe.matmul(sq_ps[:, q, 0:2], square_sum[:, q], ones[:, :], start=True,
                          stop=True).then_inc(out_mm, 1)

            def body(i, r):
                product(i, r)
                turn(i, r - 1)

            pe.wait_ge(ones_done, 1)
            each_unit(pe, body, TILES, STEPS, LEAD, TAIL)

        @block.scalar
        def _(act):
            def split(i, r):
                q = r % 2
                act.wait_ge(mixed_loaded[q], 16 * nth(i, r, 2))
                if not opening(i, r, 2):
                    act.wait_ge(out_mm, nth(i, r - 2))
                act.activation(hi[:, q], mixed[:, q], ACT.Copy).then_inc(hi_done, 1)

            def squares(i, r):
                act.wait_ge(lo_done, nth(i, r))
                act.activation(mixed[:, r % 2], mixed[:, r % 2], ACT.Square).then_inc(square_done, 1)

            def body(i, r):
                if not missing(i, r + 1) and not opening(i, r, 1):
                    split(i, r + 1)
                q = (r - 1) % 2
                if not missing(i, r - 1):
                    act.wait_ge(mean_done, nth(i, r - 1))
                    act.activation(rms[:, q], mean_sq[:, q], ACT.Sqrt).then_inc(rms_done, 1)
                if not missing(i, r - 2):
                    act.wait_ge(turned_done, nth(i, r - 2))
                    act.activation(m.xn_hi[:, :, tokens_of(i, r - 2)], turned[:, r % 2],
                                   ACT.Copy).then_inc(xn_hi_done, 1)
                if not missing(i, r - 1):
                    act.wait_ge(eps_done, nth(i, r - 1))
                    act.activation(std[:, q], var_eps[:, q], ACT.Sqrt).then_inc(std_done, 1)
                if not missing(i, r + 1):
                    squares(i, r + 1)

            for a, part in enumerate(PARTS):
                act.wait_ge(part_loaded[a], 16)
                act.activation(hi[:, 0, part], mixed[:, 0, part], ACT.Copy).then_inc(
                    part_hi_done if a < 3 else hi_done, 1)
                for n in range(part.start, part.stop):
                    w.round_hi(act, n)
            split(0, 1)
            squares(0, 0)
            each_unit(act, body, TILES, STEPS, LEAD, TAIL)

        @block.vector
        def _(dve):
            def split(i, r):
                q = r % 2
                dve.wait_ge(hi_done, nth(i, r))
                dve.tensor_tensor(lo[:, q], mixed[:, q], hi[:, q].bitcast(F32),
                                  ALU.subtract).then_inc(lo_done, 1)

            def sum_squares(i, r):
                dve.wait_ge(square_done, nth(i, r))
                dve.tensor_reduce(square_sum[:, r % 2], mixed[:, r % 2].rearrange("p k t -> p t k"),
                                  AX.X, ALU.add).then_inc(square_sum_done, 1)

            def mean(i, r):
                q = r % 2
                dve.wait_ge(out_mm, nth(i, r))
                dve.tensor_scalar(mean_sq[:, q], sq_ps[:, q, 0:1], 1.0 / INTER, LN_EPS, ALU.mult,
                                  ALU.add).then_inc(mean_done, 1)

            def finish(i, r):
                q = r % 2
                dve.wait_ge(rms_done, nth(i, r))
                dve.reciprocal(inv_rms[:, q], rms[:, q]).then_inc(inv_done, 1)
                wait_all(dve, (inv_done, nth(i, r)), (rows_loaded[q], 32 * nth(i, r, 2)),
                         *[(x1_stored[q], 16 * nth(i, r - 2, 2))][:not opening(i, r, 2)])
                dve.scalar_tensor_tensor(out=gated[:, q], in0=out_ps[:, q],
                                         scalar=inv_rms[:, q], in1=gate[:, q],
                                         op0=ALU.mult, op1=ALU.mult).then_inc(gated_done, 1)
                dve.wait_ge(gated_done, nth(i, r))
                dve.tensor_tensor(x1[:, q], gated[:, q], x[:, q], ALU.add).then_inc(x1_done, 1)

            def normalize(i, r):
                q = r % 2
                dve.wait_ge(x1_done, nth(i, r))
                dve.bn_stats(stats[:, q], x1[:, q]).then_inc(stats_done, 1)
                keep_xn_lo(i, r - 1, (stats_done, nth(i, r)))
                dve.bn_aggr(mv[:, q], stats[:, q]).then_inc(var_done, 1)
                dve.wait_ge(var_done, nth(i, r))
                dve.tensor_scalar(var_eps[:, q], mv[:, q, 1:2], LN_EPS, None, ALU.add).then_inc(eps_done, 1)
                dve.wait_ge(std_done, nth(i, r))
                dve.reciprocal(rstd[:, q], std[:, q]).then_inc(rstd_done, 1)
                wait_all(dve, (rstd_done, nth(i, r)),
                         *[(turned_done, nth(i, r - 2))][:not opening(i, r, 2)])
                dve.tensor_scalar(xn[:, q], x1[:, q], mv[:, q, 0:1], rstd[:, q, 0:1],
                                  ALU.subtract, ALU.mult).then_inc(xn_done, 1)

            def keep_xn_lo(i, r, *also):
                wait_all(dve, *[(xn_hi_done, nth(i, r))][:not missing(i, r)], *also)
                if missing(i, r):
                    return
                dve.tensor_tensor(m.xn_lo[:, :, tokens_of(i, r)], turned[:, r % 2],
                                  m.xn_hi[:, :, tokens_of(i, r)].bitcast(F32),
                                  ALU.subtract).then_inc(xn_lo_done, 1)

            def body(i, r):
                if not missing(i, r + 1) and not opening(i, r, 1):
                    split(i, r + 1)
                if missing(i, r - 1):
                    keep_xn_lo(i, r - 2)
                else:
                    mean(i, r - 1)
                    finish(i, r - 1)
                    normalize(i, r - 1)
                if not missing(i, r + 1):
                    sum_squares(i, r + 1)

            dve.memset(ones[:, :], 1.0).then_inc(ones_done, 1)
            for a, part in enumerate(PARTS):
                if a < 3:
                    dve.wait_ge(part_hi_done, a + 1)
                else:
                    dve.wait_ge(hi_done, 1)
                dve.tensor_tensor(lo[:, 0, part], mixed[:, 0, part], hi[:, 0, part].bitcast(F32),
                                  ALU.subtract).then_inc(part_lo_done if a < 3 else lo_done, 1)
                for n in range(part.start, part.stop):
                    w.keep_lo(dve, n)
            split(0, 1)
            sum_squares(0, 0)
            each_unit(dve, body, TILES, STEPS, LEAD, TAIL)


def values_and_decays(nc, m):
    V0 = KV_HEADS
    COLS = KV_HEADS + KV_DIM + EXPERTS
    PARTS, RING = 4, 5
    W = (KV_DIM + EXPERTS) // PARTS
    GATE_OFFSET = 6.906768
    with Scope(nc, "values") as s:
        w_all = [s.sb(f"w_{x}", [P, KD, COLS], F32R) for x in ("hi", "lo")]
        w = split_weights(s, "w", [(m.w_gvr[k][:, cols], w_all[0][:, k, cols], w_all[1][:, k, cols], None)
                                   for cols in (slice(0, P), slice(P, COLS)) for k in range(KD)],
                          COLS - P)
        nxt = split_weights(s, "next", [first_piece(m.w_qqk, m.w_attention)], KD * 3 * P, 1)
        v, v_stored = m.values_out.rearrange("p q (a w) -> p q a w", a=PARTS), m.values_stored
        z, z_abs, z_exp, z_one, z_err = (
            s.sb(n, [KV_HEADS, TOK]) for n in ("z", "z_abs", "z_exp", "z_one", "z_err"))
        log_g, total, keep = z_abs, z_exp, z_one
        top8 = s.sb("top8", [P, TILES, 8])
        below, e2, rw = (s.sb(n, [P, TILES, 2]) for n in ("below", "e2", "rw"))
        esum, einv = s.sb("esum", [P, TILES, 1]), s.sb("einv", [P, TILES, 1])
        g_ps = s.ps("g_ps", [P, 2, SEQ])
        v_ps = s.ps("v_ps", [P, RING, 512])
        turn_ps = s.ps("turn_ps", [P, TILES, KV_HEADS])
        g_mm, z_done, abs_done, exp_done, one_done, log_done, err_done, log1p_done = (
            s.sem(n) for n in ("g_mm", "z_done", "abs_done", "exp_done", "one_done", "log_done",
                               "err_done", "log1p_done"))
        log_g_done, keep_done, total_done, turned, turned_read, total_stored = (
            s.sem(n) for n in ("log_g_done", "keep_done", "total_done", "turned", "turned_read",
                               "total_stored"))
        v_mm, v_read, top_done, below_done, e2_done, rw_step = (
            s.sem(n) for n in ("v_mm", "v_read", "top_done", "below_done", "e2_done", "rw_step"))
        block = s.block()
        values_t = m.values_dram.rearrange("(n p) d -> n p d", p=P)

        @block.sync
        def _(sync):
            for n in range(w.n):
                w.load(sync, n)
            nxt.load(sync, 0)
            for t in range(TILES):
                sync.wait_ge(v_read, PARTS * (t + 1))
                sync.dma_start(values_t[t], v[:, t % 2].rearrange("p a w -> p (a w)")[:, 0:KV_DIM]
                               ).then_inc(v_stored[t % 2], 16)
                if t == 1:
                    sync.wait_ge(total_done, 1)
                    sync.dma_start(m.log_gate_dram, total[:, :]).then_inc(total_stored, 16)
            sync.wait_ge(total_stored, 16)

        @block.tensor
        def _(pe):
            for b in range(B):
                if b >= 2:
                    pe.wait_ge(z_done, b - 1)
                for k in range(KD):
                    if b == 0:
                        pe.wait_ge(w.done, k + 1)
                    end = three_passes(pe, g_ps[:, b % 2], lambda k: [x[:, k, 0:P] for x in w_all],
                                       lambda k: [x[:, k, b * SEQ:(b + 1) * SEQ]
                                                  for x in (m.xn_hi, m.xn_lo)],
                                       [k], first=k == 0, last=k == KD - 1)
                end.then_inc(g_mm, 1)
            pe.wait_ge(w.done, w.n)
            for t in range(TILES):
                if t == TILES // 2:
                    pe.wait_ge(total_done, 1)
                    for n in range(TILES):
                        end = pe.transpose(turn_ps[:, n], total[:, n * P:(n + 1) * P],
                                           m.ident[0:KV_HEADS, 0:KV_HEADS])
                    end.then_inc(turned, 1)
                for a in range(PARTS):
                    n = PARTS * t + a
                    if n >= RING:
                        pe.wait_ge(v_read, n - RING + 1)
                    three_passes(pe, v_ps[:, n % RING, 0:W],
                                 lambda k: [x[:, k, t * P:(t + 1) * P] for x in (m.xn_hi, m.xn_lo)],
                                 lambda k: [x[:, k, V0 + a * W:V0 + (a + 1) * W] for x in w_all],
                                 range(KD)).then_inc(v_mm, 1)

        @block.scalar
        def _(act):
            for n in range(w.n):
                w.round_hi(act, n)
            nxt.round_hi(act, 0)
            act.wait_ge(z_done, B)
            act.activation(z_abs[:, :], z[:, :], ACT.Abs).then_inc(abs_done, 1)
            act.wait_ge(abs_done, 1)
            act.activation(z_exp[:, :], z_abs[:, :], ACT.Exp, scale=-1.0).then_inc(exp_done, 1)
            act.wait_ge(one_done, 1)
            act.activation(log_g[:, :], z_one[:, :], ACT.Ln).then_inc(log_done, 1)
            for t in range(TILES):
                if t >= 2:
                    act.wait_ge(v_stored[t % 2], 16 * (t // 2))
                    act.wait_ge(top_done, t - 1)
                for a in range(PARTS):
                    n = PARTS * t + a
                    act.wait_ge(v_mm, n + 1)
                    act.activation(v[:, t % 2, a], v_ps[:, n % RING, 0:W], ACT.Copy).then_inc(v_read, 1)
            act.wait_ge(turned, 1)
            act.activation(m.log_gate_tm[:, :, :].rearrange("p h t -> p t h"), turn_ps[:, :, :],
                           ACT.Copy).then_inc(turned_read, 1)
            act.wait_ge(below_done, 1)
            act.activation(e2[:, :, :], below[:, :, :], ACT.Exp).then_inc(e2_done, 1)
            act.wait_ge(turned_read, 1)

        @block.vector
        def _(dve):
            for k in range(KD):
                w.keep_lo(dve, k)
            for b in range(B):
                dve.wait_ge(g_mm, b + 1)
                dve.tensor_scalar(z[:, b * SEQ:(b + 1) * SEQ], g_ps[0:KV_HEADS, b % 2], GATE_OFFSET, None,
                                  ALU.add).then_inc(z_done, 1)
                w.keep_lo(dve, KD + b)
            dve.wait_ge(exp_done, 1)
            dve.tensor_scalar(z_one[:, :], z_exp[:, :], 1.0, None, ALU.add).then_inc(one_done, 1)
            dve.wait_ge(one_done, 1)
            dve.scalar_tensor_tensor(out=z_err[:, :], in0=z_one[:, :], scalar=1.0, in1=z_exp[:, :],
                                     op0=ALU.subtract, op1=ALU.subtract).then_inc(err_done, 1)
            wait_all(dve, (err_done, 1), (log_done, 1))
            dve.tensor_tensor(log_g[:, :], log_g[:, :], z_err[:, :], ALU.subtract).then_inc(log1p_done, 1)
            dve.memset(keep[:, :], 1.0).then_inc(keep_done, 1)
            dve.wait_ge(keep_done, 1)
            dve.memset(keep[:, :].rearrange("h (b t) -> h b t", b=B)[:, :, 0:1], 0.0).then_inc(keep_done, 1)
            dve.wait_ge(log1p_done, 1)
            dve.scalar_tensor_tensor(out=log_g[:, :], in0=z[:, :], scalar=0.0, in1=log_g[:, :],
                                     op0=ALU.min, op1=ALU.subtract).then_inc(log_g_done, 1)
            wait_all(dve, (log_g_done, 1), (keep_done, 2))
            dve.tensor_tensor_scan(total[:, :], keep[:, :], log_g[:, :], 0.0, ALU.mult,
                                   ALU.add).then_inc(total_done, 1)
            nxt.keep_lo(dve, 0)
            for t in range(TILES):
                dve.wait_ge(v_read, PARTS * (t + 1))
                dve.max(top8[:, t], v[:, t % 2, PARTS - 1, W - EXPERTS:W]).then_inc(top_done, 1)
            dve.wait_ge(top_done, TILES)
            dve.tensor_tensor(below[:, :, :], top8[:, :, 0:2],
                              top8[:, :, 0:1].broadcast_to([P, TILES, 2]), ALU.subtract).then_inc(below_done, 1)
            dve.wait_ge(e2_done, 1)
            dve.tensor_tensor(esum[:, :, :], e2[:, :, 0:1], e2[:, :, 1:2], ALU.add).then_inc(rw_step, 1)
            dve.wait_ge(rw_step, 1)
            dve.reciprocal(einv[:, :, :], esum[:, :, :]).then_inc(rw_step, 1)
            dve.wait_ge(rw_step, 2)
            dve.tensor_tensor(rw[:, :, :], e2[:, :, :], einv[:, :, :].broadcast_to([P, TILES, 2]),
                              ALU.mult).then_inc(rw_step, 1)
            dve.wait_ge(rw_step, 3)
            dve.tensor_tensor(m.comb_w[:, :].rearrange("p (t o) -> p t o", o=1), rw[:, :, 0:1],
                              rw[:, :, 1:2], ALU.add).then_inc(rw_step, 1)
            dve.wait_ge(rw_step, 4)


def power_attention(nc, m):
    STEPS, UNITS, LEAD, TAIL = 2 * B, KV_HEADS * B, 6, 2
    LAST = UNITS // STEPS - 1
    WIDTH = [SEQ - j * P for j in range(CH)]
    AT = [sum(WIDTH[:j]) for j in range(CH)]
    COLS = sum(WIDTH)
    SCORE_AT = [0, 512, 1024, 1280]
    VC = HEAD_D + 2
    SCALE = HEAD_D ** -0.5
    with Scope(nc, "attn") as s:
        w_raw = s.sb("w_raw", [P, KD, 3, P])
        w_hi, w_lo = m.w_attention
        nxt = split_weights(s, "next", [first_piece(m.w_gate_up, m.w_mlp)], KD * 2 * P, 1)
        gate_row = s.sb("gate_row", [P, 2, SEQ])
        gate_cols = s.sb("gate_cols", [P, 2, TILES])
        v = s.sb("v", [P, 2, CH, VC])
        qk_hi, qk_lo = s.sb("qk_hi", [P, 2, 3, SEQ], F32R), s.sb("qk_lo", [P, 2, 3, SEQ], F32R)
        decay = s.sb("decay", [P, 2, COLS])
        a = s.sb("a", [P, 2, COLS])
        norm, inv = s.sb("norm", [P, 2, CH]), s.sb("inv", [P, 2, CH])
        y, y_stored = m.attended_out, m.attended_stored
        proj_ps = s.ps("proj_ps", [P, 3, SEQ])
        score_ps = s.ps("score_ps", [P, 3 * 512])
        out_ps = s.ps("out_ps", [P, 2, 512])
        w_loaded, w_hi_done, w_lo_done = s.sem("w_loaded"), s.sem("w_hi_done"), s.sem("w_lo_done")
        rows_loaded = [s.sem(f"rows_loaded{q}") for q in range(2)]
        v_loaded = [s.sem(f"v_loaded{q}") for q in range(2)]
        ones_done, cols_done, proj_mm, qk_hi_done, qk_lo_done = (
            s.sem(n) for n in ("ones_done", "cols_done", "proj_mm", "qk_hi_done", "qk_lo_done"))
        score_mm, square_done, diff_done, decay_done, a_done = (
            s.sem(n) for n in ("score_mm", "square_done", "diff_done", "decay_done", "a_done"))
        out_mm, norm_done, inv_done, y_done = (
            s.sem(n) for n in ("out_mm", "norm_done", "inv_done", "y_done"))
        block = s.block()

        def missing(i, r):
            return opening(i, r, 0) or (isinstance(i, int) and i == LAST and r >= STEPS)

        def nth(i, r, ring=1):
            return i * (STEPS // ring) + r // ring + 1

        def head_of(i, r):
            return i * 2 + r // B

        @block.sync
        def _(sync):
            def load_weights(i, r):
                weights = row_of(sync, m.w_qqk, head_of(i, r)).rearrange("(p n) -> p n", p=P)
                wait_all(sync, *[(w_lo_done, head_of(i, r) - 1)][:not opening(i, r, 2 * B)])
                sync.dma_start(w_raw[:, :, :, :].rearrange("p k c n -> p (k c n)"),
                               weights).then_inc(w_loaded, 16)

            def body(i, r):
                b, q = r % B, r % 2
                if not missing(i, r):
                    row = row_of(sync, m.log_gate_dram, head_of(i, r))
                    values = m.values_dram.rearrange("(b c p) e -> b p c e", b=B, p=P)[
                        b][:, :, columns_of(sync, head_of(i, r), HEAD_D)]
                    if not opening(i, r, 2):
                        sync.wait_ge(diff_done, nth(i, r - 2))
                    sync.dma_start(gate_row[:, q], row.rearrange("(o t) -> o t", o=1)[
                        :, b * SEQ:(b + 1) * SEQ].broadcast_to([P, SEQ])).then_inc(rows_loaded[q], 16)
                    if not opening(i, r, 2):
                        sync.wait_ge(out_mm, 2 * nth(i, r - 2))
                    sync.dma_start(v[:, q, :, 0:HEAD_D], values).then_inc(v_loaded[q], 16)
                if r % B == 1 and not missing(i, r + B - 1):
                    load_weights(i, r + B - 1)
                if not missing(i, r - 2):
                    out = m.attended_dram.rearrange("(b c p) e -> b p c e", b=B, p=P)[
                        (r - 2) % B][:, :, columns_of(sync, head_of(i, r - 2), REP * HEAD_D)]
                    wait_all(sync, (y_done, 2 * nth(i, r - 2)))
                    sync.dma_start(out, y[:, q].rearrange("p c r e -> p c (r e)")).then_inc(
                        y_stored[q], 16)

            nxt.load(sync, 0)
            for q in range(2):
                sync.wait_ge(m.values_stored[q], 16 * TILES // 2)
            each_unit(sync, body, UNITS, STEPS, 4, TAIL)

        @block.tensor
        def _(pe):
            def project(i, r, kind):
                if missing(i, r):
                    return
                q, b = (r // B) % 2, r % B
                if b == 0 and kind == 0 and not opening(i, r, 1):
                    wait_all(pe, (w_lo_done, head_of(i, r)))
                if not opening(i, r, 1):
                    wait_all(pe, (qk_lo_done, 3 * nth(i, r) - 5 + kind))
                three_passes(pe, proj_ps[:, kind], lambda k: [x[:, q, k, kind] for x in (w_hi, w_lo)],
                             lambda k: [x[:, k, b * SEQ:(b + 1) * SEQ] for x in (m.xn_hi, m.xn_lo)],
                             range(KD)).then_inc(proj_mm, 1)

            def scores(i, r, h):
                if missing(i, r):
                    return
                q = r % 2
                wait_all(pe, (qk_lo_done, 3 * nth(i, r)),
                         *[(square_done, 2 * nth(i, r) - 2 + h)][:h or not opening(i, r, 1)])
                for j in range(CH - h):
                    heads = slice(h, h + 1) if j < CH - 1 else slice(0, REP)
                    width = WIDTH[j] * (heads.stop - heads.start)
                    end = three_passes(
                        pe, score_ps[:, SCORE_AT[j]:SCORE_AT[j] + width],
                        lambda _: [x[:, q, 2, j * P:(j + 1) * P] for x in (qk_hi, qk_lo)],
                        lambda _: [x[:, q, heads, j * P:SEQ] for x in (qk_hi, qk_lo)], [0])
                end.then_inc(score_mm, 1)

            def outputs(i, r, h):
                if missing(i, r):
                    return
                q = r % 2
                wait_all(pe, (a_done, 2 * nth(i, r) - 1 + h), (v_loaded[q], 16 * nth(i, r, 2)),
                         *[(y_done, 2 * nth(i, r) - 2 + h)][:h or not opening(i, r, 1)])
                for c in range(CH):
                    for j in range(c + 1):
                        at = AT[j] + (c - j) * P
                        end = pe.matmul(out_ps[:, c // 2, (c % 2) * VC:(c % 2 + 1) * VC],
                                        a[:, h, at:at + P], v[:, q, j], start=j == 0, stop=j == c)
                end.then_inc(out_mm, 1)

            def body(i, r):
                project(i, r, 0)
                scores(i, r - 1, 0)
                project(i, r, 1)
                outputs(i, r - 2, 1)
                scores(i, r - 1, 1)
                project(i, r, 2)
                outputs(i, r - 1, 0)

            pe.wait_ge(ones_done, 1)
            each_unit(pe, body, UNITS, STEPS, LEAD, TAIL)

        @block.scalar
        def _(act):
            def round_weights(i, r):
                q = (r // B) % 2
                wait_all(act, (w_loaded, 16 * head_of(i, r)),
                         *[(proj_mm, 3 * nth(i, r - B - 1))][:not opening(i, r, 2 * B)])
                act.activation(w_hi[:, q], w_raw[:, :, :, :], ACT.Copy).then_inc(w_hi_done, 1)

            def take(i, r, kind):
                if missing(i, r):
                    return
                wait_all(act, (proj_mm, 3 * nth(i, r) - 2 + kind),
                         *[(score_mm, 2 * nth(i, r - 2))][:not opening(i, r, 2)])
                act.activation(qk_hi[:, r % 2, kind], proj_ps[:, kind], ACT.Copy).then_inc(qk_hi_done, 1)

            def square(i, r, h):
                if missing(i, r):
                    return
                wait_all(act, (score_mm, 2 * nth(i, r) - 1 + h),
                         *[(out_mm, 2 * nth(i, r - 1) - 1 + h)][:not opening(i, r, 1)])
                last = SCORE_AT[3] + h * P
                pieces = [(AT[0], 0, AT[2]), (AT[2], SCORE_AT[2], WIDTH[2]), (AT[3], last, WIDTH[3])]
                if h == 0:
                    pieces[1:] = [(AT[2], SCORE_AT[2], WIDTH[2] + WIDTH[3])]
                for to, at, width in pieces:
                    end = act.activation(a[:, h, to:to + width], score_ps[:, at:at + width],
                                         ACT.Square, scale=SCALE)
                end.then_inc(square_done, 1)

            def body(i, r):
                take(i, r, 0)
                square(i, r - 1, 0)
                take(i, r, 1)
                square(i, r - 1, 1)
                take(i, r, 2)
                if not missing(i, r):
                    wait_all(act, (diff_done, nth(i, r)))
                    act.activation(decay[:, r % 2], decay[:, r % 2], ACT.Exp).then_inc(decay_done, 1)
                if r % B == 2 and not missing(i, r + B - 2):
                    round_weights(i, r + B - 2)

            each_unit(act, body, UNITS, STEPS, LEAD, TAIL)
            nxt.round_hi(act, 0)

        @block.vector
        def _(dve):
            def keep_lo(i, r):
                q = (r // B) % 2
                wait_all(dve, (w_hi_done, head_of(i, r)))
                dve.tensor_tensor(w_lo[:, q], w_raw[:, :, :, :], w_hi[:, q].bitcast(F32),
                                  ALU.subtract).then_inc(w_lo_done, 1)

            def take_columns(i, r):
                dve.tensor_copy(gate_cols[:, (r // B) % 2].rearrange("p (o t) -> p o t", o=1),
                                m.log_gate_tm[:, bass.ds(head_of(i, r), 1), :]).then_inc(cols_done, 1)

            def weigh(i, r, h):
                if missing(i, r):
                    return
                wait_all(dve, (square_done, 2 * nth(i, r) - 1 + h), (decay_done, nth(i, r)))
                dve.tensor_tensor(a[:, h], a[:, h], decay[:, r % 2], ALU.mult).then_inc(a_done, 1)

            def divide(i, r, h):
                if missing(i, r):
                    return
                q = r % 2
                n = 2 * nth(i, r) - 1 + h
                wait_all(dve, (out_mm, n), *[(y_stored[q], 16 * nth(i, r - 2, 2))][:not opening(i, r, 2)])
                heads = out_ps[:, :, 0:2 * VC].rearrange("p a (c e) -> p a c e", c=2)
                dve.tensor_scalar(norm[:, h].rearrange("p (a c) -> p a c", a=2), heads[:, :, :, HEAD_D],
                                  1e-6, None, ALU.add).then_inc(norm_done, 1)
                wait_all(dve, (norm_done, n))
                dve.reciprocal(inv[:, h], norm[:, h]).then_inc(inv_done, 1)
                wait_all(dve, (inv_done, n))
                dve.tensor_tensor(
                    y[:, q, :, h].rearrange("p (a c) e -> p a c e", a=2), heads[:, :, :, 0:HEAD_D],
                    inv[:, h].rearrange("p (a c o) -> p a c o", a=2, o=1).broadcast_to(
                        [P, 2, 2, HEAD_D]), ALU.mult).then_inc(y_done, 1)

            def keep_qk_lo(i, r, kind):
                if missing(i, r):
                    return
                wait_all(dve, (qk_hi_done, 3 * nth(i, r) - 2 + kind))
                dve.tensor_tensor(qk_lo[:, r % 2, kind], proj_ps[:, kind],
                                  qk_hi[:, r % 2, kind].bitcast(F32), ALU.subtract).then_inc(qk_lo_done, 1)

            def body(i, r):
                keep_qk_lo(i, r, 0)
                if not missing(i, r):
                    b, q = r % B, r % 2
                    if b == 0:
                        take_columns(i, r)
                    wait_all(dve, (rows_loaded[q], 16 * nth(i, r, 2)), (cols_done, head_of(i, r) + 1))
                    for j in range(CH):
                        col = gate_cols[:, (r // B) % 2, CH * b + j:CH * b + j + 1]
                        end = dve.scalar_tensor_tensor(
                            out=decay[:, q, AT[j]:AT[j] + P], in0=gate_row[:, q, j * P:(j + 1) * P],
                            scalar=col, in1=m.never[:, :], op0=ALU.subtract, op1=ALU.min)
                        if j < CH - 1:
                            end = dve.tensor_scalar(
                                decay[:, q, AT[j] + P:AT[j] + WIDTH[j]], gate_row[:, q, (j + 1) * P:SEQ],
                                col, 0.0, ALU.subtract, ALU.min)
                    end.then_inc(diff_done, 1)
                weigh(i, r - 1, 0)
                divide(i, r - 2, 1)
                keep_qk_lo(i, r, 1)
                weigh(i, r - 1, 1)
                keep_qk_lo(i, r, 2)
                divide(i, r - 1, 0)
                if r % B == 2 and not missing(i, r + B - 2):
                    keep_lo(i, r + B - 2)

            dve.memset(v[:, :, :, HEAD_D:VC], 1.0).then_inc(ones_done, 1)
            each_unit(dve, body, UNITS, STEPS, LEAD, TAIL)
            nxt.keep_lo(dve, 0)


def mlp_up(nc, m):
    STEPS, UNITS, LEAD, TAIL = 2 * B, BLOCKS * B, 6, 2
    LAST = UNITS // STEPS - 1
    with Scope(nc, "mlp_up") as s:
        w_raw = s.sb("w_raw", [P, KD, 2, P])
        w_hi, w_lo = m.w_mlp
        silu_gate, hidden = s.sb("silu_gate", [P, 2, SEQ]), s.sb("hidden", [P, 2, SEQ])
        gate_ps, up_ps = s.ps("gate_ps", [P, 2, SEQ]), s.ps("up_ps", [P, 2, SEQ])
        w_loaded, w_hi_done, w_lo_done, gate_mm, up_mm, gate_done, hidden_done = (
            s.sem(n) for n in ("w_loaded", "w_hi_done", "w_lo_done", "gate_mm", "up_mm", "gate_done",
                               "hidden_done"))
        stored = [s.sem(f"stored{q}") for q in range(2)]
        block = s.block()

        def missing(i, r):
            return opening(i, r, 0) or (isinstance(i, int) and i == LAST and r >= STEPS)

        def nth(i, r, ring=1):
            return i * (STEPS // ring) + r // ring + 1

        def block_of(i, r):
            return i * 2 + r // B

        @block.sync
        def _(sync):
            def load_weights(i, r):
                weights = row_of(sync, m.w_gate_up, block_of(i, r)).rearrange("(p n) -> p n", p=P)
                wait_all(sync, *[(w_lo_done, block_of(i, r) - 1)][:not opening(i, r, 2 * B)])
                sync.dma_start(w_raw[:, :, :, :].rearrange("p k c n -> p (k c n)"),
                               weights).then_inc(w_loaded, 16)

            def body(i, r):
                if r % B == 1 and not missing(i, r + B - 1):
                    load_weights(i, r + B - 1)
                if not missing(i, r - 1):
                    q, b = (r - 1) % 2, (r - 1) % B
                    out = row_of(sync, m.hidden_dram, block_of(i, r - 1)).rearrange("(p t) -> p t", p=P)
                    wait_all(sync, (hidden_done, nth(i, r - 1)))
                    sync.dma_start(out[:, b * SEQ:(b + 1) * SEQ], hidden[:, q]).then_inc(stored[q], 16)

            each_unit(sync, body, UNITS, STEPS, 4, TAIL)
            for q in range(2):
                sync.wait_ge(stored[q], 16 * UNITS // 2)
                sync.wait_ge(m.attended_stored[q], 16 * KV_HEADS * B // 2)

        @block.tensor
        def _(pe):
            def body(i, r):
                if missing(i, r):
                    return
                q, w_q, b = r % 2, (r // B) % 2, r % B
                if b == 0 and not opening(i, r, 1):
                    wait_all(pe, (w_lo_done, block_of(i, r)))
                for kind, (ps, mm) in enumerate(((gate_ps, gate_mm), (up_ps, up_mm))):
                    if kind == 0 and not opening(i, r, 2):
                        wait_all(pe, (hidden_done, nth(i, r - 2)))
                    three_passes(pe, ps[:, q], lambda k: [x[:, w_q, k, kind] for x in (w_hi, w_lo)],
                                 lambda k: [x[:, k, b * SEQ:(b + 1) * SEQ] for x in (m.xn_hi, m.xn_lo)],
                                 range(KD)).then_inc(mm, 1)

            each_unit(pe, body, UNITS, STEPS, LEAD, TAIL)

        @block.scalar
        def _(act):
            def round_weights(i, r):
                q = (r // B) % 2
                wait_all(act, (w_loaded, 16 * block_of(i, r)),
                         *[(up_mm, nth(i, r - B - 1))][:not opening(i, r, 2 * B)])
                act.activation(w_hi[:, q], w_raw[:, :, :, :], ACT.Copy).then_inc(w_hi_done, 1)

            def body(i, r):
                if not missing(i, r):
                    wait_all(act, (gate_mm, nth(i, r)),
                             *[(hidden_done, nth(i, r - 2))][:not opening(i, r, 2)])
                    act.activation(silu_gate[:, r % 2], gate_ps[:, r % 2], ACT.Silu).then_inc(gate_done, 1)
                if r % B == 2 and not missing(i, r + B - 2):
                    round_weights(i, r + B - 2)

            each_unit(act, body, UNITS, STEPS, LEAD, TAIL)

        @block.vector
        def _(dve):
            def keep_lo(i, r):
                q = (r // B) % 2
                wait_all(dve, (w_hi_done, block_of(i, r)))
                dve.tensor_tensor(w_lo[:, q], w_raw[:, :, :, :], w_hi[:, q].bitcast(F32),
                                  ALU.subtract).then_inc(w_lo_done, 1)

            def body(i, r):
                q = r % 2
                if not missing(i, r):
                    wait_all(dve, (gate_done, nth(i, r)), (up_mm, nth(i, r)),
                             *[(stored[q], 16 * nth(i, r - 2, 2))][:not opening(i, r, 2)])
                    dve.tensor_tensor(hidden[:, q], silu_gate[:, q], up_ps[:, q],
                                      ALU.mult).then_inc(hidden_done, 1)
                if r % B == 2 and not missing(i, r + B - 2):
                    keep_lo(i, r + B - 2)

            each_unit(dve, body, UNITS, STEPS, LEAD, TAIL)


def attention_output(nc, m):
    STEPS, LEAD, TAIL = 4, 3, 1
    LAST = TILES // STEPS - 1
    QUARTER = KI // 4
    with Scope(nc, "attn_out") as s:
        w_c = [s.sb(f"w_{x}", [P, KI, D], F32R) for x in ("hi", "lo")]
        w = split_weights(s, "w", [(m.w_c[k], w_c[0][:, k], w_c[1][:, k], None) for k in range(KI)], D,
                          6)
        down_raw = s.sb("down_raw", [P, 2, D])
        down_loaded = [s.sem(f"down_loaded{q}") for q in range(2)]
        down_hi_done, down_lo_done = s.sem("down_hi_done"), s.sem("down_lo_done")
        bias = s.sb("bias", [P, D])
        y = s.sb("y", [P, 2, KI, P])
        hi, lo = s.sb("y_hi", [P, 2, KI, P], F32R), s.sb("y_lo", [P, 2, KI, P], F32R)
        out = s.sb("out", [P, 2, D])
        turn_ps = s.ps("turn_ps", [P, 4, QUARTER, P])
        out_ps = s.ps("out_ps", [P, 2, D])
        bias_loaded = s.sem("bias_loaded")
        y_loaded = [s.sem(f"y_loaded{q}") for q in range(2)]
        turned, hi_done, lo_done, out_mm, out_done = (
            s.sem(n) for n in ("turned", "hi_done", "lo_done", "out_mm", "out_done"))
        stored = [s.sem(f"stored{q}") for q in range(2)]
        block = s.block()
        y_t = m.attended_dram.rearrange("(n p) d -> n p d", p=P)
        s_t = m.s_dram.rearrange("(n p) d -> n p d", p=P)

        def missing(i, r):
            return opening(i, r, 0) or (isinstance(i, int) and i == LAST and r >= STEPS)

        def nth(i, r, ring=1):
            return i * (STEPS // ring) + r // ring + 1

        def pieces(i, r):
            if opening(i, r, 2):
                return [2 * r, 2 * r + 1]
            return [] if missing(i, r) else [r + 2]

        @block.sync
        def _(sync):
            def load(i, r):
                q = r % 2
                rows = row_of(sync, y_t, i * STEPS + r).rearrange("(p d) -> p d", p=P)
                if not opening(i, r, 2):
                    sync.wait_ge(turned, 4 * nth(i, r - 2))
                sync.dma_start(y[:, q].rearrange("p k e -> p (k e)"), rows).then_inc(y_loaded[q], 16)

            def load_down(i, n):
                rows = row_of(sync, m.w_mlp_down, i * STEPS + n).rearrange("(p d) -> p d", p=P)
                if not opening(i, n, 2):
                    sync.wait_ge(down_lo_done, nth(i, n - 2))
                sync.dma_start(down_raw[:, n % 2], rows).then_inc(down_loaded[n % 2], 16)

            def body(i, r):
                if not missing(i, r + 2):
                    load(i, r + 2)
                for n in pieces(i, r):
                    load_down(i, n)
                if not missing(i, r - 1):
                    q = (r - 1) % 2
                    rows = row_of(sync, s_t, i * STEPS + r - 1).rearrange("(p d) -> p d", p=P)
                    wait_all(sync, (out_done, nth(i, r - 1)))
                    sync.dma_start(rows, out[:, q]).then_inc(stored[q], 16)

            load(0, 0)
            for n in range(w.ring):
                w.load(sync, n)
            load(0, 1)
            sync.dma_start(bias[:, :], m.b_c.broadcast_to([P, D])).then_inc(bias_loaded, 16)
            for n in range(w.ring, w.n):
                w.load(sync, n)
            each_unit(sync, body, TILES, STEPS, 2, TAIL)
            for q in range(2):
                sync.wait_ge(stored[q], 16 * TILES // 2)

        @block.tensor
        def _(pe):
            def turn(i, r):
                if missing(i, r):
                    return
                q = r % 2
                for a in range(4):
                    wait_all(pe, *[(y_loaded[q], 16 * nth(i, r, 2))][:a == 0],
                             *[(lo_done, 4 * nth(i, r) - 7 + a)][:not opening(i, r, 1)])
                    for k in range(QUARTER):
                        end = pe.transpose(turn_ps[:, a, k], y[:, q, a * QUARTER + k], m.ident[:, :])
                    end.then_inc(turned, 1)

            def body(i, r):
                turn(i, r + 1)
                if missing(i, r):
                    return
                q = r % 2
                wait_all(pe, *[(out_done, nth(i, r - 2))][:not opening(i, r, 2)])
                for k in range(KI):
                    if k % QUARTER == 0:
                        wait_all(pe, (lo_done, 4 * nth(i, r) - 3 + k // QUARTER))
                    if opening(i, r, 1):
                        pe.wait_ge(w.done, k + 1)
                    end = three_passes(pe, out_ps[:, q], lambda k: (hi[:, q, k], lo[:, q, k]),
                                       lambda k: [x[:, k] for x in w_c], [k],
                                       first=k == 0, last=k == KI - 1)
                end.then_inc(out_mm, 1)

            turn(0, 0)
            each_unit(pe, body, TILES, STEPS, LEAD, TAIL)

        @block.scalar
        def _(act):
            def body(i, r):
                if missing(i, r):
                    return
                q = r % 2
                for a in range(4):
                    wait_all(act, (turned, 4 * nth(i, r) - 3 + a),
                             *[(out_mm, nth(i, r - 2))][:not opening(i, r, 2)])
                    act.activation(hi[:, q, a * QUARTER:(a + 1) * QUARTER], turn_ps[:, a],
                                   ACT.Copy).then_inc(hi_done, 1)

            body(0, 0)
            for n in range(w.n):
                w.round_hi(act, n)

            def step(i, r):
                if not opening(i, r, 1):
                    body(i, r)
                for n in pieces(i, r):
                    wait_all(act, (down_loaded[n % 2], 16 * nth(i, n, 2)))
                    act.activation(m.w_down_hi[:, bass.ds(i * STEPS + n, 1)].rearrange("p o d -> p (o d)"),
                                   down_raw[:, n % 2], ACT.Copy).then_inc(down_hi_done, 1)

            each_unit(act, step, TILES, STEPS, LEAD, TAIL)

        @block.vector
        def _(dve):
            def split(i, r):
                q = r % 2
                for a in range(4):
                    cols = slice(a * QUARTER, (a + 1) * QUARTER)
                    wait_all(dve, (hi_done, 4 * nth(i, r) - 3 + a))
                    dve.tensor_tensor(lo[:, q, cols], turn_ps[:, a], hi[:, q, cols].bitcast(F32),
                                      ALU.subtract).then_inc(lo_done, 1)

            def body(i, r):
                if not missing(i, r) and not opening(i, r, 1):
                    split(i, r)
                if not missing(i, r - 1):
                    q = (r - 1) % 2
                    wait_all(dve, (out_mm, nth(i, r - 1)), (bias_loaded, 16),
                             *[(stored[q], 16 * nth(i, r - 3, 2))][:not opening(i, r, 3)])
                    dve.tensor_tensor(out[:, q], out_ps[:, q], bias[:, :], ALU.add).then_inc(out_done, 1)

            split(0, 0)
            for n in range(w.n):
                w.keep_lo(dve, n)
            each_unit(dve, body, TILES, STEPS, LEAD, TAIL)

        @block.gpsimd
        def _(pool):
            def body(i, r):
                for n in pieces(i, r):
                    hi, lo = (x[:, bass.ds(i * STEPS + n, 1)].rearrange("p o d -> p (o d)")
                              for x in (m.w_down_hi, m.w_down_lo))
                    wait_all(pool, (down_hi_done, nth(i, n)))
                    pool.tensor_tensor(lo, down_raw[:, n % 2], hi.bitcast(F32),
                                       ALU.subtract).then_inc(down_lo_done, 1)

            each_unit(pool, body, TILES, STEPS, 2, 0)


def mlp_down(nc, m):
    STEPS, LEAD, TAIL = 4, 3, 1
    LAST = TILES // STEPS - 1
    KS = SHARED // P
    with Scope(nc, "mlp_down") as s:
        w_down = m.w_down_hi, m.w_down_lo
        h = s.sb("h", [P, 2, BLOCKS, P])
        hi, lo = s.sb("h_hi", [P, 2, BLOCKS, P], F32R), s.sb("h_lo", [P, 2, BLOCKS, P], F32R)
        x1, mixer = s.sb("x1", [P, 4, D]), s.sb("mixer", [P, 4, D])
        routed, total, gate, out = (s.sb(n, [P, 2, D]) for n in ("routed", "total", "gate", "out"))
        shared_ps, routed_ps = s.ps("shared_ps", [P, 2, D]), s.ps("routed_ps", [P, 2, D])
        h_loaded = [s.sem(f"h_loaded{q}") for q in range(2)]
        rows_loaded = [s.sem(f"rows_loaded{q}") for q in range(2)]
        hi_done, lo_done, shared_mm, routed_done, total_done, gate_done, gated_done, out_done = (
            s.sem(n) for n in ("hi_done", "lo_done", "shared_mm", "routed_done", "total_done",
                               "gate_done", "gated_done", "out_done"))
        stored = [s.sem(f"stored{q}") for q in range(2)]
        block = s.block()
        x1_t, s_t, out_t = (d.rearrange("(n p) d -> n p d", p=P) for d in (m.x1_dram, m.s_dram, m.out))
        hidden_p = m.hidden_dram.rearrange("k p t -> p k t")
        PARTS = [slice(a, a + BLOCKS // 3) for a in range(0, BLOCKS, BLOCKS // 3)]
        part_loaded = [s.sem(f"part_loaded{a}") for a in range(2)] + [h_loaded[0]]
        part_hi_done, part_lo_done = s.sem("part_hi_done"), s.sem("part_lo_done")

        def missing(i, r):
            return opening(i, r, 0) or (isinstance(i, int) and i == LAST and r >= STEPS)

        def nth(i, r, ring=1):
            return i * (STEPS // ring) + r // ring + 1

        @block.sync
        def _(sync):
            def load(i, r):
                q, t = r % 2, i * STEPS + r
                tokens = columns_of(sync, t, P)
                rows = [row_of(sync, d, t).rearrange("(p d) -> p d", p=P) for d in (x1_t, s_t)]
                if not opening(i, r, 2):
                    sync.wait_ge(lo_done, nth(i, r - 2))
                if opening(i, r, 1):
                    for a, part in enumerate(PARTS):
                        sync.dma_start(h[:, 0, part], hidden_p[:, part, 0:P]).then_inc(part_loaded[a], 16)
                else:
                    sync.dma_start(h[:, q], hidden_p[:, :, tokens]).then_inc(h_loaded[q], 16)
                if not opening(i, r, 4):
                    sync.wait_ge(out_done, nth(i, r - 4))
                for tile, source in zip((x1, mixer), rows):
                    sync.dma_start(tile[:, r % 4], source).then_inc(rows_loaded[q], 16)

            def body(i, r):
                if not missing(i, r + 2):
                    load(i, r + 2)
                if not missing(i, r - 1):
                    q = (r - 1) % 2
                    rows = row_of(sync, out_t, i * STEPS + r - 1).rearrange("(p d) -> p d", p=P)
                    wait_all(sync, (out_done, nth(i, r - 1)))
                    sync.dma_start(rows, out[:, q]).then_inc(stored[q], 16)

            load(0, 0)
            load(0, 1)
            each_unit(sync, body, TILES, STEPS, 2, TAIL)
            for q in range(2):
                sync.wait_ge(stored[q], 16 * TILES // 2)

        @block.tensor
        def _(pe):
            def body(i, r):
                if missing(i, r):
                    return
                q = r % 2
                wait_all(pe, *[(lo_done, nth(i, r))][:not opening(i, r, 1)], *[(total_done, nth(i, r - 2))][:not opening(i, r, 2)])
                for ps, ks in ((shared_ps, range(KS)), (routed_ps, range(KS, BLOCKS))):
                    for k in ks:
                        if opening(i, r, 1):
                            if k < PARTS[-1].start:
                                pe.wait_ge(part_lo_done, k // 6 + 1)
                            else:
                                pe.wait_ge(lo_done, 1)
                        end = three_passes(pe, ps[:, q], lambda k: (hi[:, q, k], lo[:, q, k]),
                                           lambda k: [x[:, k] for x in w_down], [k],
                                           first=k == ks[0], last=k == ks[-1])
                end.then_inc(shared_mm, 1)

            each_unit(pe, body, TILES, STEPS, LEAD, TAIL)

        @block.scalar
        def _(act):
            def split(i, r):
                if missing(i, r):
                    return
                q = r % 2
                wait_all(act, (h_loaded[q], 16 * nth(i, r, 2)),
                         *[(shared_mm, nth(i, r - 2))][:not opening(i, r, 2)])
                act.activation(hi[:, q], h[:, q], ACT.Copy).then_inc(hi_done, 1)

            def body(i, r):
                if not opening(i, r, 1):
                    split(i, r)
                if not missing(i, r - 1):
                    q, t = (r - 1) % 2, i * STEPS + r - 1
                    wait_all(act, (shared_mm, nth(i, r - 1)))
                    act.activation(routed[:, q], routed_ps[:, q], ACT.Copy,
                                   scale=m.comb_w[:, bass.ds(t, 1)]).then_inc(routed_done, 1)
                    wait_all(act, (total_done, nth(i, r - 1)))
                    act.activation(gate[:, q], total[:, q], ACT.Silu).then_inc(gate_done, 1)

            for a, part in enumerate(PARTS):
                act.wait_ge(part_loaded[a], 16)
                act.activation(hi[:, 0, part], h[:, 0, part], ACT.Copy).then_inc(
                    part_hi_done if a < 2 else hi_done, 1)
            each_unit(act, body, TILES, STEPS, LEAD, TAIL)

        @block.vector
        def _(dve):
            def split(i, r):
                q = r % 2
                wait_all(dve, (hi_done, nth(i, r)))
                dve.tensor_tensor(lo[:, q], h[:, q], hi[:, q].bitcast(F32), ALU.subtract).then_inc(lo_done, 1)

            def finish(i, r):
                q = r % 2
                wait_all(dve, (routed_done, nth(i, r)),
                         *[(gate_done, nth(i, r - 2))][:not opening(i, r, 2)])
                dve.tensor_tensor(total[:, q], routed[:, q], shared_ps[:, q], ALU.add).then_inc(total_done, 1)
                wait_all(dve, (gate_done, nth(i, r)), (rows_loaded[q], 32 * nth(i, r, 2)),
                         *[(stored[q], 16 * nth(i, r - 2, 2))][:not opening(i, r, 2)])
                dve.tensor_tensor(gate[:, q], gate[:, q], mixer[:, r % 4], ALU.mult).then_inc(gated_done, 1)
                wait_all(dve, (gated_done, nth(i, r)))
                dve.tensor_tensor(out[:, q], gate[:, q], x1[:, r % 4], ALU.add).then_inc(out_done, 1)

            def body(i, r):
                if not missing(i, r) and not opening(i, r, 1):
                    split(i, r)
                if not missing(i, r - 1):
                    finish(i, r - 1)

            for a, part in enumerate(PARTS):
                if a < 2:
                    dve.wait_ge(part_hi_done, a + 1)
                else:
                    dve.wait_ge(hi_done, 1)
                dve.tensor_tensor(lo[:, 0, part], h[:, 0, part], hi[:, 0, part].bitcast(F32),
                                  ALU.subtract).then_inc(part_lo_done if a < 2 else lo_done, 1)
            each_unit(dve, body, TILES, STEPS, LEAD, TAIL)


_INS = ['L0_attn_hidden_states', 'L0_attn_W_in', 'L0_attn_conv_w', 'L0_attn_conv_b', 'L0_attn_dt_bias',
        'L0_attn_A_log', 'L0_attn_D_param', 'L0_attn_norm_w', 'L0_attn_W_out', 'L0_ffn_W_up',
        'L0_ffn_W_down', 'L0_ffn_W_gate', 'L0_ffn_W_expert', 'L1_attn_Wq', 'L1_attn_Wk', 'L1_attn_Wv',
        'L1_attn_Wg', 'L1_attn_Wc', 'L1_attn_bc', 'L1_ffn_router_weight', 'L1_ffn_sh_gate',
        'L1_ffn_sh_up', 'L1_ffn_sh_down', 'L1_ffn_r_gate', 'L1_ffn_r_up', 'L1_ffn_r_down']


def lay_out(i):
    import numpy as np
    a = {n: np.asarray(v) for n, v in i.items()}
    f = np.float32

    def rows(w):
        return w.reshape(-1, P, w.shape[1])

    def blocks(*parts):
        w = np.stack([p.reshape(-1, P, KD, P) for p in parts])
        return w.transpose(1, 4, 3, 0, 2)

    w_in = a['L0_attn_W_in']
    gate, xs, bc = w_in[:INTER], w_in[INTER:2 * INTER], w_in[2 * INTER:]
    b_w, c_w, dt_w = bc[:STATE], bc[STATE:2 * STATE], bc[2 * STATE:]
    taps = np.concatenate([a['L0_attn_conv_w'], a['L0_attn_conv_b'][:, None]], 1)
    d_rows = np.repeat(a['L0_attn_D_param'], HEAD_P)[:, None]
    pad = np.zeros((INTER, 2), f)
    q = a['L1_attn_Wq'].T.reshape(KV_HEADS, REP, HEAD_D, D)
    out = {
        'x': a['L0_attn_hidden_states'].reshape(TOK, D),
        'w_up': rows(a['L0_ffn_W_up'].T), 'w_down': rows(a['L0_ffn_W_down'].T),
        'w_expert': rows(np.concatenate([a['L0_ffn_W_expert'], a['L0_ffn_W_gate'].T], 1)),
        'w_bcd': rows(np.concatenate([b_w, dt_w, c_w]).T),
        'bc_vec': np.concatenate([taps[INTER:], np.zeros((2 * STATE, 3), f)], 1).reshape(
            2, P, 8).transpose(1, 0, 2),
        'head_vec': np.stack([a['L0_attn_dt_bias'], a['L0_attn_A_log']], 1),
        'w_gate_x': blocks(gate, xs),
        'pair_vec': np.concatenate([taps[:INTER], d_rows, pad], 1).reshape(PAIRS, P, 8),
        'norm_w': a['L0_attn_norm_w'].reshape(KI, P).T, 'w_out': rows(a['L0_attn_W_out'].T),
        'w_gvr': rows(np.concatenate([a['L1_attn_Wg'], a['L1_attn_Wv'],
                                      a['L1_ffn_router_weight'].T], 1)),
        'w_qqk': blocks(q[:, 0].reshape(-1, D), q[:, 1].reshape(-1, D), a['L1_attn_Wk'].T),
        'w_c': rows(a['L1_attn_Wc']), 'b_c': a['L1_attn_bc'].reshape(1, D),
        'w_gate_up': blocks(np.concatenate([a['L1_ffn_sh_gate'], a['L1_ffn_r_gate']]),
                            np.concatenate([a['L1_ffn_sh_up'], a['L1_ffn_r_up']])),
        'w_mlp_down': rows(np.concatenate([a['L1_ffn_sh_down'].T, a['L1_ffn_r_down'].T])),
        'ident': np.eye(P, dtype=f),
        'causal': np.triu(np.ones((P, P), f)),
        'never': np.where(np.arange(P)[None, :] >= np.arange(P)[:, None], f(0), f(-1e30)),
    }
    return {n: np.ascontiguousarray(v) for n, v in out.items()}


class Memory:

    def __init__(self, d, out):
        self.x, self.out = d["x"], out
        self.w_up, self.w_down, self.w_expert = d["w_up"], d["w_down"], d["w_expert"]
        self.w_bcd, self.w_gate_x, self.pair_vec, self.w_out = (
            d["w_bcd"], d["w_gate_x"], d["pair_vec"], d["w_out"])
        self.w_gvr, self.w_qqk, self.w_c, self.b_c = d["w_gvr"], d["w_qqk"], d["w_c"], d["b_c"]
        self.w_gate_up, self.w_mlp_down = d["w_gate_up"], d["w_mlp_down"]


def build(nc, d, out, debug=()):
    with ExitStack() as stack:
        def sb(name, shape, dtype=F32):
            return stack.enter_context(nc.sbuf_tensor(name, shape, dtype))

        def dram(name, shape):
            return nc.dram_tensor(name, shape, F32, kind="ExternalOutput" if name in debug else "Internal").ap()

        @contextmanager
        def pair(name, shape):
            with nc.sbuf_tensor(f"{name}_hi", shape, F32R) as hi, \
                    nc.sbuf_tensor(f"{name}_lo", shape, F32R) as lo:
                yield hi, lo

        m = Memory(d, out)
        m.gate_dram, m.x1_dram, m.s_dram = (dram(n, [TOK, D]) for n in ("gate_s", "x1_s", "s_s"))
        m.ell_dram = dram("ell_s", [PAIRS, 2, TOK])
        m.mixed_dram = dram("mixed_s", [PAIRS, P, TOK])
        m.log_gate_dram = dram("log_gate_s", [KV_HEADS, TOK])
        m.values_dram = dram("values_s", [TOK, KV_DIM])
        m.attended_dram = dram("attended_s", [TOK, Q_DIM])
        m.hidden_dram = dram("hidden_s", [BLOCKS, P, TOK])
        constants = ("ident", "causal", "never", "bc_vec", "head_vec", "norm_w")
        loaded = {n: sb(f"{n}_sb", list(d[n].shape)) for n in constants}
        m.ident, m.causal, m.never, m.bc_vec, m.head_vec, m.norm_w = (loaded[n] for n in constants)
        m.comb_w = sb("comb_w", [P, TILES])
        m.constants = [(loaded[n], d[n]) for n in constants]
        m.constants_loaded = nc.alloc_semaphore("constants_loaded")
        m.gate_stored = nc.alloc_semaphore("gate_stored")
        with nc.sbuf_tensor("xn_hi", [P, KD, TOK], F32R) as m.xn_hi, \
                nc.sbuf_tensor("xn_lo", [P, KD, TOK], F32R) as m.xn_lo, \
                nc.sbuf_tensor("b_tm", [P, TILES, P], F32) as m.b_tm:
            norm_and_mixture(nc, m)
            with nc.sbuf_tensor("c_fm", [P, TOK], F32) as m.c_fm, \
                    nc.sbuf_tensor("cb", [P, TILES, P], F32) as m.cb, \
                    nc.sbuf_tensor("times_tm", [P, 3 * TILES, HEADS], F32) as m.times_tm, \
                    nc.sbuf_tensor("chunk_decay", [P, HEADS, TILES], F32) as m.chunk_decay:
                m.dt_tm, m.dt_end_tm, m.ell_tm = (m.times_tm[:, n * TILES:(n + 1) * TILES]
                                                  for n in range(3))
                with pair("w_heads", [P, 2, KD, 2, P]) as m.w_heads:
                    ssm_shared(nc, m)
                    ssm_heads(nc, m)
        with nc.sbuf_tensor("xn1_hi", [P, KD, TOK], F32R) as m.xn_hi, \
                nc.sbuf_tensor("xn1_lo", [P, KD, TOK], F32R) as m.xn_lo:
            ssm_output(nc, m)
            m.values_stored = [nc.alloc_semaphore(f"values_stored{q}") for q in range(2)]
            m.attended_stored = [nc.alloc_semaphore(f"attended_stored{q}") for q in range(2)]
            with pair("w_mlp", [P, 2, KD, 2, P]) as m.w_mlp, \
                    nc.sbuf_tensor("rows_out", [P, 2, KV_DIM + EXPERTS], F32) as rows_out:
                m.values_out = rows_out[:, :, :]
                m.attended_out = rows_out[:, :, 0:CH * REP * HEAD_D].rearrange(
                    "p q (c r e) -> p q c r e", c=CH, r=REP)
                with pair("w_attention", [P, 2, KD, 3, P]) as m.w_attention, \
                        nc.sbuf_tensor("log_gate_tm", [P, KV_HEADS, TILES], F32) as m.log_gate_tm:
                    values_and_decays(nc, m)
                    power_attention(nc, m)
                mlp_up(nc, m)
        with nc.sbuf_tensor("w_down_hi", [P, BLOCKS, D], F32R) as m.w_down_hi, \
                nc.sbuf_tensor("w_down_lo", [P, BLOCKS, D], F32R) as m.w_down_lo:
            attention_output(nc, m)
            mlp_down(nc, m)


def kernel(**inputs):
    import concourse.bacc as bacc
    from concourse.bass_utils import run_bass_kernel_spmd

    arrays = lay_out({n: inputs[n] for n in _INS})
    nc = bacc.Bacc("TRN2", target_bir_lowering=False, num_devices=1)
    d = {n: nc.dram_tensor(f"in_{n}", list(a.shape), F32, kind="ExternalInput").ap()
         for n, a in arrays.items()}
    out = nc.dram_tensor("out", [TOK, D], F32, kind="ExternalOutput").ap()
    build(nc, d, out)
    r = run_bass_kernel_spmd(nc, [{f"in_{n}": a for n, a in arrays.items()}], core_ids=[0])
    return r.results[0]["out"].reshape(B, SEQ, D)
```
